# Optimizing a Trainium2 kernel written in Bass

```python
import numpy as np
import jax
import jax.numpy as jnp

def _softmax(x, axis=-1):
    return jax.nn.softmax(x, axis=axis)

def _gelu(x):
    return jax.nn.gelu(x, approximate=True)

def _silu(x):
    return jax.nn.silu(x)

def _sigmoid(x):
    return jax.nn.sigmoid(x)

def _layernorm(x, axis=-1, eps=1e-05):
    m = jnp.mean(x, axis=axis, keepdims=True)
    v = jnp.var(x, axis=axis, keepdims=True)
    return (x - m) / jnp.sqrt(v + eps)

def _scatter_add(tgt, idx, src, axis=0):
    return tgt.at[idx].add(src)

def _segment_sum(src, seg, n):
    return jax.ops.segment_sum(src, seg, n)
kernel_name = 'mk_decoder_postln_d2_seqx_r8_3b02ac'

def setup_inputs(seed: int=0):
    np.random.seed(seed)
    _w = jnp.asarray

    def _rec_inputs():
        import jax
        import jax.numpy as jnp
        _rk = jax.random.key(seed)
        x = -7.109e-05 + 0.9999 * jax.random.normal(jax.random.fold_in(_rk, 1), (4, 256, 256), jnp.float32)
        _lenS = 256 - jax.random.randint(jax.random.fold_in(_rk, 7), (4,), 0, max(1, 256 // 4) + 1, jnp.int32)
        _lenS2 = 256 - jax.random.randint(jax.random.fold_in(_rk, 8), (4,), 0, max(1, 256 // 4) + 1, jnp.int32)
        _ctx_512P = jax.random.normal(jax.random.fold_in(_rk, 11), (4, 16, 64), jnp.float32)
        _ctx_512c = jax.random.dirichlet(jax.random.fold_in(_rk, 511), 0.3 * jnp.ones((16,), jnp.float32), (4, 256))
        _ctx_512t = jnp.einsum('bsk,bkd->bsd', _ctx_512c, _ctx_512P)
        _ctx_512t = _ctx_512t * jax.lax.rsqrt(jnp.mean(jnp.square(_ctx_512t)) + 1e-12) * 0.953939
        ctx_512 = 2.81802e-05 + 1.00001 * (_ctx_512t + 0.3 * jax.random.normal(jax.random.fold_in(_rk, 611), (4, 256, 64), jnp.float32))
        return (x, ctx_512)
    x, ctx_512 = _rec_inputs()

    def _L0_attn_setup():
        import jax, jax.numpy as jnp
        import numpy as np
        from jax import lax
        B, L, H = (2, 128, 256)
        E, N, TR, K = (512, 16, 128, 4)
        key = jax.random.key(seed)
        ks = jax.random.split(key, 10)
        s = lambda d: 1.0 / np.sqrt(d)
        return {'input_states': jax.random.normal(ks[0], (B, L, H), jnp.float32), 'W_in': jax.random.normal(ks[1], (H, 2 * E), jnp.float32) * s(H), 'conv_kernel': jax.random.normal(ks[2], (E, 1, K), jnp.float32) * s(K), 'conv_bias': jax.random.normal(ks[3], (E,), jnp.float32) * 0.01, 'W_x': jax.random.normal(ks[4], (E, TR + 2 * N), jnp.float32) * s(E), 'W_dt': jax.random.normal(ks[5], (TR, E), jnp.float32) * s(TR), 'b_dt': jax.random.normal(ks[6], (E,), jnp.float32) * 0.01, 'W_out': jax.random.normal(ks[7], (E, H), jnp.float32) * s(E), 'A_log': jax.random.uniform(ks[8], (E, N), jnp.float32, 0.0, 2.0), 'D': jax.random.normal(ks[9], (E,), jnp.float32)}
    _L0_attn_all = _L0_attn_setup()
    _L0_attn_in = {k: v for k, v in _L0_attn_all.items() if k in ('W_in', 'conv_kernel', 'conv_bias', 'W_x', 'W_dt', 'b_dt', 'W_out', 'A_log', 'D')}
    del _L0_attn_all

    def _L0_xattn_setup():
        import jax, jax.numpy as jnp
        import numpy as np
        EPS = 1e-06
        IMAGE_DIMS = 256
        key = jax.random.key(seed)
        k1, k2, k3 = jax.random.split(key, 3)
        B, I, J, D = (16, 256, 256, 64)
        p = jax.random.normal(k1, (B, I, J), dtype=jnp.float32)
        k_v = jax.random.normal(k2, (B, J, D), dtype=jnp.float32)
        W_k = jax.random.normal(k3, (D, D), dtype=jnp.float32) * (1.0 / np.sqrt(D))
        b_k = jnp.zeros((D,), dtype=jnp.float32)
        ln_gamma = jnp.ones((J,), dtype=jnp.float32)
        ln_beta = jnp.zeros((J,), dtype=jnp.float32)
        return {'p': p, 'k_v': k_v, 'W_k': W_k, 'b_k': b_k, 'ln_gamma': ln_gamma, 'ln_beta': ln_beta}
    _L0_xattn_all = _L0_xattn_setup()
    _L0_xattn_in = {k: v for k, v in _L0_xattn_all.items() if k in ('W_k', 'b_k', 'ln_gamma', 'ln_beta')}
    del _L0_xattn_all

    def _L0_ffn_setup():
        import jax, jax.numpy as jnp
        import numpy as np
        D = 256
        F = 176
        E = 8
        K = 2
        FS = 352
        B, S = (2, 128)
        key = jax.random.key(seed)
        ks = jax.random.split(key, 9)
        sc = 0.02
        return {'x': jax.random.normal(ks[0], (B, S, D), dtype=jnp.float32), 'Wr': jax.random.normal(ks[1], (E, D), dtype=jnp.float32) * sc, 'Wg': jax.random.normal(ks[2], (E, F, D), dtype=jnp.float32) * sc, 'Wu': jax.random.normal(ks[3], (E, F, D), dtype=jnp.float32) * sc, 'Wd': jax.random.normal(ks[4], (E, D, F), dtype=jnp.float32) * sc, 'Wsg': jax.random.normal(ks[5], (FS, D), dtype=jnp.float32) * sc, 'Wsu': jax.random.normal(ks[6], (FS, D), dtype=jnp.float32) * sc, 'Wsd': jax.random.normal(ks[7], (D, FS), dtype=jnp.float32) * sc}
    _L0_ffn_all = _L0_ffn_setup()
    _L0_ffn_in = {k: v for k, v in _L0_ffn_all.items() if k in ('Wr', 'Wg', 'Wu', 'Wd', 'Wsg', 'Wsu', 'Wsd')}
    del _L0_ffn_all

    def _L1_attn_setup():
        import jax, jax.numpy as jnp
        import numpy as np
        D = 256
        EPS = 1e-05

        def _hgrn_scan(a, b):

            def comb(c1, c2):
                a1, b1 = c1
                a2, b2 = c2
                return (a1 * a2, b1 * a2 + b2)
            _, h = jax.lax.associative_scan(comb, (a, b), axis=1)
            return h
        key = jax.random.key(seed)
        ks = jax.random.split(key, 6)
        B, T = (4, 512)
        gain = 2 ** (-2.5)
        scale = gain * np.sqrt(6.0 / (D + D))

        def w(k):
            return jax.random.uniform(k, (D, D), jnp.float32, -scale, scale)
        return {'hidden_states': jax.random.normal(ks[0], (B, T, D), jnp.float32), 'Wi': w(ks[1]), 'Wf': w(ks[2]), 'Wg': w(ks[3]), 'Wo': w(ks[4]), 'g_norm_weight': jnp.ones((D,), jnp.float32)}
    _L1_attn_all = _L1_attn_setup()
    _L1_attn_in = {k: v for k, v in _L1_attn_all.items() if k in ('Wi', 'Wf', 'Wg', 'Wo', 'g_norm_weight')}
    del _L1_attn_all

    def _L1_xattn_setup():
        import jax, jax.numpy as jnp
        import numpy as np
        B, N, D = (16, 256, 64)
        H = 4
        TOP_K_RATIO = 0.3
        key = jax.random.key(seed)
        k1, k2, k3, k4 = jax.random.split(key, 4)
        h = jax.random.normal(k1, (B, N, D), dtype=jnp.float32)
        adj_raw = jax.random.uniform(k2, (B, N, N), dtype=jnp.float32)
        lim = 1.0 / np.sqrt(D)
        Wq = jax.random.uniform(k3, (D, D), minval=-lim, maxval=lim, dtype=jnp.float32)
        Wk = jax.random.uniform(k4, (D, D), minval=-lim, maxval=lim, dtype=jnp.float32)
        gamma_raw = jnp.float32(-0.85)
        return {'h': h, 'adj_raw': adj_raw, 'Wq': Wq, 'Wk': Wk, 'gamma_raw': gamma_raw}
    _L1_xattn_all = _L1_xattn_setup()
    _L1_xattn_in = {k: v for k, v in _L1_xattn_all.items() if k in ('Wq', 'Wk', 'gamma_raw')}
    del _L1_xattn_all

    def _L1_ffn_setup():
        import jax, jax.numpy as jnp
        import numpy as np
        N_EXPERTS = 8
        TOP_K = 2
        C = 256
        H = 128
        HS = 256
        B, T = (1, 64)
        SCALE = 0.02
        key = jax.random.key(seed)
        ks = jax.random.split(key, 10)
        x = jax.random.normal(ks[0], (B, T, C), dtype=jnp.float32)
        gate_w = jax.random.normal(ks[1], (N_EXPERTS, C), dtype=jnp.float32) * SCALE
        w_gate = jax.random.normal(ks[2], (N_EXPERTS, H, C), dtype=jnp.float32) * SCALE
        w_up = jax.random.normal(ks[3], (N_EXPERTS, H, C), dtype=jnp.float32) * SCALE
        w_down = jax.random.normal(ks[4], (N_EXPERTS, C, H), dtype=jnp.float32) * SCALE
        sh_gate = jax.random.normal(ks[5], (HS, C), dtype=jnp.float32) * SCALE
        sh_up = jax.random.normal(ks[6], (HS, C), dtype=jnp.float32) * SCALE
        sh_down = jax.random.normal(ks[7], (C, HS), dtype=jnp.float32) * SCALE
        se_gate_w = jax.random.normal(ks[8], (1, C), dtype=jnp.float32) * SCALE
        return {'x': x, 'gate_w': gate_w, 'w_gate': w_gate, 'w_up': w_up, 'w_down': w_down, 'sh_gate': sh_gate, 'sh_up': sh_up, 'sh_down': sh_down, 'se_gate_w': se_gate_w}
    _L1_ffn_all = _L1_ffn_setup()
    _L1_ffn_in = {k: v for k, v in _L1_ffn_all.items() if k in ('gate_w', 'w_gate', 'w_up', 'w_down', 'sh_gate', 'sh_up', 'sh_down', 'se_gate_w')}
    del _L1_ffn_all
    return {'x': x, 'ctx_512': ctx_512, 'L0_attn_W_in': _L0_attn_in['W_in'], 'L0_attn_conv_kernel': _L0_attn_in['conv_kernel'], 'L0_attn_conv_bias': _L0_attn_in['conv_bias'], 'L0_attn_W_x': _L0_attn_in['W_x'], 'L0_attn_W_dt': _L0_attn_in['W_dt'], 'L0_attn_b_dt': _L0_attn_in['b_dt'], 'L0_attn_W_out': _L0_attn_in['W_out'], 'L0_attn_A_log': _L0_attn_in['A_log'], 'L0_attn_D': _L0_attn_in['D'], 'L0_xattn_W_k': _L0_xattn_in['W_k'], 'L0_xattn_b_k': _L0_xattn_in['b_k'], 'L0_xattn_ln_gamma': _L0_xattn_in['ln_gamma'], 'L0_xattn_ln_beta': _L0_xattn_in['ln_beta'], 'L0_ffn_Wr': _L0_ffn_in['Wr'], 'L0_ffn_Wg': _L0_ffn_in['Wg'], 'L0_ffn_Wu': _L0_ffn_in['Wu'], 'L0_ffn_Wd': _L0_ffn_in['Wd'], 'L0_ffn_Wsg': _L0_ffn_in['Wsg'], 'L0_ffn_Wsu': _L0_ffn_in['Wsu'], 'L0_ffn_Wsd': _L0_ffn_in['Wsd'], 'L1_attn_Wi': _L1_attn_in['Wi'], 'L1_attn_Wf': _L1_attn_in['Wf'], 'L1_attn_Wg': _L1_attn_in['Wg'], 'L1_attn_Wo': _L1_attn_in['Wo'], 'L1_attn_g_norm_weight': _L1_attn_in['g_norm_weight'], 'L1_xattn_Wq': _L1_xattn_in['Wq'], 'L1_xattn_Wk': _L1_xattn_in['Wk'], 'L1_xattn_gamma_raw': _L1_xattn_in['gamma_raw'], 'L1_ffn_gate_w': _L1_ffn_in['gate_w'], 'L1_ffn_w_gate': _L1_ffn_in['w_gate'], 'L1_ffn_w_up': _L1_ffn_in['w_up'], 'L1_ffn_w_down': _L1_ffn_in['w_down'], 'L1_ffn_sh_gate': _L1_ffn_in['sh_gate'], 'L1_ffn_sh_up': _L1_ffn_in['sh_up'], 'L1_ffn_sh_down': _L1_ffn_in['sh_down'], 'L1_ffn_se_gate_w': _L1_ffn_in['se_gate_w']}

def reference(x, ctx_512, L0_attn_W_in, L0_attn_conv_kernel, L0_attn_conv_bias, L0_attn_W_x, L0_attn_W_dt, L0_attn_b_dt, L0_attn_W_out, L0_attn_A_log, L0_attn_D, L0_xattn_W_k, L0_xattn_b_k, L0_xattn_ln_gamma, L0_xattn_ln_beta, L0_ffn_Wr, L0_ffn_Wg, L0_ffn_Wu, L0_ffn_Wd, L0_ffn_Wsg, L0_ffn_Wsu, L0_ffn_Wsd, L1_attn_Wi, L1_attn_Wf, L1_attn_Wg, L1_attn_Wo, L1_attn_g_norm_weight, L1_xattn_Wq, L1_xattn_Wk, L1_xattn_gamma_raw, L1_ffn_gate_w, L1_ffn_w_gate, L1_ffn_w_up, L1_ffn_w_down, L1_ffn_sh_gate, L1_ffn_sh_up, L1_ffn_sh_down, L1_ffn_se_gate_w):
    import jax
    import jax.numpy as jnp

    def _L0_attn_ref(input_states, W_in, conv_kernel, conv_bias, W_x, W_dt, b_dt, W_out, A_log, D):
        import jax, jax.numpy as jnp
        import numpy as np
        from jax import lax
        B, L, H = (2, 128, 256)
        E, N, TR, K = (512, 16, 128, 4)
        b, l, _ = input_states.shape
        dtype = input_states.dtype
        proj = jnp.einsum('blh,he->bel', input_states, W_in)
        hidden, gate = jnp.split(proj, 2, axis=1)
        x = lax.conv_general_dilated(hidden, conv_kernel, window_strides=(1,), padding=((K - 1, K - 1),), feature_group_count=E)[..., :l]
        hidden = jax.nn.silu(x + conv_bias[None, :, None])
        hs_ble = hidden.transpose(0, 2, 1)
        ssm_p = jnp.einsum('ble,ed->bld', hs_ble, W_x)
        dt, Bm, Cm = jnp.split(ssm_p, [TR, TR + N], axis=-1)
        dts = jax.nn.softplus(jnp.einsum('blr,re->ble', dt, W_dt) + b_dt)
        A = -jnp.exp(A_log.astype(jnp.float32))
        dA = jnp.exp(dts[..., None] * A[None, None])
        dBu = dts[..., None] * Bm[:, :, None, :] * hs_ble[..., None]

        def step(state, inp):
            a, bu, c = inp
            state = a * state + bu
            y = jnp.einsum('ben,bn->be', state.astype(dtype), c)
            return (state, y)
        init = jnp.zeros((b, E, N), dtype=dtype)
        _, ys = lax.scan(step, init, (dA.transpose(1, 0, 2, 3), dBu.transpose(1, 0, 2, 3), Cm.transpose(1, 0, 2)))
        scan_out = ys.transpose(1, 2, 0)
        y = (scan_out + hidden * D[None, :, None]) * jax.nn.silu(gate)
        return jnp.einsum('bel,eh->blh', y, W_out)

    def _L0_xattn_ref(p, k_v, W_k, b_k, ln_gamma, ln_beta):
        import jax, jax.numpy as jnp
        import numpy as np
        EPS = 1e-06
        IMAGE_DIMS = 256
        kv = k_v @ W_k.T + b_k
        out = jnp.einsum('bij,bjd->bid', p, kv)
        scale = IMAGE_DIMS ** (-0.5)
        sim = jnp.einsum('bid,bjd->bij', out, kv) * scale
        mu = jnp.mean(sim, axis=-1, keepdims=True)
        var = jnp.var(sim, axis=-1, keepdims=True)
        sim = (sim - mu) * jax.lax.rsqrt(var + EPS) * ln_gamma + ln_beta
        attn = jax.nn.softmax(sim, axis=-1)
        return attn

    def _L0_ffn_ref(x, Wr, Wg, Wu, Wd, Wsg, Wsu, Wsd):
        import jax, jax.numpy as jnp
        import numpy as np
        D = 256
        F = 176
        E = 8
        K = 2
        FS = 352
        B, S = (2, 128)
        silu = jax.nn.silu
        sg = silu(jnp.einsum('bsd,fd->bsf', x, Wsg))
        su = jnp.einsum('bsd,fd->bsf', x, Wsu)
        shared_out = jnp.einsum('bsf,df->bsd', sg * su, Wsd)
        logits = jnp.einsum('bsd,ed->bse', x, Wr)
        scores = jax.nn.softmax(logits, axis=-1)
        topk_scores, topk_idx = jax.lax.top_k(scores, K)
        w_full = jnp.sum(jax.nn.one_hot(topk_idx, E, dtype=x.dtype) * topk_scores[..., None], axis=-2)
        g = silu(jnp.einsum('bsd,efd->bsef', x, Wg))
        u = jnp.einsum('bsd,efd->bsef', x, Wu)
        out_e = jnp.einsum('bsef,edf->bsed', g * u, Wd)
        routed_out = jnp.einsum('bsed,bse->bsd', out_e, w_full)
        return routed_out + shared_out

    def _L1_attn_ref(hidden_states, Wi, Wf, Wg, Wo, g_norm_weight):
        import jax, jax.numpy as jnp
        import numpy as np
        D = 256
        EPS = 1e-05

        def _hgrn_scan(a, b):

            def comb(c1, c2):
                a1, b1 = c1
                a2, b2 = c2
                return (a1 * a2, b1 * a2 + b2)
            _, h = jax.lax.associative_scan(comb, (a, b), axis=1)
            return h
        x = hidden_states
        i_raw = jnp.einsum('btd,de->bte', x, Wi)
        f_raw = jnp.einsum('btd,de->bte', x, Wf)
        i = jax.nn.silu(i_raw) * jax.nn.sigmoid(-f_raw)
        a = jnp.exp(jax.nn.log_sigmoid(f_raw))
        o = _hgrn_scan(a, i)
        g = jnp.einsum('btd,de->bte', x, Wg)
        rms = o * jax.lax.rsqrt(jnp.mean(o * o, axis=-1, keepdims=True) + EPS)
        o = rms * g_norm_weight * (g * jax.nn.sigmoid(g))
        return jnp.einsum('btd,de->bte', o, Wo)

    def _L1_xattn_ref(h, adj_raw, Wq, Wk, gamma_raw):
        import jax, jax.numpy as jnp
        import numpy as np
        B, N, D = (16, 256, 64)
        H = 4
        TOP_K_RATIO = 0.3
        b, n, dm = h.shape
        d = dm // H
        Q = (h @ Wq.T).reshape(b, n, H, d).transpose(0, 2, 1, 3)
        K = (h @ Wk.T).reshape(b, n, H, d).transpose(0, 2, 1, 3)
        sim = jnp.einsum('bhnd,bhmd->bnm', Q, K) / (jnp.sqrt(jnp.float32(d)) * H)
        k = max(1, int(n * TOP_K_RATIO))
        topk_vals = jax.lax.top_k(sim, k)[0]
        threshold = topk_vals[:, :, -1:]
        sparse_mask = (sim >= threshold).astype(sim.dtype)
        A_learned = jax.nn.sigmoid(sim) * sparse_mask
        A_learned = (A_learned + jnp.swapaxes(A_learned, -1, -2)) * 0.5
        gamma = jax.nn.sigmoid(gamma_raw)
        return (1.0 - gamma) * adj_raw + gamma * A_learned

    def _L1_ffn_ref(x, gate_w, w_gate, w_up, w_down, sh_gate, sh_up, sh_down, se_gate_w):
        import jax, jax.numpy as jnp
        import numpy as np
        N_EXPERTS = 8
        TOP_K = 2
        C = 256
        H = 128
        HS = 256
        B, T = (1, 64)
        SCALE = 0.02
        Bb, Tt, Cc = x.shape
        xf = x.reshape(-1, Cc)
        scores = xf @ gate_w.T
        ew, ei = jax.lax.top_k(scores, TOP_K)
        ew = jax.nn.softmax(ew, axis=-1)
        x1 = jax.nn.silu(jnp.einsum('td,ehd->teh', xf, w_gate))
        x3 = jnp.einsum('td,ehd->teh', xf, w_up)
        expert_out = jnp.einsum('teh,edh->ted', x1 * x3, w_down)
        onehot = jax.nn.one_hot(ei, N_EXPERTS, dtype=ew.dtype)
        comb = jnp.einsum('ta,tae->te', ew, onehot)
        routed = jnp.einsum('te,ted->td', comb, expert_out)
        shared = jax.nn.silu(xf @ sh_gate.T) * (xf @ sh_up.T) @ sh_down.T
        sgate = jax.nn.sigmoid(xf @ se_gate_w.T)
        return (routed + sgate * shared).reshape(Bb, Tt, Cc)
    x = _layernorm(x + _L0_attn_ref(x, L0_attn_W_in, L0_attn_conv_kernel, L0_attn_conv_bias, L0_attn_W_x, L0_attn_W_dt, L0_attn_b_dt, L0_attn_W_out, L0_attn_A_log, L0_attn_D), axis=-1)
    x = _layernorm(x + _L0_xattn_ref(x, ctx_512, L0_xattn_W_k, L0_xattn_b_k, L0_xattn_ln_gamma, L0_xattn_ln_beta), axis=-1)
    x = _layernorm(x + _L0_ffn_ref(x, L0_ffn_Wr, L0_ffn_Wg, L0_ffn_Wu, L0_ffn_Wd, L0_ffn_Wsg, L0_ffn_Wsu, L0_ffn_Wsd), axis=-1)
    x = _layernorm(x + _L1_attn_ref(x, L1_attn_Wi, L1_attn_Wf, L1_attn_Wg, L1_attn_Wo, L1_attn_g_norm_weight), axis=-1)
    x = _layernorm(x + _L1_xattn_ref(ctx_512, x, L1_xattn_Wq, L1_xattn_Wk, L1_xattn_gamma_raw), axis=-1)
    x = _layernorm(x + _L1_ffn_ref(x, L1_ffn_gate_w, L1_ffn_w_gate, L1_ffn_w_up, L1_ffn_w_down, L1_ffn_sh_gate, L1_ffn_sh_up, L1_ffn_sh_down, L1_ffn_se_gate_w), axis=-1)
    return x

_drawn_inputs = setup_inputs


def setup_inputs(seed=0):
    import zlib

    import numpy as np

    out = dict(_drawn_inputs(seed))
    spreads = {'L0_xattn_b_k': (0.0, 0.8),
     'L0_xattn_ln_gamma': (1.0, 0.6),
     'L0_xattn_ln_beta': (0.0, 0.8),
     'L1_attn_g_norm_weight': (1.0, 0.6)}
    factors = {'L0_attn_conv_bias': 8.0,
     'L0_attn_b_dt': 8.0,
     'L0_xattn_W_k': 8.0,
     'L0_ffn_Wr': 8.0,
     'L0_ffn_Wg': 8.0,
     'L0_ffn_Wu': 8.0,
     'L0_ffn_Wd': 8.0,
     'L0_ffn_Wsg': 2.881,
     'L0_ffn_Wsu': 2.849,
     'L0_ffn_Wsd': 2.85,
     'L1_attn_Wi': 3.505,
     'L1_attn_Wf': 8.0,
     'L1_attn_Wg': 3.448,
     'L1_attn_Wo': 3.456,
     'L1_ffn_gate_w': 7.612,
     'L1_ffn_w_gate': 6.74,
     'L1_ffn_w_up': 6.633,
     'L1_ffn_w_down': 6.663,
     'L1_ffn_sh_gate': 6.706,
     'L1_ffn_sh_up': 6.625,
     'L1_ffn_sh_down': 6.617,
     'L1_ffn_se_gate_w': 8.0}
    for name, (base, spread) in spreads.items():
        noise = np.random.default_rng([zlib.crc32(name.encode()), seed]).standard_normal(out[name].shape)
        drawn = base * np.exp(spread * noise) if base else spread * noise
        out[name] = jnp.asarray(drawn.astype(out[name].dtype))
    for name, factor in factors.items():
        out[name] = (out[name] * factor).astype(out[name].dtype)
    return out
```

```python
from contextlib import ExitStack

import concourse.bass as bass
from concourse import mybir

F32 = mybir.dt.float32
BF16 = mybir.dt.bfloat16
U32 = mybir.dt.uint32
ALU = mybir.AluOpType
ACT = mybir.ActivationFunctionType
AX = mybir.AxisListType

P = 128
B, L, H = 4, 256, 256
LT = L // P
HT = H // P
E, N, TR, KC = 512, 16, 128, 4
ET = E // P
C = 64
TOPK = int(L * 0.3)
F0E, F0F, F0S = 8, 176, 352
F1E, F1F, F1S = 8, 128, 256
F0, F1 = F0E * F0F + F0S, F1E * F1F + F1S
F0T, F1T = -(-F0 // P), F1 // P
G = 8
GN = N // G
ROUNDS = -(-TOPK // 8)
DA_RING, DB_RING, ST_RING = 6, 8, 8


DOWN0, DOWN1 = 3 + F0T // 2, 3 + F1T // 2


def rest_steps():
    sizes = [("out", 3), ("xat0", 5), ("ffn0", DOWN0 + 2), ("hgrn", 6), ("ffn1", DOWN1 + 2)]
    return [(stage, k) for stage, n in sizes for k in range(n)]


def timeline():
    order = [("init", 0, 0)] + [("pre", 0, k) for k in range(4)]
    scans = [[("scan", b, g) for g in range(G + 1)] for b in range(B)]
    adjs = [[("adj", b, k) for k in range(ROUNDS + 5)] for b in range(B)]
    rest = [[(s, b, k) for s, k in rest_steps()] for b in range(B)]

    def merge(*lists):
        out = []
        for l in lists:
            out += [((i + 0.5) / len(l), x) for i, x in enumerate(l)]
        return [x for _, x in sorted(out, key=lambda y: y[0])]

    order += merge(scans[0], adjs[0]) + [("init", 0, 1)]
    order += [("pre", 1, k) for k in range(4)]
    for b in range(1, B):
        order += merge(scans[b], adjs[b], rest[b - 1])
        if b + 1 < B:
            order += [("pre", b + 1, k) for k in range(4)]
    return order + rest[B - 1]


BANKS = {
    ("pre", 0): ["hid0", "hid1"], ("pre", 1): ["dtbc"], ("pre", 2): ["z0", "z1"],
    ("pre", 3): ["duT0", "duT1"],
    ("adj", 0): ["qk"], ("adj", 1): ["sim"], ("adj", ROUNDS + 4): ["adjT"],
    ("out", 0): ["kv", "gate0", "gate1", "yT0", "yT1"], ("out", 1): ["mamba", "gram"],
    ("xat0", 0): ["x1T"], ("xat0", 1): ["att"],
    ("ffn0", 0): ["x2T"], ("ffn0", 1): ["logit0"], ("ffn0", 2): ["w0T"],
    ("ffn0", DOWN0): ["ffn0"],
    ("hgrn", 0): ["x3T"], ("hgrn", 1): ["hi", "hf", "hg"], ("hgrn", 2): ["ss", "hgrn"],
    ("ffn1", 0): ["x5T"], ("ffn1", 1): ["logit1"], ("ffn1", 2): ["w1T"],
    ("ffn1", DOWN1): ["ffn1"],
}
for _t in range(F0T // 2):
    BANKS["ffn0", 3 + _t] = [f"g0_{_t}", f"u0_{_t}"] + ([f"e0_{_t}"] if 2 * P * _t < F0E * F0F else [])
for _t in range(F1T // 2):
    BANKS["ffn1", 3 + _t] = [f"g1_{_t}", f"u1_{_t}", f"e1_{_t}"]


ROOTS = [("out", 1), ("xat0", 1), ("xat0", 3), ("ffn0", DOWN0), ("hgrn", 2), ("hgrn", 3), ("hgrn", 4), ("ffn1", DOWN1)]
ROWS = [("out", 2), ("xat0", 4), ("ffn0", DOWN0 + 1), ("hgrn", 4), ("hgrn", 5), ("ffn1", DOWN1 + 1)]


def decoder(nc, d, out):
    order = timeline()
    with ExitStack() as ctx:
        def sb(name, shape, dt=F32):
            return ctx.enter_context(nc.sbuf_tensor(name, shape, dt))

        def sem(name):
            return ctx.enter_context(nc.semaphore(name))

        loads = []
        xT = sb("xT", [P, 2, HT, L])
        ctxT = sb("ctxT", [C, 2, L])
        loads.append((xT[:, 0], d["xT"][:, :, 0:L], 0))

        def load(name, shape, src, part, dst=None, dt=F32):
            t = sb(name, shape, dt)
            loads.append((t[:] if dst is None else dst(t), src, part))
            return t

        w_in = load("w_in", [P, HT, 2 * E], d["w_in"], 0)
        cw = load("cw", [P, ET, KC], d["cw"], 0)
        cb = load("cb", [P, ET], d["cb"], 0)
        ident = load("ident", [P, P], d["ident"], 0)
        w_x = load("w_x", [P, ET, TR + 2 * N], d["w_x"], 1)
        w_dt = load("w_dt", [P, E], d["w_dt"], 1)
        b_dt = load("b_dt", [P, ET], d["b_dt"], 1)
        a_log = load("a_log", [P, ET, N], d["a_log"], 1)
        loads.append((ctxT[:, 0], d["ctxT"][:, 0:L], 2))
        loads.append((ctxT[:, 1], d["ctxT"][:, L:2 * L], 2))
        loads.append((xT[:, 1], d["xT"][:, :, L:2 * L], 2))
        wqT = load("wqT", [C, C], d["wqT"], 2)
        wkT = load("wkT", [C, C], d["wkT"], 2)
        wkvT = load("wkvT", [C, C], d["wkvT"], 2)
        b_k = load("b_k", [C, 1], d["b_k"], 2)
        gam = load("gam", [P, 1], d["gam"].partition_broadcast(P), 2)
        skip = load("skip", [P, ET], d["skip"], 3)
        w_out = load("w_out", [P, ET, H], d["w_out"], 3)
        even, odd = sb("even", [P, LT, H]), sb("odd", [P, LT, H])
        loads.append((even[:, :, :], d["x"][:, 0:LT, :], 3))
        lng = load("lng", [P, L], d["lng"].partition_broadcast(P), 3)
        lnb = load("lnb", [P, L], d["lnb"].partition_broadcast(P), 3)
        iota = load("iota", [P, F0E], d["iota"].partition_broadcast(P), 3)
        sel0 = load("sel0", [3 * F0E, F0E * F0F], d["sel0"], 3, dt=BF16)
        sel1 = load("sel1", [3 * (F1E + 1), F1], d["sel1"], 3, dt=BF16)
        wr = load("wr", [P, HT, F0E], d["wr"], 3)
        wg0 = load("wg0", [P, HT, F0T * P], d["wg0"], 3, dst=lambda t: t[:, :, 0:F0])
        wu0 = load("wu0", [P, HT, F0T * P], d["wu0"], 3, dst=lambda t: t[:, :, 0:F0])
        full0 = F0 // P
        wd = sb("wd", [P, F0T, H])
        whi = load("whi", [P, HT, H], d["whi"], 4)
        whf = load("whf", [P, HT, H], d["whf"], 4)
        whg = load("whg", [P, HT, H], d["whg"], 4)
        who = load("who", [P, HT, H], d["who"], 4)
        gn = load("gn", [P, HT], d["gn"], 4)
        wr1 = load("wr1", [P, HT, F1E + 1], d["wr1"], 4)
        wg1 = load("wg1", [P, HT, F1], d["wg1"], 4)
        wu1 = load("wu1", [P, HT, F1], d["wu1"], 4)
        PARTS = 5

        a_neg = sb("a_neg", [P, ET, N])
        ones = sb("ones", [P, 1])
        mhalf = sb("mhalf", [P, LT])
        gth = sb("gth", [P, 1])
        gq = sb("gq", [P, 1])
        g2 = sb("g2", [P, 1])

        big = sb("big", [P, F0T, L])
        conv, za, zr = big[:, 0:ET, :], big[:, ET:2 * ET, :], big[:, 2 * ET:3 * ET, :]
        du, sg, yg = conv, za, zr
        si, tf, sgg, o, sq = (big[:, HT * i:HT * (i + 1), :] for i in range(5))

        hs = sb("hs", [P, 2, ET, L])
        dtbc = sb("dtbc", [P, 2, L + LT * 2 * N])
        dts = sb("dts", [P, ET, L])
        duT = sb("duT", [P, LT, E])
        dA = sb("dA", [P, DA_RING, GN, L])
        dbT = sb("dbT", [P, DB_RING, E])
        st = sb("st", [P, ST_RING, GN * L])
        acc = sb("acc", [P, LT, E])
        qk = sb("qk", [C, 2 * L])
        kv = sb("kv", [C, L])
        gram = sb("gram", [P, LT, L])
        sim = sb("sim", [P, LT, L])
        wk = sb("wk", [P, LT, L])
        m8 = sb("m8", [P, LT, 8])
        S = sb("S", [P, LT, L])
        rows = [even, odd] * 3 + [even]
        r = sb("r", [P, LT, H])
        gu = r
        xsT = sb("xsT", [P, HT, L])
        gs = sb("gs", [P, 2, 2, L])
        ex = gs[:, 0]
        bst = sb("bst", [P, LT, 6])
        mv = sb("mv", [P, LT, 2])
        var = sb("var", [P, LT])
        rstd = sb("rstd", [P, LT])
        nmx = sb("nmx", [P, LT])
        es = sb("es", [P, LT])
        ri = sb("ri", [P, LT])
        dsc = sb("dsc", [P, LT, 2])
        ths = sb("ths", [P, LT, 2])
        lgs = sb("lgs", [P, LT, F1E + 1])
        exr = sb("exr", [P, LT, F0E])
        sc = sb("sc", [P, LT, F0E])
        t8 = sb("t8", [P, LT, 8])
        i8 = sb("i8", [P, LT, 8], U32)
        if8 = sb("if8", [P, LT, 2])
        pr = sb("pr", [P, LT, 2])
        wa = sb("wa", [P, LT, F0E])
        wb = sb("wb", [P, LT, F0E])
        wf = sb("wf", [P, LT, 2, F1E + 1])
        whl = sb("whl", [P, LT, 3 * (F1E + 1)])
        wpart = sb("wpart", [P, LT, F1E + 1], BF16)
        wT = sb("wT", [3 * (F1E + 1), L], BF16)

        def bank(name):
            return ctx.enter_context(nc.psum_tensor(name, [P, 512], F32))

        dbu = [bank(f"dbu{i}") for i in range(2)]
        stT = [bank(f"stT{i}") for i in range(2)]
        work = [bank(f"work{i}") for i in range(4)]

        loaded = [sem(f"loaded{i}") for i in range(PARTS)]
        part_size = [16 * sum(1 for l in loads if l[2] == i) for i in range(PARTS)]
        work_full = [sem(f"work_full{i}") for i in range(4)]
        work_read = [sem(f"work_read{i}") for i in range(4)]
        names = """consts_ready a_exp a_ready gam_tanh conv0 conv_ready hs_ready abs_ready exp_ready sp_ready dts_ready
            du_ready dA_ready dbT_ready dbu_ready scan_done stT_ready acc_done th_ready adj_ready
            yg_ready var_ready rstd_ready rows_ready att_max att_exp att_norm nmx_ready dsc_ready ths_ready
            whl_ready init_late q_ready o_ready sq_ready dve_link out_done ctxT_loaded xT_loaded x_loaded wd_loaded mask_ready""".split()
        s = {n: sem(n) for n in names}

        use, root, row = {}, {}, {}
        for stage, b, k in order:
            for n in BANKS.get((stage, k), []):
                use[n, b] = (len(use) % 4, len(use) // 4)
            if (stage, k) in ROOTS:
                root[stage, b, k] = len(root) + 1
            if (stage, k) in ROWS:
                row[ROWS.index((stage, k)) + 1, b] = len(row) + 1
        pairs = [(n, b) for n, b in use if n[0] == "u" and "_" in n]

        def stq(b, g, t):
            return (b * G + g) * ET + t

        def whl_count(lay, b):
            return [x for x in order if x[0] in ("ffn0", "ffn1") and x[2] == 2].index((f"ffn{lay}", b, 2)) + 1

        def left(lay, c):
            return min(P, (F0, F1)[lay] - c * P)

        wd_count = {}
        for b in range(B):
            wd_count[0, b] = 16 * (3 * b + 2)
            wd_count[1, b] = 16 * (3 * b + 3)

        def work_bank(n, b):
            return work[use[n, b][0]]

        def full(n, b):
            return work_full[use[n, b][0]], use[n, b][1] + 1

        def read(n, b):
            return work_read[use[n, b][0]], use[n, b][1] + 1

        def halves(t):
            return t[:, :].rearrange("p (t l) -> p t l", t=2)

        block = ctx.enter_context(nc.Block())

        @block.sync
        def _(sp):
            for dst, src, part in loads:
                sp.dma_start(dst, src).then_inc(loaded[part], 16)

            def load_wd0():
                sp.dma_start(wd[:, 0:full0, :], d["wd0"][0:full0 * P, :].rearrange("(t p) h -> p t h", p=P))\
                    .then_inc(s["wd_loaded"], 16)
                sp.dma_start(wd[0:F0 - full0 * P, full0, :], d["wd0"][full0 * P:F0, :]).then_inc(s["wd_loaded"], 16)

            load_wd0()
            for stage, b, k in order:
                if (stage, k) == ("out", 0) and b + 2 < B:
                    sp.wait_ge(*full("kv", b))
                    sp.dma_start(ctxT[:, b % 2], d["ctxT"][:, (b + 2) * L:(b + 3) * L]).then_inc(s["ctxT_loaded"], 16)
                if (stage, k) == ("out", 0) and b + 2 < B:
                    sp.wait_ge(*full("gate1", b))
                    sp.dma_start(xT[:, b % 2], d["xT"][:, :, (b + 2) * L:(b + 3) * L]).then_inc(s["xT_loaded"], 16)
                if (stage, k) == ("ffn0", DOWN0 + 1):
                    sp.wait_ge(*full("ffn0", b))
                    sp.dma_start(wd[:, 0:F1T, :], d["wd1"]).then_inc(s["wd_loaded"], 16)
                if (stage, k) == ("ffn1", DOWN1 + 1):
                    sp.wait_ge(s["rows_ready"], row[6, b])
                    sp.dma_start(out[:, b * LT:(b + 1) * LT, :], rows[6][:, :, :]).then_inc(s["out_done"], 16)
                    if b + 1 < B:
                        load_wd0()
                        sp.wait_ge(s["out_done"], 16 * (b + 1))
                        sp.dma_start(rows[0][:, :, :], d["x"][:, (b + 1) * LT:(b + 2) * LT, :])\
                            .then_inc(s["x_loaded"], 16)
            sp.wait_ge(s["out_done"], 16 * B)

        @block.gpsimd
        def _(pool):
            gp = nc.gpsimd
            gp.memset(ones[:], 1.0)
            gp.memset(mhalf[:], -0.5)
            gp.memset(dA[:, :, :, 0:1], 0.0)
            gp.memset(wg0[:, :, F0:], 0.0)
            gp.memset(wu0[:, :, F0:], 0.0).then_inc(s["consts_ready"], 1)
            pool.wait_ge(s["consts_ready"], 1)
            var_ready = 0
            for stage, b, k in order:
                if stage == "scan" and k < G:
                    gi = b * G + k
                    if k == 0:
                        pool.wait_ge(*read("duT1", b))
                    if gi >= 2:
                        pool.wait_ge(s["dbu_ready"], (gi - 1) * ET)
                    for j in range(GN):
                        for lt in range(LT):
                            slot = (gi * GN * LT + j * LT + lt) % DB_RING
                            col = L + lt * 2 * N + k * GN + j
                            last = gp.tensor_scalar(dbT[:, slot, :], duT[:, lt, :], dtbc[:, b % 2, col:col + 1],
                                                    1.0, ALU.mult, ALU.mult)
                    last.then_inc(s["dbT_ready"], 1)
                if (stage, b, k) in root:
                    if stage == "hgrn" and k == 2:
                        pool.wait_ge(*read("ss", b))
                    else:
                        var_ready += 1
                        pool.wait_ge(s["var_ready"], var_ready)
                    gp.tensor_tensor(rstd[:, :], var[:, :], mhalf[:, :], ALU.pow).then_inc(s["rstd_ready"], 1)

        @block.tensor
        def _(pe):
            mm = nc.tensor.matmul

            def transpose(dst, src):
                return nc.tensor.transpose(dst, src, ident[:, :])

            def claim(n, b):
                i, u = use[n, b]
                if u:
                    pe.wait_ge(work_read[i], u)
                return work[i]

            def fill(last, n, b):
                last.then_inc(work_full[use[n, b][0]], 1)

            def transposes(n, b, src, rows_, cols, width=P):
                t = claim(n, b)
                for c in range(cols):
                    for r_ in range(rows_):
                        last = transpose(t[0:width, (c * rows_ + r_) * P:(c * rows_ + r_ + 1) * P], src(r_, c))
                fill(last, n, b)

            def product(t, col, lhs, rhs, depth, width):
                for c in range(depth):
                    last = mm(t[:, col:col + width], lhs(c), rhs(c), start=(c == 0), stop=(c == depth - 1))
                return last

            def in_projection(b, names, first):
                for i, n in enumerate(names):
                    t = claim(n, b)
                    for f in range(2):
                        m = first + (2 * i + f) * P
                        last = product(t, f * L, lambda c: w_in[:, c, m:m + P], lambda c: xT[:, b % 2, c, :], HT, L)
                    fill(last, n, b)

            def ffn(b, k, lay, wg, wu, sel, nexp, routed, wrt, h, tiles):
                down = 3 + tiles // 2
                if k == 0:
                    n = 2 if lay == 0 else 5
                    pe.wait_ge(s["rows_ready"], row[n, b])
                    transposes(f"x{n}T", b, lambda r_, c: rows[n][:, r_, c * P:(c + 1) * P], LT, HT)
                elif k == 1:
                    pe.wait_ge(*read(f"x{2 if lay == 0 else 5}T", b))
                    t = claim(f"logit{lay}", b)
                    for lt in range(LT):
                        last = product(t, lt * nexp, lambda c: xsT[:, c, lt * P:(lt + 1) * P], lambda c: wrt[:, c, :],
                                       HT, nexp)
                    fill(last, f"logit{lay}", b)
                elif k == 2:
                    pe.wait_ge(s["whl_ready"], whl_count(lay, b))
                    transposes(f"w{lay}T", b, lambda r_, c: whl[:, r_, 0:3 * nexp], LT, 1, 3 * nexp)
                elif k < down:
                    i = k - 3
                    for kind, w in (("g", wg), ("u", wu)):
                        n = f"{kind}{lay}_{i}"
                        t = claim(n, b)
                        for f in range(2):
                            m = (2 * i + f) * P
                            last = product(t, f * L, lambda c: w[:, c, m:m + P], lambda c: xsT[:, c, :], HT, L)
                        fill(last, n, b)
                    if f"e{lay}_{i}" in BANKS[f"ffn{lay}", k]:
                        n = f"e{lay}_{i}"
                        t = claim(n, b)
                        if i == 0:
                            pe.wait_ge(*read(f"w{lay}T", b))
                        for f in range(2):
                            m = (2 * i + f) * P
                            if m < routed:
                                last = mm(t[:, f * L:(f + 1) * L], sel[:, m:m + P], wT[0:3 * nexp, :],
                                          start=True, stop=True)
                        fill(last, n, b)
                elif k == down:
                    i = tiles // 2 - 1
                    pe.wait_ge(*read(BANKS[f"ffn{lay}", 3 + i][-1], b))
                    t = claim(f"ffn{lay}", b)
                    pe.wait_ge(s["wd_loaded"], wd_count[lay, b])
                    for lt in range(LT):
                        last = product(t, lt * H, lambda c: h[0:left(lay, c), c, lt * P:(lt + 1) * P],
                                       lambda c: wd[0:left(lay, c), c, :], tiles, H)
                    fill(last, f"ffn{lay}", b)

            for stage, b, k in order:
                p = b % 2
                if stage == "init" and k == 0:
                    pe.wait_ge(loaded[0], part_size[0])
                if stage == "init" and k == 1:
                    for i in range(1, PARTS):
                        pe.wait_ge(loaded[i], part_size[i])
                    pe.wait_ge(s["consts_ready"], 1)
                    pe.wait_ge(s["init_late"], 1)
                if stage == "pre" and k == 0:
                    if b >= 2:
                        pe.wait_ge(s["xT_loaded"], 16 * (b - 1))
                    in_projection(b, ["hid0", "hid1"], 0)
                if stage == "pre" and k == 1:
                    if b == 0:
                        pe.wait_ge(loaded[1], part_size[1])
                    t = claim("dtbc", b)
                    pe.wait_ge(s["hs_ready"], b + 1)
                    product(t, 0, lambda c: w_x[:, c, 0:TR], lambda c: hs[:, p, c, :], ET, L)
                    for lt in range(LT):
                        last = product(t, L + lt * 2 * N, lambda c: hs[:, p, c, lt * P:(lt + 1) * P],
                                       lambda c: w_x[:, c, TR:TR + 2 * N], ET, 2 * N)
                    fill(last, "dtbc", b)
                if stage == "pre" and k == 2:
                    pe.wait_ge(*read("dtbc", b))
                    for i in range(2):
                        t = claim(f"z{i}", b)
                        for f in range(2):
                            m = (2 * i + f) * P
                            last = product(t, f * L, lambda c: w_dt[:, m:m + P], lambda c: dtbc[:, p, 0:L], 1, L)
                        fill(last, f"z{i}", b)
                if stage == "pre" and k == 3:
                    pe.wait_ge(s["du_ready"], b + 1)
                    for lt in range(LT):
                        transposes(f"duT{lt}", b, lambda r_, c: du[:, r_, lt * P:(lt + 1) * P], ET, 1)
                if stage == "adj" and k == 0:
                    if b == 0:
                        pe.wait_ge(loaded[2], part_size[2])
                    if b >= 2:
                        pe.wait_ge(s["ctxT_loaded"], 16 * (b - 1))
                    t = claim("qk", b)
                    mm(t[0:C, 0:L], wqT[:, :], ctxT[:, p], start=True, stop=True)
                    fill(mm(t[0:C, L:2 * L], wkT[:, :], ctxT[:, p], start=True, stop=True), "qk", b)
                if stage == "adj" and k == 1:
                    pe.wait_ge(*read("qk", b))
                    t = claim("sim", b)
                    for lt in range(LT):
                        last = mm(t[:, lt * L:(lt + 1) * L], qk[:, lt * P:(lt + 1) * P], qk[:, L:2 * L],
                                  start=True, stop=True)
                    fill(last, "sim", b)
                if stage == "adj" and k == ROUNDS + 4:
                    pe.wait_ge(s["adj_ready"], b + 1)
                    transposes("adjT", b, lambda r_, c: wk[:, r_, c * P:(c + 1) * P], LT, LT)
                if stage == "scan":
                    gi = b * G + k
                    for t in range(ET):
                        if k < G:
                            i = gi * ET + t
                            if t == 0:
                                pe.wait_ge(s["dbT_ready"], gi + 1)
                            if i >= 2:
                                pe.wait_ge(s["scan_done"], i - 1)
                            for j in range(GN):
                                for lt in range(LT):
                                    slot = (gi * GN * LT + j * LT + lt) % DB_RING
                                    col = j * L + lt * P
                                    last = transpose(dbu[i % 2][:, col:col + P], dbT[:, slot, t * P:(t + 1) * P])
                            last.then_inc(s["dbu_ready"], 1)
                        if k > 0:
                            j, lt = divmod(t, LT)
                            qn = stq(b, k - 1, t)
                            if t == 0:
                                pe.wait_ge(s["scan_done"], gi * ET)
                            if qn >= 2:
                                pe.wait_ge(s["acc_done"], qn - 1)
                            for c in range(ET):
                                slot = ((gi - 1) * ET + c) % ST_RING
                                last = transpose(stT[qn % 2][:, c * P:(c + 1) * P],
                                                 st[:, slot, j * L + lt * P:j * L + (lt + 1) * P])
                            last.then_inc(s["stT_ready"], 1)
                if stage == "out" and k == 0:
                    t = claim("kv", b)
                    fill(mm(t[0:C, 0:L], wkvT[:, :], ctxT[:, p], start=True, stop=True), "kv", b)
                    in_projection(b, ["gate0", "gate1"], E)
                    pe.wait_ge(s["acc_done"], stq(b, G - 1, ET - 1) + 1)
                    for i in range(2):
                        transposes(f"yT{i}", b, lambda r_, c: acc[:, r_, (2 * i + c) * P:(2 * i + c + 1) * P],
                                   LT, 2)
                if stage == "out" and k == 1:
                    pe.wait_ge(s["yg_ready"], b + 1)
                    t = claim("mamba", b)
                    for lt in range(LT):
                        last = product(t, lt * H, lambda c: yg[:, c, lt * P:(lt + 1) * P], lambda c: w_out[:, c, :],
                                       ET, H)
                    fill(last, "mamba", b)
                    pe.wait_ge(*read("kv", b))
                    t = claim("gram", b)
                    for lt in range(LT):
                        last = mm(t[:, lt * L:(lt + 1) * L], kv[:, lt * P:(lt + 1) * P], kv[:, :],
                                  start=True, stop=True)
                    fill(last, "gram", b)
                if stage == "xat0" and k == 0:
                    pe.wait_ge(s["rows_ready"], row[1, b])
                    transposes("x1T", b, lambda r_, c: rows[1][:, r_, c * P:(c + 1) * P], LT, HT)
                if stage == "xat0" and k == 1:
                    pe.wait_ge(*read("x1T", b))
                    pe.wait_ge(*read("gram", b))
                    t = claim("att", b)
                    for lt in range(LT):
                        last = product(t, lt * L, lambda c: xsT[:, c, lt * P:(lt + 1) * P],
                                       lambda c: gram[:, c, :], LT, L)
                    fill(last, "att", b)
                if stage == "ffn0":
                    ffn(b, k, 0, wg0, wu0, sel0, F0E, F0E * F0F, wr, big, F0T)
                if stage == "ffn1":
                    ffn(b, k, 1, wg1, wu1, sel1, F1E + 1, F1, wr1, big, F1T)
                if stage == "hgrn" and k == 0:
                    pe.wait_ge(s["rows_ready"], row[3, b])
                    transposes("x3T", b, lambda r_, c: rows[3][:, r_, c * P:(c + 1) * P], LT, HT)
                if stage == "hgrn" and k == 1:
                    pe.wait_ge(*read("x3T", b))
                    for n, w in (("hi", whi), ("hf", whf), ("hg", whg)):
                        t = claim(n, b)
                        for f in range(HT):
                            last = product(t, f * L, lambda c: w[:, c, f * P:(f + 1) * P], lambda c: xsT[:, c, :],
                                           HT, L)
                        fill(last, n, b)
                if stage == "hgrn" and k == 2:
                    t = claim("ss", b)
                    pe.wait_ge(s["sq_ready"], b + 1)
                    for lt in range(LT):
                        last = product(t, lt, lambda c: sq[:, c, lt * P:(lt + 1) * P], lambda c: ones[:, :], HT, 1)
                    fill(last, "ss", b)
                    t = claim("hgrn", b)
                    pe.wait_ge(s["q_ready"], b + 1)
                    for lt in range(LT):
                        last = product(t, lt * H, lambda c: sgg[:, c, lt * P:(lt + 1) * P], lambda c: who[:, c, :],
                                       HT, H)
                    fill(last, "hgrn", b)

        @block.scalar
        def _(act):
            A = nc.scalar.activation

            def evacuate(n, b, dst, src=None, func=ACT.Copy, **kw):
                act.wait_ge(*full(n, b))
                A(dst, work_bank(n, b)[:, :] if src is None else src, func, **kw).then_inc(work_read[use[n, b][0]], 1)

            def ffn(b, k, lay, nexp, down):
                if k == 0:
                    n = f"x{2 if lay == 0 else 5}T"
                    evacuate(n, b, xsT[:, :, :].rearrange("p t l -> p (t l)"))
                elif k == 1 and lay == 0:
                    act.wait_ge(s["nmx_ready"], b + 1)
                    t = work_bank("logit0", b)
                    for lt in range(LT):
                        last = A(exr[:, lt, :], t[:, lt * nexp:(lt + 1) * nexp], ACT.Exp, bias=nmx[:, lt:lt + 1],
                                 accum_out=es[:, lt:lt + 1])
                    last.then_inc(work_read[use["logit0", b][0]], 1)
                elif k == 1:
                    act.wait_ge(s["dsc_ready"], b + 1)
                    A(ths[:, :, :], dsc[:, :, :], ACT.Tanh, scale=0.5).then_inc(s["ths_ready"], 1)
                elif k == 2:
                    evacuate(f"w{lay}T", b, wT[0:3 * nexp, :], work_bank(f"w{lay}T", b)[0:3 * nexp, 0:L])
                elif k < down:
                    n = f"g{lay}_{k - 3}"
                    i = pairs.index((f"u{lay}_{k - 3}", b))
                    if i >= 2:
                        act.wait_ge(*read(*pairs[i - 2]))
                    evacuate(n, b, gs[:, i % 2, :, :].rearrange("p t l -> p (t l)"), func=ACT.Silu)

            for stage, b, k in order:
                p = b % 2
                if stage == "init" and k == 0:
                    act.wait_ge(loaded[0], part_size[0])
                if stage == "pre" and k == 0:
                    if b >= 2:
                        act.wait_ge(*full("ffn1", b - 2))
                    for i in range(2):
                        act.wait_ge(*full(f"hid{i}", b))
                        for f in range(2):
                            t = 2 * i + f
                            last = A(conv[:, t, :], work_bank(f"hid{i}", b)[:, f * L:(f + 1) * L], ACT.Identity,
                                     scale=cw[:, t, KC - 1:KC], bias=cb[:, t:t + 1])
                        last.then_inc(s["conv0"], 1)
                    if b >= 2:
                        act.wait_ge(s["yg_ready"], b - 1)
                    act.wait_ge(*read("hid0", b))
                    act.wait_ge(*read("hid1", b))
                    A(hs[:, p], conv[:, :, :], ACT.Silu).then_inc(s["hs_ready"], 1)
                if stage == "pre" and k == 1:
                    evacuate("dtbc", b, dtbc[:, p, :], work_bank("dtbc", b)[:, 0:L + LT * 2 * N])
                if stage == "pre" and k == 2:
                    if b == 0:
                        act.wait_ge(loaded[1], part_size[1])
                        A(a_neg[:, :, :], a_log[:, :, :], ACT.Exp).then_inc(s["a_exp"], 1)
                    for i in range(2):
                        act.wait_ge(*full(f"z{i}", b))
                        for f in range(2):
                            t = 2 * i + f
                            src = work_bank(f"z{i}", b)[:, f * L:(f + 1) * L]
                            A(za[:, t, :], src, ACT.Abs, bias=b_dt[:, t:t + 1])
                            last = A(zr[:, t, :], src, ACT.Relu, bias=b_dt[:, t:t + 1])
                        last.then_inc(work_read[use[f"z{i}", b][0]], 1)
                    act.wait_ge(*read("z1", b))
                    A(za[:, :, :], za[:, :, :], ACT.Exp, scale=-1.0).then_inc(s["exp_ready"], 1)
                    act.wait_ge(s["exp_ready"], b + 1)
                    A(za[:, :, :], za[:, :, :], ACT.Ln, bias=1.0).then_inc(s["sp_ready"], 1)
                if stage == "pre" and k == 3:
                    for lt in range(LT):
                        evacuate(f"duT{lt}", b, duT[:, lt, :])
                if stage == "adj" and k == 0:
                    if b == 0:
                        act.wait_ge(loaded[2], part_size[2])
                        A(gth[:, :], gam[:, :], ACT.Tanh, scale=0.5).then_inc(s["gam_tanh"], 1)
                    evacuate("qk", b, qk[:, :], work_bank("qk", b)[0:C, :])
                if stage == "adj" and k == 1:
                    if b:
                        act.wait_ge(s["adj_ready"], b)
                    evacuate("sim", b, sim[:, :, :].rearrange("p t l -> p (t l)"), scale=1.0 / 16)
                if stage == "adj" and k == ROUNDS + 2:
                    act.wait_ge(s["mask_ready"], b + 1)
                    A(sim[:, :, :], sim[:, :, :], ACT.Tanh, scale=0.5).then_inc(s["th_ready"], 1)
                if stage == "scan" and k < G:
                    gi = b * G + k
                    if k == 0:
                        act.wait_ge(s["dts_ready"], b + 1)
                    if gi == 0:
                        act.wait_ge(s["a_ready"], 1)
                        act.wait_ge(s["consts_ready"], 1)
                    for t in range(ET):
                        i = gi * ET + t
                        if i >= DA_RING:
                            act.wait_ge(s["scan_done"], i - DA_RING + 1)
                        for j in range(GN):
                            n = k * GN + j
                            last = A(dA[:, i % DA_RING, j, 1:L], dts[:, t, 1:L], ACT.Exp,
                                     scale=a_neg[:, t, n:n + 1])
                        last.then_inc(s["dA_ready"], 1)
                if stage == "out" and k == 1:
                    evacuate("gram", b, gram[:, :, :].rearrange("p t l -> p (t l)"), scale=1.0 / 16)
                if stage == "out" and k == 0:
                    evacuate("kv", b, kv[:, :], work_bank("kv", b)[0:C, 0:L], func=ACT.Identity, bias=b_k[:, :])
                    for i in range(2):
                        evacuate(f"gate{i}", b, sg[:, 2 * i:2 * i + 2, :].rearrange("p t l -> p (t l)"),
                                 func=ACT.Silu)
                if stage == "xat0" and k == 0:
                    evacuate("x1T", b, xsT[:, :, :].rearrange("p t l -> p (t l)"))
                if stage == "xat0" and k == 2:
                    act.wait_ge(s["att_max"], b + 1)
                    for lt in range(LT):
                        last = A(ex[:, lt, :], ex[:, lt, :], ACT.Exp, bias=nmx[:, lt:lt + 1],
                                 accum_out=es[:, lt:lt + 1])
                    last.then_inc(s["att_exp"], 1)
                if stage == "ffn0":
                    ffn(b, k, 0, F0E, DOWN0)
                if stage == "ffn1":
                    ffn(b, k, 1, F1E + 1, DOWN1)
                if stage == "hgrn" and k == 0:
                    evacuate("x3T", b, xsT[:, :, :].rearrange("p t l -> p (t l)"))
                if stage == "hgrn" and k == 1:
                    for n, dst, func, scale in (("hi", si, ACT.Silu, 1.0), ("hf", tf, ACT.Tanh, 0.5),
                                                ("hg", sgg, ACT.Silu, 1.0)):
                        evacuate(n, b, dst[:, :, :].rearrange("p t l -> p (t l)"), func=func, scale=scale)
                    act.wait_ge(s["o_ready"], b + 1)
                    A(sq[:, :, :], o[:, :, :], ACT.Square).then_inc(s["sq_ready"], 1)

        @block.vector
        def _(dve):
            V = nc.vector
            links = [0]

            def link(ins):
                links[0] += 1
                ins.then_inc(s["dve_link"], 1)
                dve.wait_ge(s["dve_link"], links[0])

            def release(ins, n, b):
                ins.then_inc(work_read[use[n, b][0]], 1)

            def stats(src, eps):
                for lt in range(LT):
                    last = V.bn_stats(bst[:, lt, :], src(lt))
                link(last)
                for lt in range(LT):
                    last = V.bn_aggr(mv[:, lt, :], bst[:, lt, :])
                link(last)
                V.tensor_scalar(var[:, :], mv[:, :, 1], eps, None, ALU.add).then_inc(s["var_ready"], 1)

            def normalize(key, i, b):
                dve.wait_ge(s["rstd_ready"], root[key])
                for lt in range(LT):
                    last = V.tensor_scalar(rows[i][:, lt, :], r[:, lt, :], mv[:, lt, 0:1], rstd[:, lt:lt + 1],
                                           ALU.subtract, ALU.mult)
                last.then_inc(s["rows_ready"], 1)

            def add_bank(n, b, rows_):
                dve.wait_ge(*full(n, b))
                release(V.tensor_tensor(r[:, :, :], halves(work_bank(n, b)), rows_, ALU.add), n, b)
                dve.wait_ge(*read(n, b))
                stats(lambda lt: r[:, lt, :], 1e-5)

            def route(lay, b, prob, nexp):
                link(V.tensor_copy(if8[:, :, :], i8[:, :, 0:2]))
                for i, dst in ((0, wa), (1, wb)):
                    for lt in range(LT):
                        last = V.tensor_scalar(dst[:, lt, :], iota[:, :], if8[:, lt, i:i + 1], prob[:, lt, i:i + 1],
                                               ALU.is_equal, ALU.mult)
                link(last)
                link(V.tensor_tensor(wf[:, :, 0, 0:F0E], wa[:, :, :], wb[:, :, :], ALU.add))
                for part in range(3):
                    now, left = wf[:, :, part % 2, 0:nexp], wf[:, :, (part + 1) % 2, 0:nexp]
                    link(V.tensor_copy(wpart[:, :, 0:nexp], now))
                    last = V.tensor_copy(whl[:, :, part * nexp:(part + 1) * nexp], wpart[:, :, 0:nexp])
                    if part < 2:
                        link(V.tensor_tensor(left, now, wpart[:, :, 0:nexp], ALU.subtract))
                last.then_inc(s["whl_ready"], 1)

            def ffn(b, k, lay, nexp, routed, h, tiles, rows_in):
                down = 3 + tiles // 2
                if k == 1 and lay == 0:
                    dve.wait_ge(*full("logit0", b))
                    t = work_bank("logit0", b)[:, 0:LT * nexp].rearrange("p (t e) -> p t e", t=LT)
                    V.tensor_reduce(nmx[:, :], t, AX.X, ALU.max, negate=True).then_inc(s["nmx_ready"], 1)
                elif k == 2 and lay == 0:
                    dve.wait_ge(*read("logit0", b))
                    link(V.reciprocal(ri[:, :], es[:, :]))
                    for lt in range(LT):
                        last = V.tensor_scalar(sc[:, lt, :], exr[:, lt, :], ri[:, lt:lt + 1], None, ALU.mult)
                    link(last)
                    for lt in range(LT):
                        last = V.max(out=t8[:, lt, :], in_=sc[:, lt, :])
                    link(last)
                    for lt in range(LT):
                        last = V.max_index(out=i8[:, lt, :], in_max=t8[:, lt, :], in_values=sc[:, lt, :])
                    link(last)
                    route(0, b, t8, nexp)
                elif k == 1:
                    dve.wait_ge(*full("logit1", b))
                    t = work_bank("logit1", b)[:, 0:LT * nexp].rearrange("p (t e) -> p t e", t=LT)
                    release(V.tensor_copy(lgs[:, :, :], t), "logit1", b)
                    dve.wait_ge(*read("logit1", b))
                    for lt in range(LT):
                        last = V.max(out=t8[:, lt, :], in_=lgs[:, lt, 0:F1E])
                    link(last)
                    V.tensor_copy(dsc[:, :, 1], lgs[:, :, F1E])
                    V.tensor_tensor(dsc[:, :, 0], t8[:, :, 0], t8[:, :, 1], ALU.subtract)\
                        .then_inc(s["dsc_ready"], 1)
                    for lt in range(LT):
                        last = V.max_index(out=i8[:, lt, :], in_max=t8[:, lt, :], in_values=lgs[:, lt, 0:F1E])
                    link(last)
                elif k == 2:
                    dve.wait_ge(s["ths_ready"], b + 1)
                    V.tensor_scalar(pr[:, :, 0], ths[:, :, 0], 0.5, 0.5, ALU.mult, ALU.add)
                    V.tensor_scalar(wf[:, :, 0, F1E], ths[:, :, 1], 0.5, 0.5, ALU.mult, ALU.add)
                    link(V.tensor_scalar(pr[:, :, 1], ths[:, :, 0], -0.5, 0.5, ALU.mult, ALU.add))
                    route(1, b, pr, nexp)
                elif 3 <= k < down:
                    i = k - 3
                    m = pairs.index((f"u{lay}_{i}", b)) % 2
                    un, en = f"u{lay}_{i}", f"e{lay}_{i}"
                    dve.wait_ge(*read(f"g{lay}_{i}", b))
                    dve.wait_ge(*full(un, b))
                    u = halves(work_bank(un, b))
                    weighted = max(0, min(2, routed // P - 2 * i))
                    if weighted < 2:
                        last = V.tensor_tensor(h[:, 2 * i + weighted:2 * i + 2, :], gs[:, m, weighted:2, :],
                                               u[:, weighted:2, :], ALU.mult)
                    if weighted:
                        if i:
                            dve.wait_ge(*read(f"e{lay}_{i - 1}", b))
                        last = V.tensor_tensor(gu[:, 0:weighted, :], gs[:, m, 0:weighted, :], u[:, 0:weighted, :],
                                               ALU.mult)
                    release(last, un, b)
                    if weighted:
                        dve.wait_ge(*read(un, b))
                        dve.wait_ge(*full(en, b))
                        release(V.tensor_tensor(h[:, 2 * i:2 * i + weighted, :], gu[:, 0:weighted, :],
                                                halves(work_bank(en, b))[:, 0:weighted, :], ALU.mult), en, b)
                elif k == down:
                    add_bank(f"ffn{lay}", b, rows[rows_in][:, :, :])
                elif k == down + 1:
                    normalize((f"ffn{lay}", b, down), rows_in + 1, b)

            for stage, b, k in order:
                p = b % 2
                if stage == "init" and k == 0:
                    dve.wait_ge(loaded[0], part_size[0])
                if stage == "init" and k == 1:
                    dve.wait_ge(loaded[3], part_size[3])
                    dve.wait_ge(loaded[4], part_size[4])
                    for t in range(HT):
                        last = V.tensor_scalar(who[:, t, :], who[:, t, :], gn[:, t:t + 1], -1.0,
                                               ALU.mult, ALU.mult)
                    last.then_inc(s["init_late"], 1)
                if stage == "pre" and k == 0:
                    for i in range(2):
                        dve.wait_ge(s["conv0"], 2 * b + i + 1)
                        for tap in range(KC - 2, -1, -1):
                            off = KC - 1 - tap
                            for f in range(2):
                                t = 2 * i + f
                                last = V.scalar_tensor_tensor(
                                    out=conv[:, t, off:L], in0=work_bank(f"hid{i}", b)[:, f * L:(f + 1) * L - off],
                                    scalar=cw[:, t, tap:tap + 1], in1=conv[:, t, off:L], op0=ALU.mult, op1=ALU.add)
                            if tap:
                                link(last)
                        release(last, f"hid{i}", b)
                if stage == "pre" and k == 2:
                    if b == 0:
                        dve.wait_ge(s["a_exp"], 1)
                        V.tensor_scalar(a_neg[:, :, :], a_neg[:, :, :], -1.0, None, ALU.mult)\
                            .then_inc(s["a_ready"], 1)
                    dve.wait_ge(s["sp_ready"], b + 1)
                    V.tensor_tensor(dts[:, :, :], zr[:, :, :], za[:, :, :], ALU.add).then_inc(s["dts_ready"], 1)
                    dve.wait_ge(s["dts_ready"], b + 1)
                    V.tensor_tensor(du[:, :, :], dts[:, :, :], hs[:, p], ALU.mult).then_inc(s["du_ready"], 1)
                if stage == "adj" and 2 <= k < ROUNDS + 2:
                    i = k - 2
                    if i == 0:
                        dve.wait_ge(*read("sim", b))
                    src = sim if i == 0 else wk
                    for lt in range(LT):
                        last = V.max(out=m8[:, lt, :], in_=src[:, lt, :])
                    link(last)
                    if i < ROUNDS - 1:
                        for lt in range(LT):
                            last = V.match_replace(out=wk[:, lt, :], in_to_replace=m8[:, lt, :],
                                                   in_values=src[:, lt, :], imm_value=-3.0e38)
                        link(last)
                if stage == "adj" and k == ROUNDS + 2:
                    if b == 0:
                        dve.wait_ge(s["gam_tanh"], 1)
                        V.tensor_scalar(gq[:, :], gth[:, :], 0.125, 0.125, ALU.mult, ALU.add)
                        link(V.tensor_scalar(g2[:, :], gth[:, :], -0.5, 1.5, ALU.mult, ALU.add))
                    at = (TOPK - 1) % 8
                    for lt in range(LT):
                        last = V.tensor_scalar(wk[:, lt, :], sim[:, lt, :], m8[:, lt, at:at + 1], gq[:, 0:1],
                                               ALU.is_ge, ALU.mult)
                    last.then_inc(s["mask_ready"], 1)
                if stage == "adj" and k == ROUNDS + 3:
                    dve.wait_ge(s["th_ready"], b + 1)
                    V.scalar_tensor_tensor(out=wk[:, :, :], in0=sim[:, :, :], scalar=1.0, in1=wk[:, :, :],
                                           op0=ALU.add, op1=ALU.mult).then_inc(s["adj_ready"], 1)
                if stage == "adj" and k == ROUNDS + 4:
                    dve.wait_ge(*full("adjT", b))
                    release(V.tensor_tensor(S[:, :, :], wk[:, :, :], halves(work_bank("adjT", b)), ALU.add), "adjT", b)
                if stage == "scan":
                    gi = b * G + k
                    for t in range(ET):
                        if k < G:
                            i = gi * ET + t
                            dve.wait_ge(s["dA_ready"], i + 1)
                            dve.wait_ge(s["dbu_ready"], i + 1)
                            V.tensor_tensor_scan(st[:, i % ST_RING, :],
                                                 dA[:, i % DA_RING].rearrange("p j l -> p (j l)"), dbu[i % 2][:, :],
                                                 0.0, ALU.mult, ALU.add).then_inc(s["scan_done"], 1)
                        if k > 0:
                            j, lt = divmod(t, LT)
                            n = (k - 1) * GN + j
                            qn = stq(b, k - 1, t)
                            dve.wait_ge(s["stT_ready"], qn + 1)
                            if qn >= 2:
                                dve.wait_ge(s["acc_done"], qn - 1)
                            col = L + lt * 2 * N + N + n
                            cs = dtbc[:, p, col:col + 1]
                            if n == 0:
                                ins = V.tensor_scalar(acc[:, lt, :], stT[qn % 2][:, :], cs, None, ALU.mult)
                            else:
                                ins = V.scalar_tensor_tensor(out=acc[:, lt, :], in0=stT[qn % 2][:, :], scalar=cs,
                                                             in1=acc[:, lt, :], op0=ALU.mult, op1=ALU.add)
                            ins.then_inc(s["acc_done"], 1)
                if stage == "out" and k == 0:
                    for i in range(2):
                        dve.wait_ge(*full(f"yT{i}", b))
                        for f in range(2):
                            t = 2 * i + f
                            last = V.scalar_tensor_tensor(out=yg[:, t, :], in0=hs[:, p, t, :], scalar=skip[:, t:t + 1],
                                                          in1=work_bank(f"yT{i}", b)[:, f * L:(f + 1) * L],
                                                          op0=ALU.mult, op1=ALU.add)
                        release(last, f"yT{i}", b)
                    dve.wait_ge(*read("yT1", b))
                    dve.wait_ge(*read("gate1", b))
                    V.tensor_tensor(yg[:, :, :], yg[:, :, :], sg[:, :, :], ALU.mult).then_inc(s["yg_ready"], 1)
                if stage == "out" and k == 1:
                    if b:
                        dve.wait_ge(s["x_loaded"], 16 * b)
                    else:
                        dve.wait_ge(loaded[3], part_size[3])
                    add_bank("mamba", b, rows[0][:, :, :])
                if stage == "out" and k == 2:
                    normalize(("out", b, 1), 1, b)
                if stage == "xat0" and k == 1:
                    dve.wait_ge(*full("att", b))
                    stats(lambda lt: work_bank("att", b)[:, lt * L:(lt + 1) * L], 1e-6)
                if stage == "xat0" and k == 2:
                    dve.wait_ge(s["rstd_ready"], root["xat0", b, 1])
                    for lt in range(LT):
                        last = V.tensor_scalar(ex[:, lt, :], work_bank("att", b)[:, lt * L:(lt + 1) * L],
                                               mv[:, lt, 0:1], rstd[:, lt:lt + 1], ALU.subtract, ALU.mult)
                    release(last, "att", b)
                    dve.wait_ge(*read("att", b))
                    for lt in range(LT):
                        last = V.tensor_tensor(ex[:, lt, :], ex[:, lt, :], lng[:, :], ALU.mult)
                    link(last)
                    for lt in range(LT):
                        last = V.tensor_tensor(ex[:, lt, :], ex[:, lt, :], lnb[:, :], ALU.add)
                    link(last)
                    V.tensor_reduce(nmx[:, :], ex[:, :, :], AX.X, ALU.max, negate=True).then_inc(s["att_max"], 1)
                if stage == "xat0" and k == 3:
                    dve.wait_ge(s["att_exp"], b + 1)
                    link(V.reciprocal(ri[:, :], es[:, :]))
                    for lt in range(LT):
                        last = V.scalar_tensor_tensor(out=r[:, lt, :], in0=ex[:, lt, :], scalar=ri[:, lt:lt + 1],
                                                      in1=rows[1][:, lt, :], op0=ALU.mult, op1=ALU.add)
                    link(last)
                    stats(lambda lt: r[:, lt, :], 1e-5)
                if stage == "xat0" and k == 4:
                    normalize(("xat0", b, 3), 2, b)
                if stage == "ffn0":
                    ffn(b, k, 0, F0E, F0E * F0F, big, F0T, 2)
                if stage == "ffn1":
                    ffn(b, k, 1, F1E + 1, F1, big, F1T, 5)
                if stage == "hgrn" and k == 1:
                    dve.wait_ge(*read("hf", b))
                    link(V.tensor_scalar(tf[:, :, :], tf[:, :, :], 0.5, 0.5, ALU.mult, ALU.add))
                    link(V.scalar_tensor_tensor(out=si[:, :, :], in0=tf[:, :, :], scalar=1.0, in1=si[:, :, :],
                                                op0=ALU.subtract, op1=ALU.mult))
                    for t in range(HT):
                        last = V.tensor_tensor_scan(o[:, t, :], tf[:, t, :], si[:, t, :], 0.0, ALU.mult, ALU.add)
                    last.then_inc(s["o_ready"], 1)
                    dve.wait_ge(s["o_ready"], b + 1)
                    dve.wait_ge(*read("hg", b))
                    V.tensor_tensor(sgg[:, :, :], o[:, :, :], sgg[:, :, :], ALU.mult).then_inc(s["q_ready"], 1)
                if stage == "hgrn" and k == 2:
                    dve.wait_ge(*full("ss", b))
                    release(V.tensor_scalar(var[:, :], work_bank("ss", b)[:, 0:LT], 1.0 / H, 1e-5, ALU.mult, ALU.add),
                            "ss", b)
                if stage == "hgrn" and k == 3:
                    dve.wait_ge(*full("hgrn", b))
                    dve.wait_ge(s["rstd_ready"], root["hgrn", b, 2])
                    for lt in range(LT):
                        last = V.scalar_tensor_tensor(out=r[:, lt, :], in0=work_bank("hgrn", b)[:, lt * H:(lt + 1) * H],
                                                      scalar=rstd[:, lt:lt + 1], in1=rows[3][:, lt, :],
                                                      op0=ALU.mult, op1=ALU.add)
                    release(last, "hgrn", b)
                    dve.wait_ge(*read("hgrn", b))
                    stats(lambda lt: r[:, lt, :], 1e-5)
                if stage == "hgrn" and k == 4:
                    normalize(("hgrn", b, 3), 4, b)
                    dve.wait_ge(s["rows_ready"], row[4, b])
                    link(V.scalar_tensor_tensor(out=r[:, :, :], in0=rows[4][:, :, :], scalar=g2[:, 0:1], in1=S[:, :, :],
                                                op0=ALU.mult, op1=ALU.add))
                    stats(lambda lt: r[:, lt, :], 1e-5)
                if stage == "hgrn" and k == 5:
                    normalize(("hgrn", b, 4), 5, b)


def kernel(**inputs):
    import ml_dtypes
    import numpy as np
    import concourse.bacc as bacc
    from concourse.bass_utils import run_bass_kernel_spmd

    v = {k: np.asarray(a) for k, a in inputs.items()}

    def tiles(a):
        return a.reshape(-1, P, a.shape[-1]).transpose(1, 0, 2)

    def up(routed, shared):
        return tiles(np.concatenate([routed.reshape(-1, H), shared], 0).T)

    def down(routed, shared):
        return np.concatenate([routed.transpose(0, 2, 1).reshape(-1, H), shared.T], 0)

    def members(width, n, rows):
        expert = np.minimum(np.arange(n) // width, rows - 1)
        return np.tile(expert[None, :] == np.arange(rows)[:, None], (3, 1)).astype(ml_dtypes.bfloat16)

    xf = v["x"].reshape(B * L, H)
    a = {
        "x": tiles(xf), "xT": tiles(xf.T), "ctxT": v["ctx_512"].reshape(B * L, C).T,
        "w_in": tiles(v["L0_attn_W_in"]), "cw": tiles(v["L0_attn_conv_kernel"].reshape(E, KC)),
        "cb": v["L0_attn_conv_bias"].reshape(ET, P).T, "w_x": tiles(v["L0_attn_W_x"]), "w_dt": v["L0_attn_W_dt"],
        "b_dt": v["L0_attn_b_dt"].reshape(ET, P).T, "a_log": tiles(v["L0_attn_A_log"]),
        "skip": v["L0_attn_D"].reshape(ET, P).T, "w_out": tiles(v["L0_attn_W_out"]),
        "wkvT": v["L0_xattn_W_k"].T, "b_k": v["L0_xattn_b_k"].reshape(C, 1),
        "lng": v["L0_xattn_ln_gamma"].reshape(L), "lnb": v["L0_xattn_ln_beta"].reshape(L),
        "wr": tiles(v["L0_ffn_Wr"].T), "wg0": up(v["L0_ffn_Wg"], v["L0_ffn_Wsg"]),
        "wu0": up(v["L0_ffn_Wu"], v["L0_ffn_Wsu"]), "wd0": down(v["L0_ffn_Wd"], v["L0_ffn_Wsd"]),
        "whi": tiles(v["L1_attn_Wi"]), "whf": tiles(v["L1_attn_Wf"]), "whg": tiles(v["L1_attn_Wg"]),
        "who": tiles(v["L1_attn_Wo"]), "gn": v["L1_attn_g_norm_weight"].reshape(HT, P).T,
        "wqT": v["L1_xattn_Wq"].T, "wkT": v["L1_xattn_Wk"].T, "gam": v["L1_xattn_gamma_raw"].reshape(1),
        "wr1": tiles(np.concatenate([v["L1_ffn_gate_w"], v["L1_ffn_se_gate_w"]], 0).T),
        "wg1": up(v["L1_ffn_w_gate"], v["L1_ffn_sh_gate"]), "wu1": up(v["L1_ffn_w_up"], v["L1_ffn_sh_up"]),
        "wd1": tiles(down(v["L1_ffn_w_down"], v["L1_ffn_sh_down"])),
        "ident": np.eye(P, dtype=np.float32), "iota": np.arange(F0E, dtype=np.float32),
        "sel0": members(F0F, F0E * F0F, F0E), "sel1": members(F1F, F1, F1E + 1),
    }
    arrays = {f"in_{k}": np.ascontiguousarray(t) for k, t in a.items()}
    nc = bacc.Bacc("TRN2", target_bir_lowering=False, num_devices=1)
    d = {k: nc.dram_tensor(f"in_{k}", arrays[f"in_{k}"].shape, mybir.dt.from_np(arrays[f"in_{k}"].dtype),
                           kind="ExternalInput").ap() for k in a}
    out = nc.dram_tensor("out", (P, B * LT, H), F32, kind="ExternalOutput").ap()
    decoder(nc, d, out)
    got = run_bass_kernel_spmd(nc, [arrays], core_ids=[0]).results[0]["out"]
    return got.transpose(1, 0, 2).reshape(B, L, H)
```

```python
from contextlib import ExitStack

import concourse.bass as bass
from concourse import mybir

F32 = mybir.dt.float32
BF16 = mybir.dt.bfloat16
U32 = mybir.dt.uint32
ALU = mybir.AluOpType
ACT = mybir.ActivationFunctionType
AX = mybir.AxisListType

P = 128
B, L, H = 4, 256, 256
LT = L // P
HT = H // P
E, N, TR, KC = 512, 16, 128, 4
ET = E // P
C = 64
TOPK = int(L * 0.3)
F0E, F0F, F0S = 8, 176, 352
F1E, F1F, F1S = 8, 128, 256
F0, F1 = F0E * F0F + F0S, F1E * F1F + F1S
F0T, F1T = -(-F0 // P), F1 // P
EP = ET // 2
ROUNDS = -(-TOPK // 8)
DA_RING, DBU_RING, ST_RING = 6, 4, 4
WORK = 5


DOWN0, DOWN1 = 3 + 3 * (F0T // 2), 3 + 3 * (F1T // 2)
DOWN_STEPS = 4


PRE_STEPS, ADJ_STEPS = 6, ROUNDS + 5


def rest_steps():
    def ffn(stage, down):
        gate, up, weigh = (list(range(3 + i, down, 3)) for i in range(3))
        steps = [0, 1, gate[0], up[0], 2]
        for i in range(1, len(gate)):
            steps += [gate[i], up[i], weigh[i - 1]]
        return [(stage, k) for k in steps + [weigh[-1]] + list(range(down, down + DOWN_STEPS + 1))]

    return ([("out", k) for k in range(4)] + [("xat0", k) for k in range(5)] + ffn("ffn0", DOWN0)
            + [("hgrn", k) for k in range(8)] + ffn("ffn1", DOWN1))


AT = {'out': [0, 0.25, 1.25, 1.25], 'xat0': [2.0, 2.5, 2.5, 2.5, 2.5], 'ffn0': [2.5, 3.0, 3.0, 3.0, 3.0, 3.25, 3.0, 3.0, 4.0, 4.0, 4.0, 5.25, 4.0, 5.25, 5.5, 5.5, 5.5, 6.25, 6.0, 6.0, 6.5, 6.25, 6.5, 6.5, 7.5, 7.5, 7.5, 8.0, 8.0], 'hgrn': [8.25, 9.0, 9.5, 9.75, 10.0, 10.0, 10.5, 10.75], 'ffn1': [11.0, 11.0, 11.5, 11.0, 11.0, 11.75, 11.75, 11.75, 13.25, 12.0, 12.75, 13.25, 13.25, 13.25, 13.25, 13.25, 13.25, 13.25, 14.0, 14.5, 15.0, 15.5, 16.75], 'adj': [1.5, 1.75, 1.75, 2.75, 4.0, 7.25, 7.25, 7.25, 8.0, 8.0, 12.5, 13.5, 14.0, 14.5, 15.25], 'pre': [8.0, 9.5, 10.75, 11.25, 13.25, 14.25], 'first adj': [-3.5, -1.25, -0.75, 0.75, 5.5, 8.5, 10.25, 10.25, 10.25, 10.25, 11.0, 11.75, 12.5, 15.75, 16.25], 'first pre': [9.25, 10.0, 11.25, 12.25, 13.75, 14.75]}
LAG = {('pe', 'ffn1', 4): -2, ('pool', 'ffn0', 21): 1, ('dve', 'adj', 8): -0.5, ('dve', 'ffn0', 19): 0.75, ('pool', 'ffn0', 4): 0.75, ('act', 'ffn1', 20): 0.25, ('dve', 'ffn0', 7): 1.5, ('pool', 'ffn1', 1): 1, ('pe', 'ffn1', 7): 1, ('pe', 'adj', 9): -0.5, ('pool', 'pre', 4): 0.75, ('pe', 'ffn0', 14): -1.75, ('pool', 'ffn0', 11): -0.25, ('dve', 'ffn0', 13): 0.5, ('act', 'ffn1', 16): -0.25, ('act', 'xat0', 1): -0.5, ('act', 'out', 3): -1.75, ('dve', 'pre', 3): 0.5, ('pe', 'ffn0', 2): -1.25, ('pool', 'ffn1', 5): 2, ('act', 'ffn0', 27): 0.75, ('act', 'ffn0', 17): -0.25, ('pe', 'ffn0', 19): -0.5, ('pe', 'adj', 7): 0.25, ('act', 'hgrn', 1): -1, ('pool', 'ffn0', 1): -0.5, ('dve', 'xat0', 4): -0.25, ('pool', 'ffn0', 13): 0.25, ('pool', 'ffn0', 12): 1.25, ('pe', 'adj', 2): -0.5, ('act', 'ffn1', 17): 1, ('pool', 'hgrn', 3): 0.5, ('pe', 'adj', 0): 0.25, ('dve', 'ffn1', 15): -0.25, ('dve', 'pre', 5): -0.5, ('pool', 'ffn0', 3): -1, ('act', 'ffn1', 1): 0.25, ('pe', 'out', 0): 0.5, ('pool', 'ffn1', 13): 1, ('pe', 'ffn0', 0): -1, ('pe', 'hgrn', 7): -0.5, ('act', 'ffn0', 12): 0.5, ('pe', 'ffn0', 17): -0.5, ('pool', 'ffn1', 18): 0.25, ('dve', 'xat0', 2): -0.25, ('dve', 'ffn1', 19): 1, ('act', 'ffn1', 14): 1, ('act', 'adj', 7): 1, ('pe', 'adj', 8): -0.25, ('act', 'out', 2): 1, ('pool', 'out', 3): -1, ('pool', 'hgrn', 2): 0.25, ('pe', 'xat0', 3): -0.25, ('dve', 'ffn1', 4): -0.25, ('act', 'out', 1): -1, ('act', 'ffn0', 26): -1, ('pool', 'ffn1', 9): -1, ('dve', 'ffn0', 25): -0.5, ('pe', 'hgrn', 6): -0.25, ('act', 'adj', 2): -0.25, ('pe', 'hgrn', 0): 0.25, ('act', 'ffn0', 11): 0.5, ('act', 'adj', 13): 1, ('pool', 'pre', 2): 0.25, ('act', 'ffn0', 25): -0.25, ('pool', 'ffn0', 25): -0.25, ('pool', 'ffn1', 22): -0.25, ('pe', 'adj', 12): 1, ('pool', 'out', 0): 0.5, ('act', 'adj', 4): 1, ('pool', 'hgrn', 6): -0.25, ('pe', 'ffn0', 3): 0.5}


def timeline(engine):
    order = [("init", 0, 0)]
    for b in range(B + 1):
        chains = [
            [("adj", b, k) for k in range(ADJ_STEPS)] if b < B else [],
            [(stage, b - 1, k) for stage, k in rest_steps()] if b else [],
            [("pre", b + 1, k) for k in range(PRE_STEPS)] if b + 1 < B else [],
        ]
        placed = [(k, step) for k, step in enumerate([("scan", b, k) for k in range(N + 1)] if b < B else [])]
        if b == 0:
            placed += [(k - PRE_STEPS, ("pre", 0, k)) for k in range(PRE_STEPS)]
        for steps in chains:
            place = -PRE_STEPS
            for step in steps:
                stage, _, k = step
                at = AT["first " + stage if b == 0 else stage][k]
                place = max(place, at + LAG.get((engine, stage, k), 0))
                placed.append((place, step))
        order += [step for _, step in sorted(placed, key=lambda x: x[0])]
        if b == 0:
            order.append(("init", 0, 1))
    return order


BANKS = {
    ("pre", 0): ["hid0", "hid1"], ("pre", 2): ["dtbc", "bT"], ("pre", 3): ["z0", "z1"],
    ("adj", 0): ["qk"], ("adj", 1): ["sim"], ("adj", ROUNDS + 4): ["adjT"],
    ("out", 0): ["kv", "gate0", "gate1"], ("out", 1): ["gram", "yT0", "yT1"], ("out", 2): ["mamba"],
    ("xat0", 0): ["x1T"], ("xat0", 1): ["att"],
    ("ffn0", 0): ["x2T"], ("ffn0", 1): ["logit0"], ("ffn0", 2): ["w0T"],
    ("ffn0", DOWN0): ["ffn0"],
    ("hgrn", 0): ["x3T"], ("hgrn", 1): ["hi"], ("hgrn", 2): ["hf"], ("hgrn", 3): ["hg"],
    ("hgrn", 4): ["ss", "hgrn"],
    ("ffn1", 0): ["x5T"], ("ffn1", 1): ["logit1"], ("ffn1", 2): ["w1T"],
    ("ffn1", DOWN1): ["ffn1"],
}
for _lay, _tiles, _routed in ((0, F0T, F0E * F0F), (1, F1T, F1)):
    for _t in range(_tiles // 2):
        BANKS[f"ffn{_lay}", 3 + 3 * _t] = [f"g{_lay}_{_t}"]
        BANKS[f"ffn{_lay}", 4 + 3 * _t] = [f"u{_lay}_{_t}"]
        BANKS[f"ffn{_lay}", 5 + 3 * _t] = [f"e{_lay}_{_t}"] if 2 * P * _t < _routed else []


SUM0, SUM1 = DOWN0 + DOWN_STEPS - 1, DOWN1 + DOWN_STEPS - 1
ROOTS = [("out", 2), ("xat0", 1), ("xat0", 3), ("ffn0", SUM0), ("hgrn", 4), ("hgrn", 5), ("hgrn", 6), ("ffn1", SUM1)]
ROWS = [("out", 3), ("xat0", 4), ("ffn0", SUM0 + 1), ("hgrn", 6), ("hgrn", 7), ("ffn1", SUM1 + 1)]


def decoder(nc, d, out):
    pe_order, dve_order, act_order, pool_order = (timeline(engine) for engine in ("pe", "dve", "act", "pool"))
    with ExitStack() as ctx:
        def sb(name, shape, dt=F32):
            return ctx.enter_context(nc.sbuf_tensor(name, shape, dt))

        def sem(name):
            return ctx.enter_context(nc.semaphore(name))

        loads = []
        xT = sb("xT", [P, 2, HT, L])
        ctxT = sb("ctxT", [C, 2, L])
        loads.append((xT[:, 0], d["xT"][:, :, 0:L], 0))

        def load(name, shape, src, part, dst=None, dt=F32):
            t = sb(name, shape, dt)
            loads.append((t[:] if dst is None else dst(t), src, part))
            return t

        w_in = load("w_in", [P, HT, 2 * E], d["w_in"], 0)
        cw = load("cw", [P, ET, KC], d["cw"], 0)
        cb = load("cb", [P, ET], d["cb"], 0)
        ident = load("ident", [P, P], d["ident"], 0)
        w_x = load("w_x", [P, ET, TR + P], d["w_x"], 1)
        w_dt = load("w_dt", [P, E], d["w_dt"], 1)
        b_dt = load("b_dt", [P, ET], d["b_dt"], 1)
        a_log = load("a_log", [P, ET, N], d["a_log"], 1)
        loads.append((ctxT[:, 0], d["ctxT"][:, 0:L], 2))
        loads.append((ctxT[:, 1], d["ctxT"][:, L:2 * L], 2))
        loads.append((xT[:, 1], d["xT"][:, :, L:2 * L], 2))
        wqT = load("wqT", [C, C], d["wqT"], 2)
        wkT = load("wkT", [C, C], d["wkT"], 2)
        wkvT = load("wkvT", [C, C], d["wkvT"], 2)
        b_k = load("b_k", [C, 1], d["b_k"], 2)
        gam = load("gam", [P, 1], d["gam"].partition_broadcast(P), 2)
        skip = load("skip", [P, ET], d["skip"], 3)
        w_out = load("w_out", [P, ET, H], d["w_out"], 3)
        even, odd = sb("even", [P, LT, H]), sb("odd", [P, LT, H])
        loads.append((even[:, :, :], d["x"][:, 0:LT, :], 3))
        lng = load("lng", [P, L], d["lng"].partition_broadcast(P), 3)
        lnb = load("lnb", [P, L], d["lnb"].partition_broadcast(P), 3)
        sel_b = load("sel_b", [P, N], d["sel_b"], 1, dt=BF16)
        iota = load("iota", [P, F0E], d["iota"].partition_broadcast(P), 3)
        sel0 = load("sel0", [3 * F0E, F0E * F0F], d["sel0"], 3, dt=BF16)
        sel1 = load("sel1", [3 * (F1E + 1), F1T], d["sel1"], 3, dt=BF16)
        wr = load("wr", [P, HT, F0E], d["wr"], 3)
        wg0 = load("wg0", [P, HT, F0T * P], d["wg0"], 3, dst=lambda t: t[:, :, 0:F0])
        wu0 = load("wu0", [P, HT, F0T * P], d["wu0"], 3, dst=lambda t: t[:, :, 0:F0])
        full0 = F0 // P
        wd = sb("wd", [P, F0T, H])
        whi = load("whi", [P, HT, H], d["whi"], 4)
        whf = load("whf", [P, HT, H], d["whf"], 4)
        whg = load("whg", [P, HT, H], d["whg"], 4)
        who = load("who", [P, HT, H], d["who"], 4)
        gn = load("gn", [P, HT], d["gn"], 4)
        wr1 = load("wr1", [P, HT, F1E + 1], d["wr1"], 4)
        wg1 = load("wg1", [P, HT, F1], d["wg1"], 4)
        wu1 = load("wu1", [P, HT, F1], d["wu1"], 4)
        PARTS = 5

        a_neg = sb("a_neg", [P, ET, N])
        ones = sb("ones", [P, 1])
        mhalf = sb("mhalf", [P, LT])
        gth = sb("gth", [P, 1])
        gq = sb("gq", [P, 1])
        g2 = sb("g2", [P, 1])

        big = sb("big", [P, F0T, L])
        sg, yg = big[:, 0:ET, :], big[:, ET:2 * ET, :]
        si, tf, sgg, o, sq = (big[:, HT * i:HT * (i + 1), :] for i in range(5))

        hs = sb("hs", [P, 2, ET, L])
        dtbc = sb("dtbc", [P, 2, L + LT * 2 * N])
        du = sb("du", [P, 2, ET, L])
        za = sb("za", [P, ET, L])
        dts = sb("dts", [P, 2, ET, L])
        bparts = sb("bparts", [P, 2, L], BF16)
        bb = sb("bb", [P, 2, 2, L])
        dA = sb("dA", [P, DA_RING, 2, L])
        dbu = sb("dbu", [P, DBU_RING, 2, L])
        st = sb("st", [P, ST_RING, 2 * L])
        acc = sb("acc", [P, LT, E])
        qk = sb("qk", [C, 2 * L])
        kv = sb("kv", [C, L])
        gram = sb("gram", [P, LT, L])
        sim = sb("sim", [P, LT, L])
        wk = sb("wk", [P, LT, L])
        m8 = sb("m8", [P, LT, 8])
        S = sb("S", [P, LT, L])
        rows = [even, odd] * 3 + [even]
        r = sb("r", [P, LT, H])
        xsT = sb("xsT", [P, HT, L])
        gs = sb("gs", [P, 2, 2, L])
        ex = gs[:, 0]
        bst = sb("bst", [P, LT, 6])
        mv = sb("mv", [P, LT, 2])
        var = sb("var", [P, LT])
        rstd = sb("rstd", [P, LT])
        nmx = sb("nmx", [P, LT])
        es = sb("es", [P, LT])
        ri = sb("ri", [P, LT])
        dsc = sb("dsc", [P, LT, 2])
        ths = sb("ths", [P, LT, 2])
        lgs = sb("lgs", [P, LT, F1E + 1])
        exr = sb("exr", [P, LT, F0E])
        sc = sb("sc", [P, LT, F0E])
        t8 = sb("t8", [P, LT, 8])
        i8 = sb("i8", [P, LT, 8], U32)
        if8 = sb("if8", [P, LT, 2])
        pr = sb("pr", [P, LT, 2])
        wa = sb("wa", [P, LT, F0E])
        wb = sb("wb", [P, LT, F0E])
        wf = sb("wf", [P, LT, 2, F1E + 1])
        whl = sb("whl", [P, LT, 3 * (F1E + 1)])
        wpart = sb("wpart", [P, LT, F1E + 1], BF16)
        wT = sb("wT", [3 * (F1E + 1), L], BF16)

        def bank(name):
            return ctx.enter_context(nc.psum_tensor(name, [P, 512], F32))

        bbank = bank("bbank")
        stT = [bank(f"stT{i}") for i in range(2)]
        work = [bank(f"work{i}") for i in range(WORK)]

        loaded = [sem(f"loaded{i}") for i in range(PARTS)]
        part_size = [16 * sum(1 for l in loads if l[2] == i) for i in range(PARTS)]
        work_full = [sem(f"work_full{i}") for i in range(WORK)]
        work_read = [sem(f"work_read{i}") for i in range(WORK)]
        names = """consts_ready a_exp a_ready gam_tanh conv0 conv_ready hs_ready abs_ready exp_ready sp_ready dts_ready
            du_ready dA_ready bparts_ready bbank_full bb_ready dbu_ready scan_done stT_ready acc_done th_ready adj_ready
            yg_ready var_ready rstd_ready rows_ready att_max att_exp att_norm nmx_ready dsc_ready ths_ready
            whl_ready init_late q_ready o_ready sq_ready dve_link gate_tanh out_done ctxT_loaded xT_loaded x_loaded wd_loaded mask_ready""".split()
        s = {n: sem(n) for n in names}

        use, root, row = {}, {}, {}
        for stage, b, k in pe_order:
            for n in BANKS.get((stage, k), []):
                use[n, b] = (len(use) % WORK, len(use) // WORK)
            if (stage, k) in ROOTS:
                root[stage, b, k] = len(root) + 1
            if (stage, k) in ROWS:
                row[ROWS.index((stage, k)) + 1, b] = len(row) + 1
        pairs = [(n, b) for n, b in use if n[0] == "u" and "_" in n]

        def whl_count(lay, b):
            return [x for x in pe_order if x[0] in ("ffn0", "ffn1") and x[2] == 2].index((f"ffn{lay}", b, 2)) + 1

        def left(lay, c):
            return min(P, (F0, F1)[lay] - c * P)

        wd_count = {}
        for b in range(B):
            wd_count[0, b] = 16 * (3 * b + 2)
            wd_count[1, b] = 16 * (3 * b + 3)

        def work_bank(n, b):
            return work[use[n, b][0]]

        def full(n, b):
            return work_full[use[n, b][0]], use[n, b][1] + 1

        def read(n, b):
            return work_read[use[n, b][0]], use[n, b][1] + 1

        def halves(t):
            return t[:, :].rearrange("p (t l) -> p t l", t=2)

        block = ctx.enter_context(nc.Block())

        @block.sync
        def _(sp):
            for dst, src, part in loads:
                sp.dma_start(dst, src).then_inc(loaded[part], 16)

            def load_wd0():
                sp.dma_start(wd[:, 0:full0, :], d["wd0"][0:full0 * P, :].rearrange("(t p) h -> p t h", p=P))\
                    .then_inc(s["wd_loaded"], 16)
                sp.dma_start(wd[0:F0 - full0 * P, full0, :], d["wd0"][full0 * P:F0, :]).then_inc(s["wd_loaded"], 16)

            load_wd0()
            for stage, b, k in pe_order:
                if (stage, k) == ("out", 0) and b + 2 < B:
                    sp.wait_ge(*full("kv", b))
                    sp.dma_start(ctxT[:, b % 2], d["ctxT"][:, (b + 2) * L:(b + 3) * L]).then_inc(s["ctxT_loaded"], 16)
                if (stage, k) == ("out", 0) and b + 2 < B:
                    sp.wait_ge(*full("gate1", b))
                    sp.dma_start(xT[:, b % 2], d["xT"][:, :, (b + 2) * L:(b + 3) * L]).then_inc(s["xT_loaded"], 16)
                if (stage, k) == ("ffn0", SUM0 + 1):
                    sp.wait_ge(*full("ffn0", b))
                    sp.dma_start(wd[:, 0:F1T, :], d["wd1"]).then_inc(s["wd_loaded"], 16)
                if (stage, k) == ("ffn1", SUM1 + 1):
                    sp.wait_ge(s["rows_ready"], row[6, b])
                    sp.dma_start(out[:, b * LT:(b + 1) * LT, :], rows[6][:, :, :]).then_inc(s["out_done"], 16)
                    if b + 1 < B:
                        load_wd0()
                        sp.wait_ge(s["out_done"], 16 * (b + 1))
                        sp.dma_start(rows[0][:, :, :], d["x"][:, (b + 1) * LT:(b + 2) * LT, :])\
                            .then_inc(s["x_loaded"], 16)
            sp.wait_ge(s["out_done"], 16 * B)

        @block.gpsimd
        def _(pool):
            gp = nc.gpsimd
            gp.memset(ones[:], 1.0)
            gp.memset(mhalf[:], -0.5)
            gp.memset(dA[:, :, :, 0:1], 0.0)
            gp.memset(wg0[:, :, F0:], 0.0)
            gp.memset(wu0[:, :, F0:], 0.0).then_inc(s["consts_ready"], 1)
            pool.wait_ge(s["consts_ready"], 1)
            var_ready = 0
            for stage, b, k in pool_order:
                if stage == "scan" and k < N:
                    i = b * N + k
                    if k == 0:
                        pool.wait_ge(s["du_ready"], b + 1)
                    if k % 2 == 0:
                        pool.wait_ge(s["bb_ready"], i // 2 + 1)
                    for q in range(EP):
                        tile = i * EP + q
                        if tile >= DBU_RING:
                            pool.wait_ge(s["scan_done"], tile - DBU_RING + 1)
                        gp.tensor_tensor(dbu[:, tile % DBU_RING], du[:, b % 2, 2 * q:2 * q + 2, :],
                                         bb[:, i // 2 % 2, k % 2:k % 2 + 1, :].to_broadcast([P, 2, L]),
                                         ALU.mult).then_inc(s["dbu_ready"], 1)
                if (stage, b, k) in root:
                    if stage == "hgrn" and k == 4:
                        pool.wait_ge(*read("ss", b))
                    else:
                        var_ready += 1
                        pool.wait_ge(s["var_ready"], var_ready)
                    gp.tensor_tensor(rstd[:, :], var[:, :], mhalf[:, :], ALU.pow).then_inc(s["rstd_ready"], 1)

        @block.tensor
        def _(pe):
            mm = nc.tensor.matmul

            def transpose(dst, src):
                return nc.tensor.transpose(dst, src, ident[:, :])

            def claim(n, b):
                i, u = use[n, b]
                if u:
                    pe.wait_ge(work_read[i], u)
                return work[i]

            def fill(last, n, b):
                last.then_inc(work_full[use[n, b][0]], 1)

            def transposes(n, b, src, rows_, cols, width=P):
                t = claim(n, b)
                for c in range(cols):
                    for r_ in range(rows_):
                        last = transpose(t[0:width, (c * rows_ + r_) * P:(c * rows_ + r_ + 1) * P], src(r_, c))
                fill(last, n, b)

            def product(t, col, lhs, rhs, depth, width):
                for c in range(depth):
                    last = mm(t[:, col:col + width], lhs(c), rhs(c), start=(c == 0), stop=(c == depth - 1))
                return last

            def in_projection(b, names, first):
                for i, n in enumerate(names):
                    t = claim(n, b)
                    for f in range(2):
                        m = first + (2 * i + f) * P
                        last = product(t, f * L, lambda c: w_in[:, c, m:m + P], lambda c: xT[:, b % 2, c, :], HT, L)
                    fill(last, n, b)

            def ffn(b, k, lay, wg, wu, sel, nexp, routed, wrt, h, tiles):
                down = 3 + 3 * (tiles // 2)
                if k == 0:
                    n = 2 if lay == 0 else 5
                    pe.wait_ge(s["rows_ready"], row[n, b])
                    transposes(f"x{n}T", b, lambda r_, c: rows[n][:, r_, c * P:(c + 1) * P], LT, HT)
                elif k == 1:
                    pe.wait_ge(*read(f"x{2 if lay == 0 else 5}T", b))
                    t = claim(f"logit{lay}", b)
                    for lt in range(LT):
                        last = product(t, lt * nexp, lambda c: xsT[:, c, lt * P:(lt + 1) * P], lambda c: wrt[:, c, :],
                                       HT, nexp)
                    fill(last, f"logit{lay}", b)
                elif k == 2:
                    pe.wait_ge(s["whl_ready"], whl_count(lay, b))
                    transposes(f"w{lay}T", b, lambda r_, c: whl[:, r_, 0:3 * nexp], LT, 1, 3 * nexp)
                elif k < down:
                    i, kind = divmod(k - 3, 3)
                    if kind < 2:
                        w = (wg, wu)[kind]
                        n = f"{'gu'[kind]}{lay}_{i}"
                        t = claim(n, b)
                        for f in range(2):
                            m = (2 * i + f) * P
                            last = product(t, f * L, lambda c: w[:, c, m:m + P], lambda c: xsT[:, c, :], HT, L)
                        fill(last, n, b)
                    elif BANKS[f"ffn{lay}", k]:
                        n = f"e{lay}_{i}"
                        t = claim(n, b)
                        if i == 0:
                            pe.wait_ge(*read(f"w{lay}T", b))
                        for f in range(2):
                            m = (2 * i + f) * P
                            if m < routed:
                                member = sel[:, m:m + P] if lay == 0 else \
                                    sel[:, m // P:m // P + 1].to_broadcast([3 * nexp, P])
                                last = mm(t[:, f * L:(f + 1) * L], member, wT[0:3 * nexp, :], start=True, stop=True)
                        fill(last, n, b)
                elif k < down + DOWN_STEPS:
                    lt, half = divmod(k - down, 2)
                    if k == down:
                        pe.wait_ge(*read(f"u{lay}_{tiles // 2 - 1}", b))
                        pe.wait_ge(*read(f"e{lay}_{(routed - 1) // (2 * P)}", b))
                        claim(f"ffn{lay}", b)
                        pe.wait_ge(s["wd_loaded"], wd_count[lay, b])
                    t = work_bank(f"ffn{lay}", b)
                    for c in range(half * tiles // 2, (half + 1) * tiles // 2):
                        last = mm(t[:, lt * H:(lt + 1) * H], h[0:left(lay, c), c, lt * P:(lt + 1) * P],
                                  wd[0:left(lay, c), c, :], start=(c == 0), stop=(c == tiles - 1))
                    if k == down + DOWN_STEPS - 1:
                        fill(last, f"ffn{lay}", b)

            def broadcast_b(b, pair):
                i = b * N // 2 + pair
                if i:
                    pe.wait_ge(s["bb_ready"], i)
                for j in range(2):
                    n = 2 * pair + j
                    last = mm(bbank[:, j * L:(j + 1) * L], sel_b[:, n:n + 1].to_broadcast([P, P]),
                              bparts[:, b % 2, :], start=True, stop=True)
                last.then_inc(s["bbank_full"], 1)

            for stage, b, k in pe_order:
                p = b % 2
                if stage == "init" and k == 0:
                    pe.wait_ge(loaded[0], part_size[0])
                if stage == "init" and k == 1:
                    for i in range(1, PARTS):
                        pe.wait_ge(loaded[i], part_size[i])
                    pe.wait_ge(s["consts_ready"], 1)
                    pe.wait_ge(s["init_late"], 1)
                if stage == "pre" and k == 0:
                    if b >= 2:
                        pe.wait_ge(s["xT_loaded"], 16 * (b - 1))
                    in_projection(b, ["hid0", "hid1"], 0)
                if stage == "pre" and k == 2:
                    if b == 0:
                        pe.wait_ge(loaded[1], part_size[1])
                    t = claim("dtbc", b)
                    pe.wait_ge(s["hs_ready"], b + 1)
                    product(t, 0, lambda c: w_x[:, c, 0:TR], lambda c: hs[:, p, c, :], ET, L)
                    for lt in range(LT):
                        last = product(t, L + lt * 2 * N, lambda c: hs[:, p, c, lt * P:(lt + 1) * P],
                                       lambda c: w_x[:, c, TR:TR + 2 * N], ET, 2 * N)
                    fill(last, "dtbc", b)
                    t = claim("bT", b)
                    fill(product(t, 0, lambda c: w_x[:, c, TR:TR + P],
                                 lambda c: hs[:, p, c, :], ET, L), "bT", b)
                if stage == "pre" and k == 3:
                    pe.wait_ge(*read("dtbc", b))
                    for i in range(2):
                        t = claim(f"z{i}", b)
                        for f in range(2):
                            m = (2 * i + f) * P
                            last = product(t, f * L, lambda c: w_dt[:, m:m + P], lambda c: dtbc[:, p, 0:L], 1, L)
                        fill(last, f"z{i}", b)
                if stage == "pre" and k == 5:
                    pe.wait_ge(s["bparts_ready"], b + 1)
                    broadcast_b(b, 0)
                if stage == "adj" and k == 0:
                    if b == 0:
                        pe.wait_ge(loaded[2], part_size[2])
                    if b >= 2:
                        pe.wait_ge(s["ctxT_loaded"], 16 * (b - 1))
                    t = claim("qk", b)
                    mm(t[0:C, 0:L], wqT[:, :], ctxT[:, p], start=True, stop=True)
                    fill(mm(t[0:C, L:2 * L], wkT[:, :], ctxT[:, p], start=True, stop=True), "qk", b)
                if stage == "adj" and k == 1:
                    pe.wait_ge(*read("qk", b))
                    t = claim("sim", b)
                    for lt in range(LT):
                        last = mm(t[:, lt * L:(lt + 1) * L], qk[:, lt * P:(lt + 1) * P], qk[:, L:2 * L],
                                  start=True, stop=True)
                    fill(last, "sim", b)
                if stage == "adj" and k == ROUNDS + 4:
                    pe.wait_ge(s["adj_ready"], b + 1)
                    transposes("adjT", b, lambda r_, c: wk[:, r_, c * P:(c + 1) * P], LT, LT)
                if stage == "scan":
                    if k % 2 and k + 1 < N:
                        broadcast_b(b, (k + 1) // 2)
                    for q in range(2):
                        if k > 0:
                            done = (b * N + k - 1) * LT + q
                            if q == 0:
                                pe.wait_ge(s["scan_done"], (b * N + k) * EP)
                            if done >= 2:
                                pe.wait_ge(s["acc_done"], done - 1)
                            for t in range(ET):
                                slot = ((b * N + k - 1) * EP + t // 2) % ST_RING
                                at = t % 2 * L + q * P
                                last = transpose(stT[done % 2][:, t * P:(t + 1) * P], st[:, slot, at:at + P])
                            last.then_inc(s["stT_ready"], 1)
                if stage == "out" and k == 0:
                    t = claim("kv", b)
                    fill(mm(t[0:C, 0:L], wkvT[:, :], ctxT[:, p], start=True, stop=True), "kv", b)
                    in_projection(b, ["gate0", "gate1"], E)
                if stage == "out" and k == 1:
                    pe.wait_ge(*read("kv", b))
                    t = claim("gram", b)
                    for lt in range(LT):
                        last = mm(t[:, lt * L:(lt + 1) * L], kv[:, lt * P:(lt + 1) * P], kv[:, :],
                                  start=True, stop=True)
                    fill(last, "gram", b)
                    pe.wait_ge(s["acc_done"], (b + 1) * N * LT)
                    for i in range(2):
                        transposes(f"yT{i}", b, lambda r_, c: acc[:, r_, (2 * i + c) * P:(2 * i + c + 1) * P],
                                   LT, 2)
                if stage == "out" and k == 2:
                    pe.wait_ge(s["yg_ready"], b + 1)
                    t = claim("mamba", b)
                    for lt in range(LT):
                        last = product(t, lt * H, lambda c: yg[:, c, lt * P:(lt + 1) * P], lambda c: w_out[:, c, :],
                                       ET, H)
                    fill(last, "mamba", b)
                if stage == "xat0" and k == 0:
                    pe.wait_ge(s["rows_ready"], row[1, b])
                    transposes("x1T", b, lambda r_, c: rows[1][:, r_, c * P:(c + 1) * P], LT, HT)
                if stage == "xat0" and k == 1:
                    pe.wait_ge(*read("x1T", b))
                    pe.wait_ge(*read("gram", b))
                    t = claim("att", b)
                    for lt in range(LT):
                        last = product(t, lt * L, lambda c: xsT[:, c, lt * P:(lt + 1) * P],
                                       lambda c: gram[:, c, :], LT, L)
                    fill(last, "att", b)
                if stage == "ffn0":
                    ffn(b, k, 0, wg0, wu0, sel0, F0E, F0E * F0F, wr, big, F0T)
                if stage == "ffn1":
                    ffn(b, k, 1, wg1, wu1, sel1, F1E + 1, F1, wr1, big, F1T)
                if stage == "hgrn" and k == 0:
                    pe.wait_ge(s["rows_ready"], row[3, b])
                    transposes("x3T", b, lambda r_, c: rows[3][:, r_, c * P:(c + 1) * P], LT, HT)
                if stage == "hgrn" and 1 <= k < 4:
                    n, w = (("hi", whi), ("hf", whf), ("hg", whg))[k - 1]
                    pe.wait_ge(*read("x3T", b))
                    t = claim(n, b)
                    for f in range(HT):
                        last = product(t, f * L, lambda c: w[:, c, f * P:(f + 1) * P], lambda c: xsT[:, c, :], HT, L)
                    fill(last, n, b)
                if stage == "hgrn" and k == 4:
                    t = claim("ss", b)
                    pe.wait_ge(s["sq_ready"], b + 1)
                    for lt in range(LT):
                        last = product(t, lt, lambda c: sq[:, c, lt * P:(lt + 1) * P], lambda c: ones[:, :], HT, 1)
                    fill(last, "ss", b)
                    t = claim("hgrn", b)
                    pe.wait_ge(s["q_ready"], b + 1)
                    for lt in range(LT):
                        last = product(t, lt * H, lambda c: sgg[:, c, lt * P:(lt + 1) * P], lambda c: who[:, c, :],
                                       HT, H)
                    fill(last, "hgrn", b)

        @block.scalar
        def _(act):
            A = nc.scalar.activation

            def evacuate(n, b, dst, src=None, func=ACT.Copy, **kw):
                act.wait_ge(*full(n, b))
                A(dst, work_bank(n, b)[:, :] if src is None else src, func, **kw).then_inc(work_read[use[n, b][0]], 1)

            def gate_tanh(n, b, dst):
                act.wait_ge(*full(n, b))
                A(dst.rearrange("p t l -> p (t l)"), work_bank(n, b)[:, :], ACT.Tanh, scale=0.5)\
                    .then_inc(s["gate_tanh"], 1)

            def ffn(b, k, lay, nexp, down):
                if k == 0:
                    n = f"x{2 if lay == 0 else 5}T"
                    evacuate(n, b, xsT[:, :, :].rearrange("p t l -> p (t l)"))
                elif k == 1 and lay == 0:
                    act.wait_ge(s["nmx_ready"], b + 1)
                    t = work_bank("logit0", b)
                    for lt in range(LT):
                        last = A(exr[:, lt, :], t[:, lt * nexp:(lt + 1) * nexp], ACT.Exp, bias=nmx[:, lt:lt + 1],
                                 accum_out=es[:, lt:lt + 1])
                    last.then_inc(work_read[use["logit0", b][0]], 1)
                elif k == 1:
                    act.wait_ge(s["dsc_ready"], b + 1)
                    A(ths[:, :, :], dsc[:, :, :], ACT.Tanh, scale=0.5).then_inc(s["ths_ready"], 1)
                elif k == 2:
                    evacuate(f"w{lay}T", b, wT[0:3 * nexp, :], work_bank(f"w{lay}T", b)[0:3 * nexp, 0:L])
                elif k < down and (k - 3) % 3 == 0:
                    n = f"g{lay}_{(k - 3) // 3}"
                    i = pairs.index((f"u{lay}_{(k - 3) // 3}", b))
                    if i >= 2:
                        act.wait_ge(*read(*pairs[i - 2]))
                    gate_tanh(n, b, gs[:, i % 2, :, :])

            def spread_b(b, pair):
                i = b * N // 2 + pair
                act.wait_ge(s["bbank_full"], i + 1)
                if i >= 2:
                    act.wait_ge(s["dbu_ready"], (i - 1) * 2 * EP)
                A(bb[:, i % 2].rearrange("p j l -> p (j l)"), bbank[:, :], ACT.Copy).then_inc(s["bb_ready"], 1)

            for stage, b, k in act_order:
                p = b % 2
                if stage == "init" and k == 0:
                    act.wait_ge(loaded[0], part_size[0])
                if stage == "pre" and k == 0:
                    if b >= 2:
                        act.wait_ge(s["dbu_ready"], (b - 1) * N * EP)
                    for i in range(2):
                        act.wait_ge(*full(f"hid{i}", b))
                        for f in range(2):
                            t = 2 * i + f
                            last = A(du[:, p, t, :], work_bank(f"hid{i}", b)[:, f * L:(f + 1) * L], ACT.Identity,
                                     scale=cw[:, t, KC - 1:KC], bias=cb[:, t:t + 1])
                        last.then_inc(s["conv0"], 1)
                if stage == "pre" and k == 1:
                    if b >= 2:
                        act.wait_ge(s["yg_ready"], b - 1)
                    act.wait_ge(*read("hid0", b))
                    act.wait_ge(*read("hid1", b))
                    A(hs[:, p], du[:, p], ACT.Silu).then_inc(s["hs_ready"], 1)
                if stage == "pre" and k == 2:
                    if b >= 2:
                        act.wait_ge(s["acc_done"], (b - 1) * N * LT)
                    evacuate("dtbc", b, dtbc[:, p, :], work_bank("dtbc", b)[:, 0:L + LT * 2 * N])
                if stage == "pre" and k == 3:
                    if b == 0:
                        act.wait_ge(loaded[1], part_size[1])
                        A(a_neg[:, :, :], a_log[:, :, :], ACT.Exp).then_inc(s["a_exp"], 1)
                    if b >= 2:
                        act.wait_ge(s["dA_ready"], (b - 1) * N * EP)
                    act.wait_ge(s["bparts_ready"], b + 1)
                    for i in range(2):
                        act.wait_ge(*full(f"z{i}", b))
                        for f in range(2):
                            t = 2 * i + f
                            src = work_bank(f"z{i}", b)[:, f * L:(f + 1) * L]
                            A(za[:, t, :], src, ACT.Abs, bias=b_dt[:, t:t + 1])
                            last = A(dts[:, p, t, :], src, ACT.Relu, bias=b_dt[:, t:t + 1])
                        last.then_inc(work_read[use[f"z{i}", b][0]], 1)
                    act.wait_ge(*read("z1", b))
                    A(za[:, :, :], za[:, :, :], ACT.Exp, scale=-1.0).then_inc(s["exp_ready"], 1)
                if stage == "pre" and k == 4:
                    act.wait_ge(s["exp_ready"], b + 1)
                    A(za[:, :, :], za[:, :, :], ACT.Ln, bias=1.0).then_inc(s["sp_ready"], 1)
                if stage == "pre" and k == 5:
                    spread_b(b, 0)
                if stage == "adj" and k == 0:
                    if b == 0:
                        act.wait_ge(loaded[2], part_size[2])
                        A(gth[:, :], gam[:, :], ACT.Tanh, scale=0.5).then_inc(s["gam_tanh"], 1)
                    evacuate("qk", b, qk[:, :], work_bank("qk", b)[0:C, :])
                if stage == "adj" and k == 1:
                    if b:
                        act.wait_ge(s["adj_ready"], b)
                    evacuate("sim", b, sim[:, :, :].rearrange("p t l -> p (t l)"), scale=1.0 / 16)
                if stage == "adj" and k == ROUNDS + 2:
                    act.wait_ge(s["mask_ready"], b + 1)
                    A(sim[:, :, :], sim[:, :, :], ACT.Tanh, scale=0.5).then_inc(s["th_ready"], 1)
                if stage == "scan" and k < N:
                    if k % 2 and k + 1 < N:
                        spread_b(b, (k + 1) // 2)
                    if k == 0:
                        act.wait_ge(s["dts_ready"], b + 1)
                    if b == 0 and k == 0:
                        act.wait_ge(s["a_ready"], 1)
                        act.wait_ge(s["consts_ready"], 1)
                    for q in range(EP):
                        i = (b * N + k) * EP + q
                        if i >= DA_RING:
                            act.wait_ge(s["scan_done"], i - DA_RING + 1)
                        for f in range(2):
                            t = 2 * q + f
                            last = A(dA[:, i % DA_RING, f, 1:L], dts[:, p, t, 1:L], ACT.Exp,
                                     scale=a_neg[:, t, k:k + 1])
                        last.then_inc(s["dA_ready"], 1)
                if stage == "out" and k == 1:
                    evacuate("gram", b, gram[:, :, :].rearrange("p t l -> p (t l)"), scale=1.0 / 16)
                if stage == "out" and k == 0:
                    evacuate("kv", b, kv[:, :], work_bank("kv", b)[0:C, 0:L], func=ACT.Identity, bias=b_k[:, :])
                    if b:
                        act.wait_ge(*full("ffn1", b - 1))
                    for i in range(2):
                        gate_tanh(f"gate{i}", b, sg[:, 2 * i:2 * i + 2, :])
                if stage == "xat0" and k == 0:
                    evacuate("x1T", b, xsT[:, :, :].rearrange("p t l -> p (t l)"))
                if stage == "xat0" and k == 2:
                    act.wait_ge(s["att_max"], b + 1)
                    for lt in range(LT):
                        last = A(ex[:, lt, :], ex[:, lt, :], ACT.Exp, bias=nmx[:, lt:lt + 1],
                                 accum_out=es[:, lt:lt + 1])
                    last.then_inc(s["att_exp"], 1)
                if stage == "ffn0":
                    ffn(b, k, 0, F0E, DOWN0)
                if stage == "ffn1":
                    ffn(b, k, 1, F1E + 1, DOWN1)
                if stage == "hgrn" and k == 0:
                    evacuate("x3T", b, xsT[:, :, :].rearrange("p t l -> p (t l)"))
                if stage == "hgrn" and 1 <= k < 4:
                    n, dst = (("hi", si), ("hf", tf), ("hg", sgg))[k - 1]
                    if n == "hf":
                        evacuate(n, b, dst[:, :, :].rearrange("p t l -> p (t l)"), func=ACT.Tanh, scale=0.5)
                    else:
                        gate_tanh(n, b, dst[:, :, :])
                if stage == "hgrn" and k == 4:
                    act.wait_ge(s["o_ready"], b + 1)
                    A(sq[:, :, :], o[:, :, :], ACT.Square).then_inc(s["sq_ready"], 1)

        @block.vector
        def _(dve):
            V = nc.vector
            links = [0]

            def link(ins):
                links[0] += 1
                ins.then_inc(s["dve_link"], 1)
                dve.wait_ge(s["dve_link"], links[0])

            def release(ins, n, b):
                ins.then_inc(work_read[use[n, b][0]], 1)

            def stats(src, eps):
                for lt in range(LT):
                    last = V.bn_stats(bst[:, lt, :], src(lt))
                link(last)
                for lt in range(LT):
                    last = V.bn_aggr(mv[:, lt, :], bst[:, lt, :])
                link(last)
                V.tensor_scalar(var[:, :], mv[:, :, 1], eps, None, ALU.add).then_inc(s["var_ready"], 1)

            def normalize(key, i, b):
                dve.wait_ge(s["rstd_ready"], root[key])
                for lt in range(LT):
                    last = V.tensor_scalar(rows[i][:, lt, :], r[:, lt, :], mv[:, lt, 0:1], rstd[:, lt:lt + 1],
                                           ALU.subtract, ALU.mult)
                last.then_inc(s["rows_ready"], 1)

            def add_bank(n, b, rows_):
                dve.wait_ge(*full(n, b))
                release(V.tensor_tensor(r[:, :, :], halves(work_bank(n, b)), rows_, ALU.add), n, b)
                dve.wait_ge(*read(n, b))
                stats(lambda lt: r[:, lt, :], 1e-5)

            tanhs = [0]

            def twice_silu(n, b, th):
                tanhs[0] += 1
                dve.wait_ge(s["gate_tanh"], tanhs[0])
                release(V.scalar_tensor_tensor(out=th, in0=th, scalar=1.0, in1=halves(work_bank(n, b)),
                                               op0=ALU.add, op1=ALU.mult), n, b)

            def route(lay, b, prob, nexp):
                link(V.tensor_copy(if8[:, :, :], i8[:, :, 0:2]))
                for i, dst in ((0, wa), (1, wb)):
                    for lt in range(LT):
                        last = V.tensor_scalar(dst[:, lt, :], iota[:, :], if8[:, lt, i:i + 1], prob[:, lt, i:i + 1],
                                               ALU.is_equal, ALU.mult)
                link(last)
                link(V.tensor_tensor(wf[:, :, 0, 0:F0E], wa[:, :, :], wb[:, :, :], ALU.add))
                for part in range(3):
                    now, left = wf[:, :, part % 2, 0:nexp], wf[:, :, (part + 1) % 2, 0:nexp]
                    link(V.tensor_copy(wpart[:, :, 0:nexp], now))
                    last = V.tensor_copy(whl[:, :, part * nexp:(part + 1) * nexp], wpart[:, :, 0:nexp])
                    if part < 2:
                        link(V.tensor_tensor(left, now, wpart[:, :, 0:nexp], ALU.subtract))
                last.then_inc(s["whl_ready"], 1)

            def ffn(b, k, lay, nexp, routed, h, tiles, rows_in):
                down = 3 + 3 * (tiles // 2)
                if k == 1 and lay == 0:
                    dve.wait_ge(*full("logit0", b))
                    t = work_bank("logit0", b)[:, 0:LT * nexp].rearrange("p (t e) -> p t e", t=LT)
                    V.tensor_reduce(nmx[:, :], t, AX.X, ALU.max, negate=True).then_inc(s["nmx_ready"], 1)
                elif k == 2 and lay == 0:
                    dve.wait_ge(*read("logit0", b))
                    link(V.reciprocal(ri[:, :], es[:, :]))
                    for lt in range(LT):
                        last = V.tensor_scalar(sc[:, lt, :], exr[:, lt, :], ri[:, lt:lt + 1], 0.5, ALU.mult,
                                               ALU.mult)
                    link(last)
                    for lt in range(LT):
                        last = V.max(out=t8[:, lt, :], in_=sc[:, lt, :])
                    link(last)
                    for lt in range(LT):
                        last = V.max_index(out=i8[:, lt, :], in_max=t8[:, lt, :], in_values=sc[:, lt, :])
                    link(last)
                    route(0, b, t8, nexp)
                elif k == 1:
                    dve.wait_ge(*full("logit1", b))
                    t = work_bank("logit1", b)[:, 0:LT * nexp].rearrange("p (t e) -> p t e", t=LT)
                    release(V.tensor_copy(lgs[:, :, :], t), "logit1", b)
                    dve.wait_ge(*read("logit1", b))
                    for lt in range(LT):
                        last = V.max(out=t8[:, lt, :], in_=lgs[:, lt, 0:F1E])
                    link(last)
                    V.tensor_copy(dsc[:, :, 1], lgs[:, :, F1E])
                    V.tensor_tensor(dsc[:, :, 0], t8[:, :, 0], t8[:, :, 1], ALU.subtract)\
                        .then_inc(s["dsc_ready"], 1)
                    for lt in range(LT):
                        last = V.max_index(out=i8[:, lt, :], in_max=t8[:, lt, :], in_values=lgs[:, lt, 0:F1E])
                    link(last)
                elif k == 2:
                    dve.wait_ge(s["ths_ready"], b + 1)
                    V.tensor_scalar(pr[:, :, 0], ths[:, :, 0], 0.25, 0.25, ALU.mult, ALU.add)
                    V.tensor_scalar(wf[:, :, 0, F1E], ths[:, :, 1], 0.25, 0.25, ALU.mult, ALU.add)
                    link(V.tensor_scalar(pr[:, :, 1], ths[:, :, 0], -0.25, 0.25, ALU.mult, ALU.add))
                    route(1, b, pr, nexp)
                elif 3 <= k < down:
                    i, kind = divmod(k - 3, 3)
                    m = pairs.index((f"u{lay}_{i}", b)) % 2
                    gn_, un, en = f"g{lay}_{i}", f"u{lay}_{i}", f"e{lay}_{i}"
                    weighted = max(0, min(2, routed // P - 2 * i))
                    if kind == 0:
                        twice_silu(gn_, b, gs[:, m, :, :])
                    elif kind == 1:
                        dve.wait_ge(*read(gn_, b))
                        dve.wait_ge(*full(un, b))
                        u = halves(work_bank(un, b))
                        if weighted:
                            last = V.tensor_tensor(h[:, 2 * i:2 * i + weighted, :], gs[:, m, 0:weighted, :],
                                                   u[:, 0:weighted, :], ALU.mult)
                        if weighted < 2:
                            last = V.scalar_tensor_tensor(out=h[:, 2 * i + weighted:2 * i + 2, :],
                                                          in0=gs[:, m, weighted:2, :], scalar=0.5,
                                                          in1=u[:, weighted:2, :], op0=ALU.mult, op1=ALU.mult)
                        release(last, un, b)
                    elif weighted:
                        dve.wait_ge(*read(un, b))
                        dve.wait_ge(*full(en, b))
                        tile = h[:, 2 * i:2 * i + weighted, :]
                        release(V.tensor_tensor(tile, tile, halves(work_bank(en, b))[:, 0:weighted, :], ALU.mult),
                                en, b)
                elif k == down + DOWN_STEPS - 1:
                    add_bank(f"ffn{lay}", b, rows[rows_in][:, :, :])
                elif k == down + DOWN_STEPS:
                    normalize((f"ffn{lay}", b, k - 1), rows_in + 1, b)

            for stage, b, k in dve_order:
                p = b % 2
                if stage == "init" and k == 0:
                    dve.wait_ge(loaded[0], part_size[0])
                if stage == "init" and k == 1:
                    dve.wait_ge(loaded[3], part_size[3])
                    dve.wait_ge(loaded[4], part_size[4])
                    for t in range(HT):
                        last = V.tensor_scalar(who[:, t, :], who[:, t, :], gn[:, t:t + 1], -0.125,
                                               ALU.mult, ALU.mult)
                    last.then_inc(s["init_late"], 1)
                if stage == "pre" and k == 0:
                    for i in range(2):
                        dve.wait_ge(s["conv0"], 2 * b + i + 1)
                        for tap in range(KC - 2, -1, -1):
                            off = KC - 1 - tap
                            for f in range(2):
                                t = 2 * i + f
                                last = V.scalar_tensor_tensor(
                                    out=du[:, p, t, off:L], in0=work_bank(f"hid{i}", b)[:, f * L:(f + 1) * L - off],
                                    scalar=cw[:, t, tap:tap + 1], in1=du[:, p, t, off:L], op0=ALU.mult, op1=ALU.add)
                            if tap:
                                link(last)
                        release(last, f"hid{i}", b)
                if stage == "pre" and k == 2:
                    dve.wait_ge(*full("bT", b))
                    if b:
                        dve.wait_ge(s["sp_ready"], b)
                    t = work_bank("bT", b)
                    link(V.tensor_copy(bparts[:, p, :], t[:, 0:L]))
                    h_, q_ = P // 2, 3 * P // 4
                    last = V.tensor_tensor(za[h_:P, 0, :], t[h_:P, 0:L], bparts[h_:P, p, :], ALU.subtract)
                    release(last, "bT", b)
                    dve.wait_ge(*read("bT", b))
                    link(V.tensor_copy(bparts[h_:P, p, :], za[h_:P, 0, :]))
                    link(V.tensor_tensor(za[q_:P, 1, :], za[q_:P, 0, :], bparts[q_:P, p, :], ALU.subtract))
                    V.tensor_copy(bparts[q_:P, p, :], za[q_:P, 1, :]).then_inc(s["bparts_ready"], 1)
                if stage == "pre" and k == 4:
                    if b == 0:
                        dve.wait_ge(s["a_exp"], 1)
                        V.tensor_scalar(a_neg[:, :, :], a_neg[:, :, :], -1.0, None, ALU.mult)\
                            .then_inc(s["a_ready"], 1)
                    dve.wait_ge(s["sp_ready"], b + 1)
                    V.tensor_tensor(dts[:, p], dts[:, p], za[:, :, :], ALU.add).then_inc(s["dts_ready"], 1)
                    dve.wait_ge(s["dts_ready"], b + 1)
                    V.tensor_tensor(du[:, p], dts[:, p], hs[:, p], ALU.mult).then_inc(s["du_ready"], 1)
                if stage == "adj" and 2 <= k < ROUNDS + 2:
                    i = k - 2
                    if i == 0:
                        dve.wait_ge(*read("sim", b))
                    src = sim if i == 0 else wk
                    for lt in range(LT):
                        last = V.max(out=m8[:, lt, :], in_=src[:, lt, :])
                    link(last)
                    if i < ROUNDS - 1:
                        for lt in range(LT):
                            last = V.match_replace(out=wk[:, lt, :], in_to_replace=m8[:, lt, :],
                                                   in_values=src[:, lt, :], imm_value=-3.0e38)
                        link(last)
                if stage == "adj" and k == ROUNDS + 2:
                    if b == 0:
                        dve.wait_ge(s["gam_tanh"], 1)
                        V.tensor_scalar(gq[:, :], gth[:, :], 0.125, 0.125, ALU.mult, ALU.add)
                        link(V.tensor_scalar(g2[:, :], gth[:, :], -0.5, 1.5, ALU.mult, ALU.add))
                    at = (TOPK - 1) % 8
                    for lt in range(LT):
                        last = V.tensor_scalar(wk[:, lt, :], sim[:, lt, :], m8[:, lt, at:at + 1], gq[:, 0:1],
                                               ALU.is_ge, ALU.mult)
                    last.then_inc(s["mask_ready"], 1)
                if stage == "adj" and k == ROUNDS + 3:
                    dve.wait_ge(s["th_ready"], b + 1)
                    V.scalar_tensor_tensor(out=wk[:, :, :], in0=sim[:, :, :], scalar=1.0, in1=wk[:, :, :],
                                           op0=ALU.add, op1=ALU.mult).then_inc(s["adj_ready"], 1)
                if stage == "adj" and k == ROUNDS + 4:
                    dve.wait_ge(*full("adjT", b))
                    release(V.tensor_tensor(S[:, :, :], wk[:, :, :], halves(work_bank("adjT", b)), ALU.add), "adjT", b)
                if stage == "scan":
                    for q in range(2):
                        if k < N:
                            i = (b * N + k) * EP + q
                            dve.wait_ge(s["dA_ready"], i + 1)
                            dve.wait_ge(s["dbu_ready"], i + 1)
                            if i >= ST_RING:
                                dve.wait_ge(s["stT_ready"], (b * N + k - 1) * LT)
                            V.tensor_tensor_scan(st[:, i % ST_RING, :],
                                                 dA[:, i % DA_RING].rearrange("p f l -> p (f l)"), 
                                                 dbu[:, i % DBU_RING].rearrange("p f l -> p (f l)"),
                                                 0.0, ALU.mult, ALU.add).then_inc(s["scan_done"], 1)
                        if k > 0:
                            n = k - 1
                            done = (b * N + n) * LT + q
                            dve.wait_ge(s["stT_ready"], done + 1)
                            if done >= 2:
                                dve.wait_ge(s["acc_done"], done - 1)
                            if n == 0 and b:
                                dve.wait_ge(*full("yT1", b - 1))
                            col = L + q * 2 * N + N + n
                            cs = dtbc[:, p, col:col + 1]
                            if n == 0:
                                ins = V.tensor_scalar(acc[:, q, :], stT[done % 2][:, :], cs, None, ALU.mult)
                            else:
                                ins = V.scalar_tensor_tensor(out=acc[:, q, :], in0=stT[done % 2][:, :], scalar=cs,
                                                             in1=acc[:, q, :], op0=ALU.mult, op1=ALU.add)
                            ins.then_inc(s["acc_done"], 1)
                if stage == "out" and k == 0:
                    for i in range(2):
                        twice_silu(f"gate{i}", b, sg[:, 2 * i:2 * i + 2, :])
                if stage == "out" and k == 1:
                    for i in range(2):
                        dve.wait_ge(*full(f"yT{i}", b))
                        for f in range(2):
                            t = 2 * i + f
                            last = V.scalar_tensor_tensor(out=yg[:, t, :], in0=hs[:, p, t, :], scalar=skip[:, t:t + 1],
                                                          in1=work_bank(f"yT{i}", b)[:, f * L:(f + 1) * L],
                                                          op0=ALU.mult, op1=ALU.add)
                        release(last, f"yT{i}", b)
                    dve.wait_ge(*read("yT1", b))
                    dve.wait_ge(*read("gate1", b))
                    V.scalar_tensor_tensor(out=yg[:, :, :], in0=yg[:, :, :], scalar=0.5, in1=sg[:, :, :],
                                           op0=ALU.mult, op1=ALU.mult).then_inc(s["yg_ready"], 1)
                if stage == "out" and k == 2:
                    if b:
                        dve.wait_ge(s["x_loaded"], 16 * b)
                    else:
                        dve.wait_ge(loaded[3], part_size[3])
                    add_bank("mamba", b, rows[0][:, :, :])
                if stage == "out" and k == 3:
                    normalize(("out", b, 2), 1, b)
                if stage == "xat0" and k == 1:
                    dve.wait_ge(*full("att", b))
                    stats(lambda lt: work_bank("att", b)[:, lt * L:(lt + 1) * L], 1e-6)
                if stage == "xat0" and k == 2:
                    dve.wait_ge(s["rstd_ready"], root["xat0", b, 1])
                    for lt in range(LT):
                        last = V.tensor_scalar(ex[:, lt, :], work_bank("att", b)[:, lt * L:(lt + 1) * L],
                                               mv[:, lt, 0:1], rstd[:, lt:lt + 1], ALU.subtract, ALU.mult)
                    release(last, "att", b)
                    dve.wait_ge(*read("att", b))
                    for lt in range(LT):
                        last = V.tensor_tensor(ex[:, lt, :], ex[:, lt, :], lng[:, :], ALU.mult)
                    link(last)
                    for lt in range(LT):
                        last = V.tensor_tensor(ex[:, lt, :], ex[:, lt, :], lnb[:, :], ALU.add)
                    link(last)
                    V.tensor_reduce(nmx[:, :], ex[:, :, :], AX.X, ALU.max, negate=True).then_inc(s["att_max"], 1)
                if stage == "xat0" and k == 3:
                    dve.wait_ge(s["att_exp"], b + 1)
                    link(V.reciprocal(ri[:, :], es[:, :]))
                    for lt in range(LT):
                        last = V.scalar_tensor_tensor(out=r[:, lt, :], in0=ex[:, lt, :], scalar=ri[:, lt:lt + 1],
                                                      in1=rows[1][:, lt, :], op0=ALU.mult, op1=ALU.add)
                    link(last)
                    stats(lambda lt: r[:, lt, :], 1e-5)
                if stage == "xat0" and k == 4:
                    normalize(("xat0", b, 3), 2, b)
                if stage == "ffn0":
                    ffn(b, k, 0, F0E, F0E * F0F, big, F0T, 2)
                if stage == "ffn1":
                    ffn(b, k, 1, F1E + 1, F1, big, F1T, 5)
                if stage == "hgrn" and k == 1:
                    twice_silu("hi", b, si[:, :, :])
                if stage == "hgrn" and k == 3:
                    twice_silu("hg", b, sgg[:, :, :])
                    dve.wait_ge(*read("hi", b))
                    dve.wait_ge(*read("hf", b))
                    link(V.scalar_tensor_tensor(out=si[:, :, :], in0=tf[:, :, :], scalar=1.0, in1=si[:, :, :],
                                                op0=ALU.subtract, op1=ALU.mult))
                    link(V.tensor_scalar(tf[:, :, :], tf[:, :, :], 0.5, 0.5, ALU.mult, ALU.add))
                    for t in range(HT):
                        last = V.tensor_tensor_scan(o[:, t, :], tf[:, t, :], si[:, t, :], 0.0, ALU.mult, ALU.add)
                    last.then_inc(s["o_ready"], 1)
                    dve.wait_ge(s["o_ready"], b + 1)
                    dve.wait_ge(*read("hg", b))
                    V.tensor_tensor(sgg[:, :, :], o[:, :, :], sgg[:, :, :], ALU.mult).then_inc(s["q_ready"], 1)
                if stage == "hgrn" and k == 4:
                    dve.wait_ge(*full("ss", b))
                    release(V.tensor_scalar(var[:, :], work_bank("ss", b)[:, 0:LT], 1.0 / (16 * H), 1e-5, ALU.mult, ALU.add),
                            "ss", b)
                if stage == "hgrn" and k == 5:
                    dve.wait_ge(*full("hgrn", b))
                    dve.wait_ge(s["rstd_ready"], root["hgrn", b, 4])
                    for lt in range(LT):
                        last = V.scalar_tensor_tensor(out=r[:, lt, :], in0=work_bank("hgrn", b)[:, lt * H:(lt + 1) * H],
                                                      scalar=rstd[:, lt:lt + 1], in1=rows[3][:, lt, :],
                                                      op0=ALU.mult, op1=ALU.add)
                    release(last, "hgrn", b)
                    dve.wait_ge(*read("hgrn", b))
                    stats(lambda lt: r[:, lt, :], 1e-5)
                if stage == "hgrn" and k == 6:
                    normalize(("hgrn", b, 5), 4, b)
                    dve.wait_ge(s["rows_ready"], row[4, b])
                    link(V.scalar_tensor_tensor(out=r[:, :, :], in0=rows[4][:, :, :], scalar=g2[:, 0:1], in1=S[:, :, :],
                                                op0=ALU.mult, op1=ALU.add))
                    stats(lambda lt: r[:, lt, :], 1e-5)
                if stage == "hgrn" and k == 7:
                    normalize(("hgrn", b, 6), 5, b)


def kernel(**inputs):
    import ml_dtypes
    import numpy as np
    import concourse.bacc as bacc
    from concourse.bass_utils import run_bass_kernel_spmd

    v = {k: np.asarray(a) for k, a in inputs.items()}

    def tiles(a):
        return a.reshape(-1, P, a.shape[-1]).transpose(1, 0, 2)

    def up(routed, shared):
        return tiles(np.concatenate([routed.reshape(-1, H), shared], 0).T)

    def down(routed, shared):
        return np.concatenate([routed.transpose(0, 2, 1).reshape(-1, H), shared.T], 0)

    def members(width, n, rows):
        expert = np.minimum(np.arange(n) // width, rows - 1)
        return np.tile(expert[None, :] == np.arange(rows)[:, None], (3, 1)).astype(ml_dtypes.bfloat16)

    picks = np.zeros((4, 2 * N, N), ml_dtypes.bfloat16)
    for quarter in (0, 2, 3):
        picks[quarter, np.arange(N), np.arange(N)] = 1
    picks = picks.reshape(P, N)
    xf = v["x"].reshape(B * L, H)
    a = {
        "x": tiles(xf), "xT": tiles(xf.T), "ctxT": v["ctx_512"].reshape(B * L, C).T,
        "w_in": tiles(v["L0_attn_W_in"]), "cw": tiles(v["L0_attn_conv_kernel"].reshape(E, KC)),
        "cb": v["L0_attn_conv_bias"].reshape(ET, P).T, "w_x": tiles(np.concatenate([v["L0_attn_W_x"]] + 3 * [v["L0_attn_W_x"][:, TR:]], 1)), "w_dt": v["L0_attn_W_dt"],
        "b_dt": v["L0_attn_b_dt"].reshape(ET, P).T, "a_log": tiles(v["L0_attn_A_log"]),
        "skip": v["L0_attn_D"].reshape(ET, P).T, "w_out": tiles(v["L0_attn_W_out"]),
        "wkvT": v["L0_xattn_W_k"].T, "b_k": v["L0_xattn_b_k"].reshape(C, 1),
        "lng": v["L0_xattn_ln_gamma"].reshape(L), "lnb": v["L0_xattn_ln_beta"].reshape(L),
        "wr": tiles(v["L0_ffn_Wr"].T), "wg0": up(v["L0_ffn_Wg"], v["L0_ffn_Wsg"]),
        "wu0": up(v["L0_ffn_Wu"], v["L0_ffn_Wsu"]), "wd0": down(v["L0_ffn_Wd"], v["L0_ffn_Wsd"]),
        "whi": tiles(v["L1_attn_Wi"]), "whf": tiles(v["L1_attn_Wf"]), "whg": tiles(v["L1_attn_Wg"]),
        "who": tiles(v["L1_attn_Wo"]), "gn": v["L1_attn_g_norm_weight"].reshape(HT, P).T,
        "wqT": v["L1_xattn_Wq"].T, "wkT": v["L1_xattn_Wk"].T, "gam": v["L1_xattn_gamma_raw"].reshape(1),
        "wr1": tiles(np.concatenate([v["L1_ffn_gate_w"], v["L1_ffn_se_gate_w"]], 0).T),
        "wg1": up(v["L1_ffn_w_gate"], v["L1_ffn_sh_gate"]), "wu1": up(v["L1_ffn_w_up"], v["L1_ffn_sh_up"]),
        "wd1": tiles(down(v["L1_ffn_w_down"], v["L1_ffn_sh_down"])),
        "ident": np.eye(P, dtype=np.float32), "iota": np.arange(F0E, dtype=np.float32),
        "sel0": members(F0F, F0E * F0F, F0E), "sel1": members(F1F, F1, F1E + 1)[:, ::P], "sel_b": picks,
    }
    arrays = {f"in_{k}": np.ascontiguousarray(t) for k, t in a.items()}
    nc = bacc.Bacc("TRN2", target_bir_lowering=False, num_devices=1)
    d = {k: nc.dram_tensor(f"in_{k}", arrays[f"in_{k}"].shape, mybir.dt.from_np(arrays[f"in_{k}"].dtype),
                           kind="ExternalInput").ap() for k in a}
    out = nc.dram_tensor("out", (P, B * LT, H), F32, kind="ExternalOutput").ap()
    decoder(nc, d, out)
    got = run_bass_kernel_spmd(nc, [arrays], core_ids=[0]).results[0]["out"]
    return got.transpose(1, 0, 2).reshape(B, L, H)
```

```python
from contextlib import ExitStack

import concourse.bass as bass
from concourse import mybir

F32 = mybir.dt.float32
BF16 = mybir.dt.bfloat16
U32 = mybir.dt.uint32
ALU = mybir.AluOpType
ACT = mybir.ActivationFunctionType
AX = mybir.AxisListType

P = 128
B, L, H = 4, 256, 256
LT = L // P
HT = H // P
E, N, TR, KC = 512, 16, 128, 4
ET = E // P
C = 64
TOPK = int(L * 0.3)
F0E, F0F, F0S = 8, 176, 352
F1E, F1F, F1S = 8, 128, 256
F0, F1 = F0E * F0F + F0S, F1E * F1F + F1S
F0T, F1T = -(-F0 // P), F1 // P
EP = ET // 2
ROUNDS = -(-TOPK // 8)
DA_RING, DBU_RING, ST_RING = 6, 4, 6
WORK = 6
STREAM_RING = 6
VECTOR_TILES = 1
GS_RING = 3


DOWN0, DOWN1 = 3 + 3 * (F0T // 2), 3 + 3 * (F1T // 2)
DOWN_STEPS = {"ffn0": F0T // 2, "ffn1": F1T // 2}
PRE_STEPS, ADJ_STEPS = 6, ROUNDS + 5


def rest_steps():
    def ffn(stage, down):
        gate, up, weigh = (list(range(3 + i, down, 3)) for i in range(3))
        steps = [0, 1, gate[0], up[0], 2]
        for i in range(1, len(gate)):
            steps += [gate[i], up[i], weigh[i - 1]]
        return [(stage, k) for k in steps + [weigh[-1]] + list(range(down, down + DOWN_STEPS[stage] + 1))]

    return ([("out", k) for k in range(4)] + [("xat0", k) for k in range(5)] + ffn("ffn0", DOWN0),
            [("hgrn", k) for k in range(8)] + ffn("ffn1", DOWN1))


AT = {
    "out": [0, 0.25, 1, 3],
    "xat0": [3, 3, 3.5, 4, 4.25],
    "ffn0": [4.25, 6, 7.25, 6, 6.75, 8, 7.5, 8, 8.5, 8.25, 8.5, 9.25, 9, 9, 10.5, 9.25, 9.5, 11.5, 11.5, 11.5,
        12, 11.75, 12, 12, 13.5, 14, 14.25, 14.75, 15, 15.5, 15.75, 16.25],
    "hgrn": [0.25, 0.25, 0.25, 0.25, 1.5, 2.25, 2.25, 2.25],
    "ffn1": [3, 3.25, 3.25, 3.25, 3.25, 5.25, 4, 4.5, 5.75, 5.25, 5.25, 6.75, 6.75, 6.75, 7.25, 6.75, 6.75,
        7.5, 8, 11.5, 11.5, 12, 13, 13.5],
    "last ffn1": [1.5, 2, 2.75, 2.5, 2.75, 3.5, 3.25, 3.5, 8.25, 3.5, 7, 9, 8.75, 9, 11, 9, 9.75, 11.25,
        12.25, 12.25, 13.75, 14.5, 15.75, 17.5],
    "last hgrn": [0, 0, 0, 0, 0.25, 0.5, 0.75, 1.25],
    "last xat0": [1, 1.25, 1.5, 2, 2],
    "last ffn0": [2, 3, 4.75, 3.25, 3.25, 7.5, 4.75, 7.25, 9, 8.5, 8.5, 14, 11, 11.25, 17.75, 17.75, 17.75,
        18, 18, 18, 18, 18, 18, 18, 18, 18, 18, 18, 18, 18, 18, 18],
    "last out": [0, 0, 0.25, 0.5],
    "adj": [1, 1.5, 1.5, 1.5, 1.75, 6.5, 7.5, 8.25, 10.25, 12, 12.75, 13, 13.75, 14.25, 16.25],
    "pre": [3.5, 5.5, 5.5, 5.5, 9.5, 11.5],
    "first adj": [-6, -5.25, -4, -4, -3.75, -3.25, 0, 1.75, 3.25, 4.25, 5.5, 7, 8.5, 9.75, 11.25],
    "first pre": [2.5, 4.75, 8.5, 12.25, 14.5, 15],
    "second out": [1, 1, 3.25, 3.5],
    "second xat0": [4, 4.25, 4.75, 5, 5],
    "second ffn0": [5, 6, 6.5, 6, 6, 8.25, 7.25, 7.75, 9.5, 8.75, 9, 10.5, 9.5, 9.75, 11.5, 11, 11.25, 12.5,
        11.5, 11.75, 12.5, 12.5, 12.5, 12.5, 13.25, 13.75, 14.25, 14.25, 15.5, 16.25, 16.25, 16.5],
    "second adj": [1.75, 1.75, 3, 3, 4.25, 6.5, 6.75, 6.75, 7, 7, 11.25, 12.75, 13, 14.25, 16.5],
    "second pre": [5.5, 6.25, 7.5, 13.25, 16, 16.75],
    "third out": [0, 0.25, 1.25, 1.75],
    "third xat0": [3, 3, 3.5, 3.75, 3.75],
    "third ffn0": [3.75, 5, 8.75, 5, 5, 8.75, 8.75, 8.75, 9, 9, 9, 9, 9, 9, 9.25, 9.25, 9.25, 11.25, 11.25,
        11.25, 13.5, 12.5, 13.25, 14.25, 14.75, 14.75, 15, 16, 16.25, 16.5, 16.75, 17.25],
    "third adj": [2.25, 2.25, 2.25, 2.25, 2.75, 4.75, 9.5, 9.5, 10.25, 11.5, 11.75, 13.5, 14.25, 15.25, 18],
    "third pre": [10.5, 12, 13, 14.75, 16.5, 17.5],
    "third hgrn": [0, 0.25, 1, 1, 2.25, 2.5, 2.5, 2.75],
    "third ffn1": [2.75, 2.75, 2.75, 2.75, 2.75, 5, 4, 5, 7, 5.5, 6.5, 7.75, 7, 7.25, 8.5, 7.75, 8, 9.25, 10,
        10.75, 11.5, 12.25, 13.25, 14],
}
LAG = {
    ("pe", "ffn0", 2): 0.25, ("pe", "ffn0", 12): 0.5, ("pe", "ffn0", 22): 0.75, ("pe", "ffn0", 23): 1,
    ("pe", "ffn0", 30): 2.5, ("pe", "ffn1", 0): 0.25, ("pe", "ffn1", 2): 1, ("pe", "ffn1", 5): -1.5,
    ("pe", "hgrn", 4): 0.5, ("pe", "xat0", 2): 1.5,
    ("act", "adj", 1): 0.5, ("act", "adj", 12): 1.25, ("act", "ffn0", 2): 0.25, ("act", "ffn1", 4): 1.5,
    ("act", "hgrn", 7): 0.25, ("act", "xat0", 2): 0.25, ("act", "xat0", 3): 1,
    ("dve", "adj", 2): 0.25, ("dve", "adj", 3): 0.5, ("dve", "adj", 4): 0.5, ("dve", "adj", 5): -0.75,
    ("dve", "adj", 8): -0.25, ("dve", "ffn0", 1): -0.25, ("dve", "ffn0", 2): -5, ("dve", "ffn0", 12): 0.5,
    ("dve", "ffn0", 17): 0.25, ("dve", "ffn0", 20): -0.5, ("dve", "ffn0", 21): -0.25,
    ("dve", "ffn1", 0): 0.75, ("dve", "ffn1", 4): -1.75, ("dve", "ffn1", 5): -1.25,
    ("dve", "ffn1", 17): -0.25, ("dve", "ffn1", 22): -1.25, ("dve", "out", 3): -1.25, ("dve", "pre", 2): 0.25,
    ("pool", "xat0", 3): 0.75,
}


def timeline(engine):
    PHASE = {0: "first ", 1: "second ", 2: "third ", B: "last "}
    layer0, layer1 = rest_steps()
    order = [("init", 0, 0)]
    for b in range(B + 2):
        chains = [
            [("adj", b, k) for k in range(ADJ_STEPS)] if b < B else [],
            [(stage, b - 1, k) for stage, k in layer0] if 1 <= b < B + 1 else [],
            [(stage, b - 2, k) for stage, k in layer1] if b >= 2 else [],
            [("pre", b + 1, k) for k in range(PRE_STEPS)] if b + 1 < B else [],
        ]
        placed = [(k, step) for k, step in enumerate([("scan", b, k) for k in range(N + 2)] if b < B else [])]
        if b == 0:
            placed += [(k - PRE_STEPS, ("pre", 0, k)) for k in range(PRE_STEPS)]
        for steps in chains:
            place = -PRE_STEPS
            for step in steps:
                stage, _, k = step
                at = AT[PHASE.get(b, "") + stage][k] if b <= B else 0
                place = max(place, at + LAG.get((engine, stage, k), 0))
                placed.append((place, step))
        order += [step for _, step in sorted(placed, key=lambda x: x[0])]
        if b == 0:
            order.append(("init", 0, 1))
    return order


BANKS = {
    ("pre", 0): ["hid0", "hid1"], ("pre", 2): ["dt", "bT"], ("pre", 3): ["z0", "z1"],
    ("adj", 0): ["qk"], ("adj", 1): ["sim"], ("adj", ROUNDS + 4): ["adjT"],
    ("out", 0): ["kv", "gate0", "gate1"], ("out", 1): ["gram"], ("out", 2): ["mamba"],
    ("xat0", 0): ["x1T"], ("xat0", 1): ["att"],
    ("ffn0", 0): ["x2T"], ("ffn0", 1): ["logit0"], ("ffn0", 2): ["w0T"],
    ("ffn0", DOWN0): ["ffn0"],
    ("hgrn", 0): ["x3T"], ("hgrn", 1): ["hi"], ("hgrn", 2): ["hf"], ("hgrn", 3): ["hg"],
    ("hgrn", 4): ["ss", "hgrn"],
    ("ffn1", 0): ["x5T"], ("ffn1", 1): ["logit1"], ("ffn1", 2): ["w1T"],
    ("ffn1", DOWN1): ["ffn1"],
}
for _lay, _tiles, _routed in ((0, F0T, F0E * F0F), (1, F1T, F1)):
    for _t in range(_tiles // 2):
        BANKS[f"ffn{_lay}", 3 + 3 * _t] = [f"g{_lay}_{_t}"]
        BANKS[f"ffn{_lay}", 4 + 3 * _t] = [f"u{_lay}_{_t}"]
        BANKS[f"ffn{_lay}", 5 + 3 * _t] = [f"e{_lay}_{_t}"] if 2 * P * _t < _routed else []


SUM0, SUM1 = DOWN0 + DOWN_STEPS["ffn0"] - 1, DOWN1 + DOWN_STEPS["ffn1"] - 1
ROOTS = [("out", 2), ("xat0", 1), ("xat0", 3), ("ffn0", SUM0), ("hgrn", 4), ("hgrn", 5), ("hgrn", 6), ("ffn1", SUM1)]
ROWS = [("out", 3), ("xat0", 4), ("ffn0", SUM0 + 1), ("hgrn", 6), ("hgrn", 7), ("ffn1", SUM1 + 1)]


def decoder(nc, d, out):
    pe_order, dve_order, act_order, pool_order = (timeline(engine) for engine in ("pe", "dve", "act", "pool"))
    with ExitStack() as ctx:
        def sb(name, shape, dt=F32):
            return ctx.enter_context(nc.sbuf_tensor(name, shape, dt))

        def sem(name):
            return ctx.enter_context(nc.semaphore(name))

        loads = []
        xT = sb("xT", [P, 2, HT, L])
        ctxT = sb("ctxT", [C, 2, L])
        loads.append((xT[:, 0], d["xT"][:, :, 0:L], 0))

        def load(name, shape, src, part, dst=None, dt=F32):
            t = sb(name, shape, dt)
            loads.append((t[:] if dst is None else dst(t), src, part))
            return t

        w_in = load("w_in", [P, HT, 2 * E], d["w_in"], 0)
        cw = load("cw", [P, ET, KC], d["cw"], 0)
        cb = load("cb", [P, ET], d["cb"], 0)
        ident = load("ident", [P, P], d["ident"], 0)
        w_x = load("w_x", [P, ET, TR + P], d["w_x"], 1)
        w_dt = load("w_dt", [P, E], d["w_dt"], 1)
        b_dt = load("b_dt", [P, ET], d["b_dt"], 1)
        a_log = load("a_log", [P, ET, N], d["a_log"], 1)
        loads.append((ctxT[:, 0], d["ctxT"][:, 0:L], 2))
        loads.append((ctxT[:, 1], d["ctxT"][:, L:2 * L], 2))
        loads.append((xT[:, 1], d["xT"][:, :, L:2 * L], 2))
        wqT = load("wqT", [C, C], d["wqT"], 2)
        wkT = load("wkT", [C, C], d["wkT"], 2)
        wkvT = load("wkvT", [C, C], d["wkvT"], 2)
        b_k = load("b_k", [C, 1], d["b_k"], 2)
        gam = load("gam", [P, 1], d["gam"].partition_broadcast(P), 2)
        skip = load("skip", [P, ET], d["skip"], 3)
        w_out = load("w_out", [P, ET, H], d["w_out"], 3)
        rows0, rows1 = (sb(f"rows_of_layer{i}", [P, 2, LT, H]) for i in range(2))
        loads.append((rows0[:, 0], d["x"][:, 0:LT, :], 3))
        lng = load("lng", [P, L], d["lng"].partition_broadcast(P), 3)
        lnb = load("lnb", [P, L], d["lnb"].partition_broadcast(P), 3)
        sel_bc = load("sel_bc", [P, 2 * N], d["sel_bc"], 1, dt=BF16)
        iota = load("iota", [P, F0E], d["iota"].partition_broadcast(P), 3)
        sel0 = load("sel0", [3 * F0E, F0E * F0F], d["sel0"], 3, dt=BF16)
        sel1 = load("sel1", [3 * (F1E + 1), F1T], d["sel1"], 3, dt=BF16)
        wr = load("wr", [P, HT, F0E], d["wr"], 3)
        stream = sb("stream", [P, STREAM_RING, 2, L])
        whi = load("whi", [P, HT, H], d["whi"], 4)
        whf = load("whf", [P, HT, H], d["whf"], 4)
        whg = load("whg", [P, HT, H], d["whg"], 4)
        who = load("who", [P, HT, H], d["who"], 4)
        gn = load("gn", [P, HT], d["gn"], 4)
        wr1 = load("wr1", [P, HT, F1E + 1], d["wr1"], 4)
        wg1 = load("wg1", [P, HT, F1], d["wg1"], 4)
        wu1 = load("wu1", [P, HT, F1], d["wu1"], 4)
        PARTS = 5

        a_neg = sb("a_neg", [P, ET, N])
        ones = sb("ones", [P, 1])
        mhalf = sb("mhalf", [P, LT])
        gth = sb("gth", [P, 1])
        gq = sb("gq", [P, 1])
        g2 = sb("g2", [P, 1])

        big0, big1 = sb("big0", [P, F0T, L]), sb("big1", [P, F1T, L])
        sg, yg = big0[:, 0:ET, :], big0[:, ET:2 * ET, :]
        si, tf, sgg, o, sq = (big1[:, HT * i:HT * (i + 1), :] for i in range(5))

        hs = sb("hs", [P, 2, ET, L])
        dt = sb("dt", [P, L])
        du = sb("du", [P, 2, ET, L])
        za = sb("za", [P, ET, L])
        dts = sb("dts", [P, 2, ET, L])
        bc_parts = sb("bc_parts", [P, 2, L], BF16)
        bc = sb("bc", [P, 2, 4, L])
        dA = sb("dA", [P, DA_RING, 2, L])
        dbu = sb("dbu", [P, DBU_RING, 2, L])
        st = sb("st", [P, ST_RING, 2, L])
        acc = sb("acc", [P, ET, L])
        qk = sb("qk", [C, 2 * L])
        kv = sb("kv", [C, L])
        gram = sb("gram", [P, LT, L])
        sim = sb("sim", [P, LT, L])
        wk = sb("wk", [P, LT, L])
        m8 = sb("m8", [P, LT, 8])
        S = sb("S", [P, 2, LT, L])
        rows = [rows0[:, i % 2] for i in range(3)] + [rows1[:, i % 2] for i in range(4)]
        r = [sb(f"r{i}", [P, LT, H]) for i in range(2)]
        xsT = [sb(f"xsT{i}", [P, HT, L]) for i in range(2)]
        ex = r[0]
        gs = sb("gs", [P, GS_RING, 2, L])
        bst = [sb(f"bst{i}", [P, LT, 6]) for i in range(2)]
        mv = [sb(f"mv{i}", [P, LT, 2]) for i in range(2)]
        var = [sb(f"var{i}", [P, LT]) for i in range(2)]
        rstd = [sb(f"rstd{i}", [P, LT]) for i in range(2)]
        nmx = sb("nmx", [P, LT])
        es = sb("es", [P, LT])
        ri = sb("ri", [P, LT])
        dsc = sb("dsc", [P, LT, 2])
        ths = sb("ths", [P, LT, 2])
        lgs = sb("lgs", [P, LT, F1E + 1])
        exr = sb("exr", [P, LT, F0E])
        sc = sb("sc", [P, LT, F0E])
        t8 = [sb(f"t8{i}", [P, LT, 8]) for i in range(2)]
        i8 = [sb(f"i8{i}", [P, LT, 8], U32) for i in range(2)]
        if8 = [sb(f"if8{i}", [P, LT, 2]) for i in range(2)]
        pr = sb("pr", [P, LT, 2])
        wa = [sb(f"wa{i}", [P, LT, F0E]) for i in range(2)]
        wb = [sb(f"wb{i}", [P, LT, F0E]) for i in range(2)]
        wf = [sb(f"wf{i}", [P, LT, 2, F1E + 1]) for i in range(2)]
        whl = [sb(f"whl{i}", [P, LT, 3 * (F1E + 1)]) for i in range(2)]
        wpart = [sb(f"wpart{i}", [P, LT, F1E + 1], BF16) for i in range(2)]
        wT = [sb(f"wT{i}", [3 * (F1E + 1), L], BF16) for i in range(2)]

        def bank(name):
            return ctx.enter_context(nc.psum_tensor(name, [P, 512], F32))

        bc_bank = [bank(f"bc_bank{i}") for i in range(2)]
        work = [bank(f"work{i}") for i in range(WORK)]

        loaded = [sem(f"loaded{i}") for i in range(PARTS)]
        part_size = [16 * sum(1 for l in loads if l[2] == i) for i in range(PARTS)]
        work_full = [sem(f"work_full{i}") for i in range(WORK)]
        work_read = [sem(f"work_read{i}") for i in range(WORK)]
        stream_loaded = [sem(f"stream_loaded{i}") for i in range(STREAM_RING)]
        names = """consts_ready a_exp a_ready gam_tanh conv0 hs_ready exp_ready sp_ready dts_ready du_ready
            dA_ready bc_parts_ready bc_full bc_ready dbu_ready scan_done prod_ready vector_prod acc_done
            th_ready adj_ready yg_ready var_ready rstd_ready rows_ready att_max att_exp nmx_ready dsc_ready
            ths_ready whl_ready init_late q_ready o_ready sq_ready dve_link gate_tanh out_done ctxT_loaded
            xT_loaded x_loaded down_used mask_ready""".split()
        s = {n: sem(n) for n in names}

        use, root, row, uses = {}, {}, {}, [0, 0]
        chunk, var_count, tanh_count = {}, {}, {}
        for stage, b, k in pe_order:
            if stage in DOWN_STEPS:
                down = (DOWN0, DOWN1)[stage == "ffn1"]
                if stage == "ffn0" and 3 <= k < down and (k - 3) % 3 < 2:
                    chunk[BANKS[stage, k][0], b] = len(chunk)
                elif down <= k < down + DOWN_STEPS[stage]:
                    chunk[f"{stage}_{k - down}", b] = len(chunk)
            for n in BANKS.get((stage, k), []):
                last_bank = n in ("ffn0", "ffn1")
                uses[last_bank] += 1
                i = uses[last_bank] - 1
                use[n, b] = (WORK - 1, i) if last_bank else (i % (WORK - 1), i // (WORK - 1))
        for stage, b, k in pool_order:
            if (stage, k) in ROOTS:
                root[stage, b, k] = len(root) + 1
        for stage, b, k in dve_order:
            if (stage, k) in ROWS:
                row[ROWS.index((stage, k)) + 1, b] = len(row) + 1
            if (stage, k) in ROOTS and (stage, k) != ("hgrn", 4):
                var_count[stage, b, k] = len(var_count) + 1
        gates = {("out", 0): ["gate0", "gate1"], ("hgrn", 1): ["hi"], ("hgrn", 3): ["hg"]}
        gated = []
        for stage, b, k in act_order:
            names_ = BANKS.get((stage, k), [])
            is_pair = stage in DOWN_STEPS and len(names_) == 1 and names_[0][0] == "g"
            for n in gates.get((stage, k), []) + (names_ if is_pair else []):
                tanh_count[n, b] = len(tanh_count) + 1
            if is_pair:
                gated.append((names_[0], b))

        def whl_count(lay, b):
            return [x for x in dve_order if x[0] in ("ffn0", "ffn1") and x[2] == 2].index((f"ffn{lay}", b, 2)) + 1

        numbers = {i: key for key, i in chunk.items()}

        def chunk_used(i):
            name, b = numbers[i]
            if not name.startswith("ffn"):
                return full(name, b)
            if name in (f"ffn0_{F0T // 2 - 1}", f"ffn1_{F1T // 2 - 1}"):
                return full(name[:4], b)
            downs = [j for j in range(i + 1) if numbers[j][0].startswith("ffn")
                     and numbers[j][0] not in (f"ffn0_{F0T // 2 - 1}", f"ffn1_{F1T // 2 - 1}")]
            return s["down_used"], len(downs)

        def vector_weighs(tile):
            return tile < N * EP and tile % (2 * EP) < VECTOR_TILES

        def weighed(tiles):
            by_vector = sum(vector_weighs(i) for i in range(tiles))
            return tiles - by_vector, by_vector

        def work_bank(n, b):
            return work[use[n, b][0]]

        def full(n, b):
            return work_full[use[n, b][0]], use[n, b][1] + 1

        def read(n, b):
            return work_read[use[n, b][0]], use[n, b][1] + 1

        def halves(t):
            return t[:, :].rearrange("p (t l) -> p t l", t=2)

        block = ctx.enter_context(nc.Block())

        @block.sync
        def _(sp):
            for dst, src, part in loads:
                sp.dma_start(dst, src).then_inc(loaded[part], 16)

            def load_chunk(i):
                if i >= len(chunk):
                    return
                if i >= STREAM_RING:
                    sp.wait_ge(*chunk_used(i - STREAM_RING))
                name, _ = numbers[i]
                lay, at = int(name[3] if name.startswith("ffn") else name[1]), int(name.split("_")[1])
                src = 2 * at + "gu".index(name[0]) if name[0] in "gu" else F0T + lay * F0T // 2 + at
                sp.dma_start(stream[:, i % STREAM_RING], d["stream"][:, src, :, :])\
                    .then_inc(stream_loaded[i % STREAM_RING], 16)

            for i in range(STREAM_RING):
                load_chunk(i)
            for stage, b, k in pe_order:
                if (stage, k) == ("out", 0) and b + 2 < B:
                    sp.wait_ge(*full("kv", b))
                    sp.wait_ge(*full("qk", b))
                    sp.dma_start(ctxT[:, b % 2], d["ctxT"][:, (b + 2) * L:(b + 3) * L]).then_inc(s["ctxT_loaded"], 16)
                    sp.wait_ge(*full("gate1", b))
                    sp.dma_start(xT[:, b % 2], d["xT"][:, :, (b + 2) * L:(b + 3) * L]).then_inc(s["xT_loaded"], 16)
                for n in BANKS.get((stage, k), []):
                    if (n, b) in chunk:
                        load_chunk(chunk[n, b] + STREAM_RING)
                if stage in DOWN_STEPS:
                    down = (DOWN0, DOWN1)[stage == "ffn1"]
                    if down <= k < down + DOWN_STEPS[stage]:
                        load_chunk(chunk[f"{stage}_{k - down}", b] + STREAM_RING)
                if (stage, k) == ("ffn0", SUM0 + 1) and b + 1 < B:
                    sp.wait_ge(s["rows_ready"], row[3, b])
                    sp.dma_start(rows[0], d["x"][:, (b + 1) * LT:(b + 2) * LT, :]).then_inc(s["x_loaded"], 16)
                if (stage, k) == ("ffn1", SUM1 + 1):
                    sp.wait_ge(s["rows_ready"], row[6, b])
                    sp.dma_start(out[:, b * LT:(b + 1) * LT, :], rows[6]).then_inc(s["out_done"], 16)
            sp.wait_ge(s["out_done"], 16 * B)

        @block.gpsimd
        def _(pool):
            gp = nc.gpsimd
            gp.memset(ones[:], 1.0)
            gp.memset(mhalf[:], -0.5)
            gp.memset(dA[:, :, :, 0:1], 0.0).then_inc(s["consts_ready"], 1)
            pool.wait_ge(s["consts_ready"], 1)
            for stage, b, k in pool_order:
                if stage == "scan" and k < N:
                    i = b * N + k
                    if k == 0:
                        pool.wait_ge(s["du_ready"], b + 1)
                    if k % 2 == 0:
                        pool.wait_ge(s["bc_ready"], i // 2 + 1)
                    for q in range(EP):
                        tile = i * EP + q
                        if tile >= DBU_RING:
                            pool.wait_ge(s["scan_done"], tile - DBU_RING + 1)
                        gp.tensor_tensor(dbu[:, tile % DBU_RING], du[:, b % 2, 2 * q:2 * q + 2, :],
                                         bc[:, i // 2 % 2, k % 2:k % 2 + 1, :].to_broadcast([P, 2, L]),
                                         ALU.mult).then_inc(s["dbu_ready"], 1)
                if stage == "scan" and 1 <= k <= N:
                    i = b * N + k - 1
                    for q in range(EP):
                        tile = i * EP + q
                        if vector_weighs(tile):
                            continue
                        pool.wait_ge(s["scan_done"], tile + 1)
                        gp.tensor_tensor(st[:, tile % ST_RING], st[:, tile % ST_RING],
                                         bc[:, i // 2 % 2, 2 + i % 2:3 + i % 2, :].to_broadcast([P, 2, L]),
                                         ALU.mult).then_inc(s["prod_ready"], 1)
                if (stage, b, k) in root:
                    if stage == "hgrn" and k == 4:
                        pool.wait_ge(*read("ss", b))
                    else:
                        pool.wait_ge(s["var_ready"], var_count[stage, b, k])
                    layer = int(stage in ("hgrn", "ffn1"))
                    gp.tensor_tensor(rstd[layer][:, :], var[layer][:, :], mhalf[:, :], ALU.pow)\
                        .then_inc(s["rstd_ready"], 1)

        @block.tensor
        def _(pe):
            mm = nc.tensor.matmul

            def transpose(dst, src):
                return nc.tensor.transpose(dst, src, ident[:, :])

            def claim(n, b):
                i, u = use[n, b]
                if u:
                    pe.wait_ge(work_read[i], u)
                return work[i]

            def fill(last, n, b):
                last.then_inc(work_full[use[n, b][0]], 1)

            def transposes(n, b, src, rows_, cols, width=P):
                t = claim(n, b)
                for c in range(cols):
                    for r_ in range(rows_):
                        last = transpose(t[0:width, (c * rows_ + r_) * P:(c * rows_ + r_ + 1) * P], src(r_, c))
                fill(last, n, b)

            def product(t, col, lhs, rhs, depth, width):
                for c in range(depth):
                    last = mm(t[:, col:col + width], lhs(c), rhs(c), start=(c == 0), stop=(c == depth - 1))
                return last

            def in_projection(b, names, first):
                for i, n in enumerate(names):
                    t = claim(n, b)
                    for f in range(2):
                        m = first + (2 * i + f) * P
                        last = product(t, f * L, lambda c: w_in[:, c, m:m + P], lambda c: xT[:, b % 2, c, :], HT, L)
                    fill(last, n, b)

            def streamed(name, b):
                i = chunk[name, b]
                pe.wait_ge(stream_loaded[i % STREAM_RING], 16 * (i // STREAM_RING + 1))
                return stream[:, i % STREAM_RING]

            def ffn(b, k, lay, wg, wu, sel, nexp, routed, wrt, h, tiles):
                down = 3 + 3 * (tiles // 2)
                if k == 0:
                    n = 2 if lay == 0 else 5
                    pe.wait_ge(s["rows_ready"], row[n, b])
                    transposes(f"x{n}T", b, lambda r_, c: rows[n][:, r_, c * P:(c + 1) * P], LT, HT)
                elif k == 1:
                    pe.wait_ge(*read(f"x{2 if lay == 0 else 5}T", b))
                    t = claim(f"logit{lay}", b)
                    for lt in range(LT):
                        last = product(t, lt * nexp, lambda c: xsT[lay][:, c, lt * P:(lt + 1) * P],
                                       lambda c: wrt[:, c, :], HT, nexp)
                    fill(last, f"logit{lay}", b)
                elif k == 2:
                    pe.wait_ge(s["whl_ready"], whl_count(lay, b))
                    transposes(f"w{lay}T", b, lambda r_, c: whl[lay][:, r_, 0:3 * nexp], LT, 1, 3 * nexp)
                elif k < down:
                    i, kind = divmod(k - 3, 3)
                    if kind < 2:
                        n = f"{'gu'[kind]}{lay}_{i}"
                        t = claim(n, b)
                        w = streamed(n, b) if lay == 0 else (wg, wu)[kind][:, :, 2 * i * P:2 * (i + 1) * P]
                        for f in range(2):
                            last = product(t, f * L, lambda c: w[:, c, f * P:(f + 1) * P], lambda c: xsT[lay][:, c, :],
                                           HT, L)
                        fill(last, n, b)
                    elif BANKS[f"ffn{lay}", k]:
                        n = f"e{lay}_{i}"
                        t = claim(n, b)
                        if i == 0:
                            pe.wait_ge(*read(f"w{lay}T", b))
                        for f in range(2):
                            m = (2 * i + f) * P
                            if m < routed:
                                member = sel[:, m:m + P] if lay == 0 else \
                                    sel[:, m // P:m // P + 1].to_broadcast([3 * nexp, P])
                                last = mm(t[:, f * L:(f + 1) * L], member, wT[lay][0:3 * nexp, :],
                                          start=True, stop=True)
                        fill(last, n, b)
                elif k < down + tiles // 2:
                    if k == down:
                        pe.wait_ge(*read(f"u{lay}_{tiles // 2 - 1}", b))
                        pe.wait_ge(*read(f"e{lay}_{(routed - 1) // (2 * P)}", b))
                        claim(f"ffn{lay}", b)
                    w = streamed(f"ffn{lay}_{k - down}", b)
                    t = work_bank(f"ffn{lay}", b)
                    for lt in range(LT):
                        for f in range(2):
                            c = 2 * (k - down) + f
                            last = mm(t[:, lt * H:(lt + 1) * H], h[:, c, lt * P:(lt + 1) * P], w[:, f, :],
                                      start=(c == 0 and lt == 0), stop=(c == tiles - 1 and lt == LT - 1))
                    if k == down + tiles // 2 - 1:
                        fill(last, f"ffn{lay}", b)
                    else:
                        last.then_inc(s["down_used"], 1)

            def broadcast_bc(b, pair):
                i = b * N // 2 + pair
                if i:
                    pe.wait_ge(s["bc_ready"], i)
                for kind in range(2):
                    for j in range(2):
                        n = kind * N + 2 * pair + j
                        last = mm(bc_bank[kind][:, j * L:(j + 1) * L], sel_bc[:, n:n + 1].to_broadcast([P, P]),
                                  bc_parts[:, b % 2, :], start=True, stop=True)
                last.then_inc(s["bc_full"], 1)

            for stage, b, k in pe_order:
                p = b % 2
                if stage == "init" and k == 0:
                    pe.wait_ge(loaded[0], part_size[0])
                if stage == "init" and k == 1:
                    for i in range(1, PARTS):
                        pe.wait_ge(loaded[i], part_size[i])
                    pe.wait_ge(s["consts_ready"], 1)
                    pe.wait_ge(s["init_late"], 1)
                if stage == "pre" and k == 0:
                    if b >= 2:
                        pe.wait_ge(s["xT_loaded"], 16 * (b - 1))
                    in_projection(b, ["hid0", "hid1"], 0)
                if stage == "pre" and k == 2:
                    if b == 0:
                        pe.wait_ge(loaded[1], part_size[1])
                    t = claim("dt", b)
                    pe.wait_ge(s["hs_ready"], b + 1)
                    fill(product(t, 0, lambda c: w_x[:, c, 0:TR], lambda c: hs[:, p, c, :], ET, L), "dt", b)
                    t = claim("bT", b)
                    fill(product(t, 0, lambda c: w_x[:, c, TR:TR + P],
                                 lambda c: hs[:, p, c, :], ET, L), "bT", b)
                if stage == "pre" and k == 3:
                    pe.wait_ge(*read("dt", b))
                    for i in range(2):
                        t = claim(f"z{i}", b)
                        for f in range(2):
                            m = (2 * i + f) * P
                            last = product(t, f * L, lambda c: w_dt[:, m:m + P], lambda c: dt[:, :], 1, L)
                        fill(last, f"z{i}", b)
                if stage == "pre" and k == 5:
                    pe.wait_ge(s["bc_parts_ready"], b + 1)
                    broadcast_bc(b, 0)
                if stage == "adj" and k == 0:
                    if b == 0:
                        pe.wait_ge(loaded[2], part_size[2])
                    if b >= 2:
                        pe.wait_ge(s["ctxT_loaded"], 16 * (b - 1))
                    t = claim("qk", b)
                    mm(t[0:C, 0:L], wqT[:, :], ctxT[:, p], start=True, stop=True)
                    fill(mm(t[0:C, L:2 * L], wkT[:, :], ctxT[:, p], start=True, stop=True), "qk", b)
                if stage == "adj" and k == 1:
                    pe.wait_ge(*read("qk", b))
                    t = claim("sim", b)
                    for lt in range(LT):
                        last = mm(t[:, lt * L:(lt + 1) * L], qk[:, lt * P:(lt + 1) * P], qk[:, L:2 * L],
                                  start=True, stop=True)
                    fill(last, "sim", b)
                if stage == "adj" and k == ROUNDS + 4:
                    pe.wait_ge(s["adj_ready"], b + 1)
                    transposes("adjT", b, lambda r_, c: wk[:, r_, c * P:(c + 1) * P], LT, LT)
                if stage == "scan":
                    if k % 2 and k + 1 < N:
                        broadcast_bc(b, (k + 1) // 2)
                if stage == "out" and k == 0:
                    t = claim("kv", b)
                    fill(mm(t[0:C, 0:L], wkvT[:, :], ctxT[:, p], start=True, stop=True), "kv", b)
                    in_projection(b, ["gate0", "gate1"], E)
                if stage == "out" and k == 1:
                    pe.wait_ge(*read("kv", b))
                    t = claim("gram", b)
                    for lt in range(LT):
                        last = mm(t[:, lt * L:(lt + 1) * L], kv[:, lt * P:(lt + 1) * P], kv[:, :],
                                  start=True, stop=True)
                    fill(last, "gram", b)
                if stage == "out" and k == 2:
                    pe.wait_ge(s["yg_ready"], b + 1)
                    t = claim("mamba", b)
                    for lt in range(LT):
                        last = product(t, lt * H, lambda c: yg[:, c, lt * P:(lt + 1) * P], lambda c: w_out[:, c, :],
                                       ET, H)
                    fill(last, "mamba", b)
                if stage == "xat0" and k == 0:
                    pe.wait_ge(s["rows_ready"], row[1, b])
                    transposes("x1T", b, lambda r_, c: rows[1][:, r_, c * P:(c + 1) * P], LT, HT)
                if stage == "xat0" and k == 1:
                    pe.wait_ge(*read("x1T", b))
                    pe.wait_ge(*read("gram", b))
                    t = claim("att", b)
                    for lt in range(LT):
                        last = product(t, lt * L, lambda c: xsT[0][:, c, lt * P:(lt + 1) * P],
                                       lambda c: gram[:, c, :], LT, L)
                    fill(last, "att", b)
                if stage == "ffn0":
                    ffn(b, k, 0, None, None, sel0, F0E, F0E * F0F, wr, big0, F0T)
                if stage == "ffn1":
                    ffn(b, k, 1, wg1, wu1, sel1, F1E + 1, F1, wr1, big1, F1T)
                if stage == "hgrn" and k == 0:
                    pe.wait_ge(s["rows_ready"], row[3, b])
                    transposes("x3T", b, lambda r_, c: rows[3][:, r_, c * P:(c + 1) * P], LT, HT)
                if stage == "hgrn" and 1 <= k < 4:
                    n, w = (("hi", whi), ("hf", whf), ("hg", whg))[k - 1]
                    pe.wait_ge(*read("x3T", b))
                    t = claim(n, b)
                    for f in range(HT):
                        last = product(t, f * L, lambda c: w[:, c, f * P:(f + 1) * P], lambda c: xsT[1][:, c, :], HT, L)
                    fill(last, n, b)
                if stage == "hgrn" and k == 4:
                    t = claim("ss", b)
                    pe.wait_ge(s["sq_ready"], b + 1)
                    for lt in range(LT):
                        last = product(t, lt, lambda c: sq[:, c, lt * P:(lt + 1) * P], lambda c: ones[:, :], HT, 1)
                    fill(last, "ss", b)
                    t = claim("hgrn", b)
                    pe.wait_ge(s["q_ready"], b + 1)
                    for lt in range(LT):
                        last = product(t, lt * H, lambda c: sgg[:, c, lt * P:(lt + 1) * P], lambda c: who[:, c, :],
                                       HT, H)
                    fill(last, "hgrn", b)

        @block.scalar
        def _(act):
            A = nc.scalar.activation

            def evacuate(n, b, dst, src=None, func=ACT.Copy, **kw):
                act.wait_ge(*full(n, b))
                A(dst, work_bank(n, b)[:, :] if src is None else src, func, **kw).then_inc(work_read[use[n, b][0]], 1)

            def gate_tanh(n, b, dst):
                act.wait_ge(*full(n, b))
                A(dst.rearrange("p t l -> p (t l)"), work_bank(n, b)[:, :], ACT.Tanh, scale=0.5)\
                    .then_inc(s["gate_tanh"], 1)

            def ffn(b, k, lay, nexp, down):
                if k == 0:
                    n = f"x{2 if lay == 0 else 5}T"
                    evacuate(n, b, xsT[lay][:, :, :].rearrange("p t l -> p (t l)"))
                elif k == 1 and lay == 0:
                    act.wait_ge(s["nmx_ready"], b + 1)
                    t = work_bank("logit0", b)
                    for lt in range(LT):
                        last = A(exr[:, lt, :], t[:, lt * nexp:(lt + 1) * nexp], ACT.Exp, bias=nmx[:, lt:lt + 1],
                                 accum_out=es[:, lt:lt + 1])
                    last.then_inc(work_read[use["logit0", b][0]], 1)
                elif k == 1:
                    act.wait_ge(s["dsc_ready"], b + 1)
                    A(ths[:, :, :], dsc[:, :, :], ACT.Tanh, scale=0.5).then_inc(s["ths_ready"], 1)
                elif k == 2:
                    evacuate(f"w{lay}T", b, wT[lay][0:3 * nexp, :], work_bank(f"w{lay}T", b)[0:3 * nexp, 0:L])
                elif k < down and (k - 3) % 3 == 0:
                    n = f"g{lay}_{(k - 3) // 3}"
                    i = gated.index((n, b))
                    if i >= GS_RING:
                        gate, b_ = gated[i - GS_RING]
                        act.wait_ge(*read("u" + gate[1:], b_))
                    gate_tanh(n, b, gs[:, i % GS_RING, :, :])

            def spread_bc(b, pair):
                i = b * N // 2 + pair
                act.wait_ge(s["bc_full"], i + 1)
                if i >= 2:
                    act.wait_ge(s["dbu_ready"], (i - 1) * 2 * EP)
                    by_pool, by_vector = weighed((i - 1) * 2 * EP)
                    act.wait_ge(s["prod_ready"], by_pool)
                    if by_vector:
                        act.wait_ge(s["vector_prod"], by_vector)
                for kind in range(2):
                    last = A(bc[:, i % 2, 2 * kind:2 * kind + 2, :].rearrange("p j l -> p (j l)"),
                             bc_bank[kind][:, :], ACT.Copy)
                last.then_inc(s["bc_ready"], 1)

            for stage, b, k in act_order:
                p = b % 2
                if stage == "init" and k == 0:
                    act.wait_ge(loaded[0], part_size[0])
                if stage == "pre" and k == 0:
                    if b >= 2:
                        act.wait_ge(s["dbu_ready"], (b - 1) * N * EP)
                    for i in range(2):
                        act.wait_ge(*full(f"hid{i}", b))
                        for f in range(2):
                            t = 2 * i + f
                            last = A(du[:, p, t, :], work_bank(f"hid{i}", b)[:, f * L:(f + 1) * L], ACT.Identity,
                                     scale=cw[:, t, KC - 1:KC], bias=cb[:, t:t + 1])
                        last.then_inc(s["conv0"], 1)
                if stage == "pre" and k == 1:
                    if b >= 2:
                        act.wait_ge(s["yg_ready"], b - 1)
                    act.wait_ge(*read("hid0", b))
                    act.wait_ge(*read("hid1", b))
                    A(hs[:, p], du[:, p], ACT.Silu).then_inc(s["hs_ready"], 1)
                if stage == "pre" and k == 2:
                    if b:
                        act.wait_ge(*full("z1", b - 1))
                    evacuate("dt", b, dt[:, :], work_bank("dt", b)[:, 0:L])
                if stage == "pre" and k == 3:
                    if b == 0:
                        act.wait_ge(loaded[1], part_size[1])
                        A(a_neg[:, :, :], a_log[:, :, :], ACT.Exp).then_inc(s["a_exp"], 1)
                    if b >= 2:
                        act.wait_ge(s["dA_ready"], (b - 1) * N * EP)
                    act.wait_ge(s["bc_parts_ready"], b + 1)
                    for i in range(2):
                        act.wait_ge(*full(f"z{i}", b))
                        for f in range(2):
                            t = 2 * i + f
                            src = work_bank(f"z{i}", b)[:, f * L:(f + 1) * L]
                            A(za[:, t, :], src, ACT.Abs, bias=b_dt[:, t:t + 1])
                            last = A(dts[:, p, t, :], src, ACT.Relu, bias=b_dt[:, t:t + 1])
                        last.then_inc(work_read[use[f"z{i}", b][0]], 1)
                    act.wait_ge(*read("z1", b))
                    A(za[:, :, :], za[:, :, :], ACT.Exp, scale=-1.0).then_inc(s["exp_ready"], 1)
                if stage == "pre" and k == 4:
                    act.wait_ge(s["exp_ready"], b + 1)
                    A(za[:, :, :], za[:, :, :], ACT.Ln, bias=1.0).then_inc(s["sp_ready"], 1)
                if stage == "pre" and k == 5:
                    spread_bc(b, 0)
                if stage == "adj" and k == 0:
                    if b == 0:
                        act.wait_ge(loaded[2], part_size[2])
                        A(gth[:, :], gam[:, :], ACT.Tanh, scale=0.5).then_inc(s["gam_tanh"], 1)
                    evacuate("qk", b, qk[:, :], work_bank("qk", b)[0:C, :])
                if stage == "adj" and k == 1:
                    if b:
                        act.wait_ge(s["adj_ready"], b)
                    evacuate("sim", b, sim[:, :, :].rearrange("p t l -> p (t l)"), scale=1.0 / 16)
                if stage == "adj" and k == ROUNDS + 2:
                    act.wait_ge(s["mask_ready"], b + 1)
                    A(sim[:, :, :], sim[:, :, :], ACT.Tanh, scale=0.5).then_inc(s["th_ready"], 1)
                if stage == "scan" and k < N:
                    if k % 2 and k + 1 < N:
                        spread_bc(b, (k + 1) // 2)
                    if k == 0:
                        act.wait_ge(s["dts_ready"], b + 1)
                    if b == 0 and k == 0:
                        act.wait_ge(s["a_ready"], 1)
                        act.wait_ge(s["consts_ready"], 1)
                    for q in range(EP):
                        i = (b * N + k) * EP + q
                        if i >= DA_RING:
                            act.wait_ge(s["scan_done"], i - DA_RING + 1)
                        for f in range(2):
                            t = 2 * q + f
                            last = A(dA[:, i % DA_RING, f, 1:L], dts[:, p, t, 1:L], ACT.Exp,
                                     scale=a_neg[:, t, k:k + 1])
                        last.then_inc(s["dA_ready"], 1)
                if stage == "out" and k == 1:
                    evacuate("gram", b, gram[:, :, :].rearrange("p t l -> p (t l)"), scale=1.0 / 16)
                if stage == "out" and k == 0:
                    evacuate("kv", b, kv[:, :], work_bank("kv", b)[0:C, 0:L], func=ACT.Identity, bias=b_k[:, :])
                    if b:
                        act.wait_ge(*full("ffn0", b - 1))
                    for i in range(2):
                        gate_tanh(f"gate{i}", b, sg[:, 2 * i:2 * i + 2, :])
                if stage == "xat0" and k == 0:
                    evacuate("x1T", b, xsT[0][:, :, :].rearrange("p t l -> p (t l)"))
                if stage == "xat0" and k == 2:
                    act.wait_ge(s["att_max"], b + 1)
                    for lt in range(LT):
                        last = A(ex[:, lt, :], ex[:, lt, :], ACT.Exp, bias=nmx[:, lt:lt + 1],
                                 accum_out=es[:, lt:lt + 1])
                    last.then_inc(s["att_exp"], 1)
                if stage == "ffn0":
                    ffn(b, k, 0, F0E, DOWN0)
                if stage == "ffn1":
                    ffn(b, k, 1, F1E + 1, DOWN1)
                if stage == "hgrn" and k == 0:
                    evacuate("x3T", b, xsT[1][:, :, :].rearrange("p t l -> p (t l)"))
                if stage == "hgrn" and 1 <= k < 4:
                    n, dst = (("hi", si), ("hf", tf), ("hg", sgg))[k - 1]
                    if b:
                        act.wait_ge(*full("ffn1", b - 1))
                    if n == "hf":
                        evacuate(n, b, dst[:, :, :].rearrange("p t l -> p (t l)"), func=ACT.Tanh, scale=0.5)
                    else:
                        gate_tanh(n, b, dst[:, :, :])
                if stage == "hgrn" and k == 4:
                    act.wait_ge(s["o_ready"], b + 1)
                    A(sq[:, :, :], o[:, :, :], ACT.Square).then_inc(s["sq_ready"], 1)

        @block.vector
        def _(dve):
            V = nc.vector
            links = [0]

            def link(ins):
                links[0] += 1
                ins.then_inc(s["dve_link"], 1)
                dve.wait_ge(s["dve_link"], links[0])

            def release(ins, n, b):
                ins.then_inc(work_read[use[n, b][0]], 1)

            def stats(src, eps, layer=0):
                for lt in range(LT):
                    last = V.bn_stats(bst[layer][:, lt, :], src(lt))
                link(last)
                for lt in range(LT):
                    last = V.bn_aggr(mv[layer][:, lt, :], bst[layer][:, lt, :])
                link(last)
                V.tensor_scalar(var[layer][:, :], mv[layer][:, :, 1], eps, None, ALU.add).then_inc(s["var_ready"], 1)

            def normalize(key, i, b):
                dve.wait_ge(s["rstd_ready"], root[key])
                layer = int(i > 3)
                for lt in range(LT):
                    last = V.tensor_scalar(rows[i][:, lt, :], r[layer][:, lt, :], mv[layer][:, lt, 0:1],
                                           rstd[layer][:, lt:lt + 1], ALU.subtract, ALU.mult)
                last.then_inc(s["rows_ready"], 1)

            def add_bank(n, b, rows_, layer=0):
                dve.wait_ge(*full(n, b))
                release(V.tensor_tensor(r[layer][:, :, :], halves(work_bank(n, b)), rows_, ALU.add), n, b)
                dve.wait_ge(*read(n, b))
                stats(lambda lt: r[layer][:, lt, :], 1e-5, layer)

            def twice_silu(n, b, th):
                dve.wait_ge(s["gate_tanh"], tanh_count[n, b])
                release(V.scalar_tensor_tensor(out=th, in0=th, scalar=1.0, in1=halves(work_bank(n, b)),
                                               op0=ALU.add, op1=ALU.mult), n, b)

            def route(lay, b, prob, nexp):
                link(V.tensor_copy(if8[lay][:, :, :], i8[lay][:, :, 0:2]))
                for i, dst in ((0, wa[lay]), (1, wb[lay])):
                    for lt in range(LT):
                        last = V.tensor_scalar(dst[:, lt, :], iota[:, :], if8[lay][:, lt, i:i + 1],
                                               prob[:, lt, i:i + 1], ALU.is_equal, ALU.mult)
                link(last)
                link(V.tensor_tensor(wf[lay][:, :, 0, 0:F0E], wa[lay][:, :, :], wb[lay][:, :, :], ALU.add))
                for part in range(3):
                    now, left = wf[lay][:, :, part % 2, 0:nexp], wf[lay][:, :, (part + 1) % 2, 0:nexp]
                    link(V.tensor_copy(wpart[lay][:, :, 0:nexp], now))
                    last = V.tensor_copy(whl[lay][:, :, part * nexp:(part + 1) * nexp], wpart[lay][:, :, 0:nexp])
                    if part < 2:
                        link(V.tensor_tensor(left, now, wpart[lay][:, :, 0:nexp], ALU.subtract))
                last.then_inc(s["whl_ready"], 1)

            def ffn(b, k, lay, nexp, routed, h, tiles, rows_in):
                down = 3 + 3 * (tiles // 2)
                if k == 1 and lay == 0:
                    dve.wait_ge(*full("logit0", b))
                    t = work_bank("logit0", b)[:, 0:LT * nexp].rearrange("p (t e) -> p t e", t=LT)
                    V.tensor_reduce(nmx[:, :], t, AX.X, ALU.max, negate=True).then_inc(s["nmx_ready"], 1)
                elif k == 2 and lay == 0:
                    dve.wait_ge(*read("logit0", b))
                    link(V.reciprocal(ri[:, :], es[:, :]))
                    for lt in range(LT):
                        last = V.tensor_scalar(sc[:, lt, :], exr[:, lt, :], ri[:, lt:lt + 1], 0.5, ALU.mult,
                                               ALU.mult)
                    link(last)
                    for lt in range(LT):
                        last = V.max(out=t8[lay][:, lt, :], in_=sc[:, lt, :])
                    link(last)
                    for lt in range(LT):
                        last = V.max_index(out=i8[lay][:, lt, :], in_max=t8[lay][:, lt, :], in_values=sc[:, lt, :])
                    link(last)
                    route(0, b, t8[0], nexp)
                elif k == 1:
                    dve.wait_ge(*full("logit1", b))
                    t = work_bank("logit1", b)[:, 0:LT * nexp].rearrange("p (t e) -> p t e", t=LT)
                    release(V.tensor_copy(lgs[:, :, :], t), "logit1", b)
                    dve.wait_ge(*read("logit1", b))
                    for lt in range(LT):
                        last = V.max(out=t8[lay][:, lt, :], in_=lgs[:, lt, 0:F1E])
                    link(last)
                    V.tensor_copy(dsc[:, :, 1], lgs[:, :, F1E])
                    V.tensor_tensor(dsc[:, :, 0], t8[lay][:, :, 0], t8[lay][:, :, 1], ALU.subtract)\
                        .then_inc(s["dsc_ready"], 1)
                    for lt in range(LT):
                        last = V.max_index(out=i8[lay][:, lt, :], in_max=t8[lay][:, lt, :], in_values=lgs[:, lt, 0:F1E])
                    link(last)
                elif k == 2:
                    dve.wait_ge(s["ths_ready"], b + 1)
                    V.tensor_scalar(pr[:, :, 0], ths[:, :, 0], 0.25, 0.25, ALU.mult, ALU.add)
                    V.tensor_scalar(wf[lay][:, :, 0, F1E], ths[:, :, 1], 0.25, 0.25, ALU.mult, ALU.add)
                    link(V.tensor_scalar(pr[:, :, 1], ths[:, :, 0], -0.25, 0.25, ALU.mult, ALU.add))
                    route(1, b, pr, nexp)
                elif 3 <= k < down:
                    i, kind = divmod(k - 3, 3)
                    m = gated.index((f"g{lay}_{i}", b)) % GS_RING
                    gn_, un, en = f"g{lay}_{i}", f"u{lay}_{i}", f"e{lay}_{i}"
                    weighted = max(0, min(2, routed // P - 2 * i))
                    if kind == 0:
                        twice_silu(gn_, b, gs[:, m, :, :])
                    elif kind == 1:
                        dve.wait_ge(*read(gn_, b))
                        dve.wait_ge(*full(un, b))
                        u = halves(work_bank(un, b))
                        if weighted:
                            last = V.tensor_tensor(h[:, 2 * i:2 * i + weighted, :], gs[:, m, 0:weighted, :],
                                                   u[:, 0:weighted, :], ALU.mult)
                        if weighted < 2:
                            last = V.scalar_tensor_tensor(out=h[:, 2 * i + weighted:2 * i + 2, :],
                                                          in0=gs[:, m, weighted:2, :], scalar=0.5,
                                                          in1=u[:, weighted:2, :], op0=ALU.mult, op1=ALU.mult)
                        release(last, un, b)
                    elif weighted:
                        dve.wait_ge(*read(un, b))
                        dve.wait_ge(*full(en, b))
                        tile = h[:, 2 * i:2 * i + weighted, :]
                        release(V.tensor_tensor(tile, tile, halves(work_bank(en, b))[:, 0:weighted, :], ALU.mult),
                                en, b)
                elif k == down + tiles // 2 - 1:
                    add_bank(f"ffn{lay}", b, rows[rows_in][:, :, :], lay)
                elif k == down + tiles // 2:
                    if lay == 0 and b:
                        dve.wait_ge(s["rows_ready"], row[6, b - 1])
                    normalize((f"ffn{lay}", b, k - 1), rows_in + 1, b)

            for stage, b, k in dve_order:
                p = b % 2
                if stage == "init" and k == 0:
                    dve.wait_ge(loaded[0], part_size[0])
                if stage == "init" and k == 1:
                    dve.wait_ge(loaded[3], part_size[3])
                    dve.wait_ge(loaded[4], part_size[4])
                    for t in range(HT):
                        last = V.tensor_scalar(who[:, t, :], who[:, t, :], gn[:, t:t + 1], -0.125,
                                               ALU.mult, ALU.mult)
                    last.then_inc(s["init_late"], 1)
                if stage == "pre" and k == 0:
                    for i in range(2):
                        dve.wait_ge(s["conv0"], 2 * b + i + 1)
                        for tap in range(KC - 2, -1, -1):
                            off = KC - 1 - tap
                            for f in range(2):
                                t = 2 * i + f
                                last = V.scalar_tensor_tensor(
                                    out=du[:, p, t, off:L], in0=work_bank(f"hid{i}", b)[:, f * L:(f + 1) * L - off],
                                    scalar=cw[:, t, tap:tap + 1], in1=du[:, p, t, off:L], op0=ALU.mult, op1=ALU.add)
                            if tap:
                                link(last)
                        release(last, f"hid{i}", b)
                if stage == "pre" and k == 2:
                    dve.wait_ge(*full("bT", b))
                    if b:
                        dve.wait_ge(s["sp_ready"], b)
                    t = work_bank("bT", b)
                    link(V.tensor_copy(bc_parts[:, p, :], t[:, 0:L]))
                    h_, q_ = P // 2, 3 * P // 4
                    last = V.tensor_tensor(za[h_:P, 0, :], t[h_:P, 0:L], bc_parts[h_:P, p, :], ALU.subtract)
                    release(last, "bT", b)
                    dve.wait_ge(*read("bT", b))
                    link(V.tensor_copy(bc_parts[h_:P, p, :], za[h_:P, 0, :]))
                    link(V.tensor_tensor(za[q_:P, 1, :], za[q_:P, 0, :], bc_parts[q_:P, p, :], ALU.subtract))
                    V.tensor_copy(bc_parts[q_:P, p, :], za[q_:P, 1, :]).then_inc(s["bc_parts_ready"], 1)
                if stage == "pre" and k == 4:
                    if b == 0:
                        dve.wait_ge(s["a_exp"], 1)
                        V.tensor_scalar(a_neg[:, :, :], a_neg[:, :, :], -1.0, None, ALU.mult)\
                            .then_inc(s["a_ready"], 1)
                    dve.wait_ge(s["sp_ready"], b + 1)
                    V.tensor_tensor(dts[:, p], dts[:, p], za[:, :, :], ALU.add).then_inc(s["dts_ready"], 1)
                    dve.wait_ge(s["dts_ready"], b + 1)
                    V.tensor_tensor(du[:, p], dts[:, p], hs[:, p], ALU.mult).then_inc(s["du_ready"], 1)
                if stage == "adj" and 2 <= k < ROUNDS + 2:
                    i = k - 2
                    if i == 0:
                        dve.wait_ge(*read("sim", b))
                    src = sim if i == 0 else wk
                    for lt in range(LT):
                        last = V.max(out=m8[:, lt, :], in_=src[:, lt, :])
                    link(last)
                    if i < ROUNDS - 1:
                        for lt in range(LT):
                            last = V.match_replace(out=wk[:, lt, :], in_to_replace=m8[:, lt, :],
                                                   in_values=src[:, lt, :], imm_value=-3.0e38)
                        link(last)
                if stage == "adj" and k == ROUNDS + 2:
                    if b == 0:
                        dve.wait_ge(s["gam_tanh"], 1)
                        V.tensor_scalar(gq[:, :], gth[:, :], 0.125, 0.125, ALU.mult, ALU.add)
                        link(V.tensor_scalar(g2[:, :], gth[:, :], -0.5, 1.5, ALU.mult, ALU.add))
                    at = (TOPK - 1) % 8
                    for lt in range(LT):
                        last = V.tensor_scalar(wk[:, lt, :], sim[:, lt, :], m8[:, lt, at:at + 1], gq[:, 0:1],
                                               ALU.is_ge, ALU.mult)
                    last.then_inc(s["mask_ready"], 1)
                if stage == "adj" and k == ROUNDS + 3:
                    dve.wait_ge(s["th_ready"], b + 1)
                    V.scalar_tensor_tensor(out=wk[:, :, :], in0=sim[:, :, :], scalar=1.0, in1=wk[:, :, :],
                                           op0=ALU.add, op1=ALU.mult).then_inc(s["adj_ready"], 1)
                if stage == "adj" and k == ROUNDS + 4:
                    dve.wait_ge(*full("adjT", b))
                    release(V.tensor_tensor(S[:, p], wk[:, :, :], halves(work_bank("adjT", b)), ALU.add), "adjT", b)
                if stage == "scan":
                    for q in range(2):
                        if k < N:
                            i = (b * N + k) * EP + q
                            dve.wait_ge(s["dA_ready"], i + 1)
                            dve.wait_ge(s["dbu_ready"], i + 1)
                            if i >= ST_RING:
                                dve.wait_ge(s["acc_done"], i - ST_RING + 1)
                            V.tensor_tensor_scan(st[:, i % ST_RING].rearrange("p f l -> p (f l)"),
                                                 dA[:, i % DA_RING].rearrange("p f l -> p (f l)"),
                                                 dbu[:, i % DBU_RING].rearrange("p f l -> p (f l)"),
                                                 0.0, ALU.mult, ALU.add).then_inc(s["scan_done"], 1)
                        if k > 1:
                            n = k - 2
                            done = (b * N + n) * EP + q
                            y, product = acc[:, 2 * q:2 * q + 2, :], st[:, done % ST_RING]
                            by_pool, by_vector = weighed(done + 1)
                            if vector_weighs(done):
                                dve.wait_ge(s["scan_done"], done + 1)
                                V.tensor_tensor(product, product,
                                                bc[:, (b * N + n) // 2 % 2, 2 + n % 2:3 + n % 2, :]
                                                .to_broadcast([P, 2, L]), ALU.mult).then_inc(s["vector_prod"], 1)
                                dve.wait_ge(s["vector_prod"], by_vector)
                            else:
                                dve.wait_ge(s["prod_ready"], by_pool)
                            if done >= 2:
                                dve.wait_ge(s["acc_done"], done - 1)
                            if n == 0:
                                if b:
                                    dve.wait_ge(s["yg_ready"], b)
                                ins = V.tensor_copy(y, product)
                            else:
                                ins = V.tensor_tensor(y, y, product, ALU.add)
                            ins.then_inc(s["acc_done"], 1)
                if stage == "out" and k == 0:
                    for i in range(2):
                        twice_silu(f"gate{i}", b, sg[:, 2 * i:2 * i + 2, :])
                if stage == "out" and k == 1:
                    dve.wait_ge(s["acc_done"], (b + 1) * N * EP)
                    for t in range(ET):
                        last = V.scalar_tensor_tensor(out=yg[:, t, :], in0=hs[:, p, t, :], scalar=skip[:, t:t + 1],
                                                      in1=acc[:, t, :], op0=ALU.mult, op1=ALU.add)
                    link(last)
                    dve.wait_ge(*read("gate1", b))
                    V.scalar_tensor_tensor(out=yg[:, :, :], in0=yg[:, :, :], scalar=0.5, in1=sg[:, :, :],
                                           op0=ALU.mult, op1=ALU.mult).then_inc(s["yg_ready"], 1)
                if stage == "out" and k == 2:
                    if b:
                        dve.wait_ge(s["x_loaded"], 16 * b)
                    else:
                        dve.wait_ge(loaded[3], part_size[3])
                    add_bank("mamba", b, rows[0][:, :, :])
                if stage == "out" and k == 3:
                    normalize(("out", b, 2), 1, b)
                if stage == "xat0" and k == 1:
                    dve.wait_ge(*full("att", b))
                    stats(lambda lt: work_bank("att", b)[:, lt * L:(lt + 1) * L], 1e-6)
                if stage == "xat0" and k == 2:
                    dve.wait_ge(s["rstd_ready"], root["xat0", b, 1])
                    for lt in range(LT):
                        last = V.tensor_scalar(ex[:, lt, :], work_bank("att", b)[:, lt * L:(lt + 1) * L],
                                               mv[0][:, lt, 0:1], rstd[0][:, lt:lt + 1], ALU.subtract, ALU.mult)
                    release(last, "att", b)
                    dve.wait_ge(*read("att", b))
                    for lt in range(LT):
                        last = V.tensor_tensor(ex[:, lt, :], ex[:, lt, :], lng[:, :], ALU.mult)
                    link(last)
                    for lt in range(LT):
                        last = V.tensor_tensor(ex[:, lt, :], ex[:, lt, :], lnb[:, :], ALU.add)
                    link(last)
                    V.tensor_reduce(nmx[:, :], ex[:, :, :], AX.X, ALU.max, negate=True).then_inc(s["att_max"], 1)
                if stage == "xat0" and k == 3:
                    dve.wait_ge(s["att_exp"], b + 1)
                    link(V.reciprocal(ri[:, :], es[:, :]))
                    for lt in range(LT):
                        last = V.scalar_tensor_tensor(out=r[0][:, lt, :], in0=ex[:, lt, :], scalar=ri[:, lt:lt + 1],
                                                      in1=rows[1][:, lt, :], op0=ALU.mult, op1=ALU.add)
                    link(last)
                    stats(lambda lt: r[0][:, lt, :], 1e-5)
                if stage == "xat0" and k == 4:
                    normalize(("xat0", b, 3), 2, b)
                if stage == "ffn0":
                    ffn(b, k, 0, F0E, F0E * F0F, big0, F0T, 2)
                if stage == "ffn1":
                    ffn(b, k, 1, F1E + 1, F1, big1, F1T, 5)
                if stage == "hgrn" and k == 1:
                    twice_silu("hi", b, si[:, :, :])
                if stage == "hgrn" and k == 3:
                    twice_silu("hg", b, sgg[:, :, :])
                    dve.wait_ge(*read("hi", b))
                    dve.wait_ge(*read("hf", b))
                    link(V.scalar_tensor_tensor(out=si[:, :, :], in0=tf[:, :, :], scalar=1.0, in1=si[:, :, :],
                                                op0=ALU.subtract, op1=ALU.mult))
                    link(V.tensor_scalar(tf[:, :, :], tf[:, :, :], 0.5, 0.5, ALU.mult, ALU.add))
                    for t in range(HT):
                        last = V.tensor_tensor_scan(o[:, t, :], tf[:, t, :], si[:, t, :], 0.0, ALU.mult, ALU.add)
                    last.then_inc(s["o_ready"], 1)
                    dve.wait_ge(s["o_ready"], b + 1)
                    dve.wait_ge(*read("hg", b))
                    V.tensor_tensor(sgg[:, :, :], o[:, :, :], sgg[:, :, :], ALU.mult).then_inc(s["q_ready"], 1)
                if stage == "hgrn" and k == 4:
                    dve.wait_ge(*full("ss", b))
                    release(V.tensor_scalar(var[1][:, :], work_bank("ss", b)[:, 0:LT], 1.0 / (16 * H), 1e-5,
                                            ALU.mult, ALU.add), "ss", b)
                if stage == "hgrn" and k == 5:
                    dve.wait_ge(*full("hgrn", b))
                    dve.wait_ge(s["rstd_ready"], root["hgrn", b, 4])
                    for lt in range(LT):
                        last = V.scalar_tensor_tensor(out=r[1][:, lt, :],
                                                      in0=work_bank("hgrn", b)[:, lt * H:(lt + 1) * H],
                                                      scalar=rstd[1][:, lt:lt + 1], in1=rows[3][:, lt, :],
                                                      op0=ALU.mult, op1=ALU.add)
                    release(last, "hgrn", b)
                    dve.wait_ge(*read("hgrn", b))
                    stats(lambda lt: r[1][:, lt, :], 1e-5, 1)
                if stage == "hgrn" and k == 6:
                    if b:
                        dve.wait_ge(s["out_done"], 16 * b)
                    normalize(("hgrn", b, 5), 4, b)
                    dve.wait_ge(s["rows_ready"], row[4, b])
                    link(V.scalar_tensor_tensor(out=r[1][:, :, :], in0=rows[4][:, :, :], scalar=g2[:, 0:1], in1=S[:, p],
                                                op0=ALU.mult, op1=ALU.add))
                    stats(lambda lt: r[1][:, lt, :], 1e-5, 1)
                if stage == "hgrn" and k == 7:
                    normalize(("hgrn", b, 6), 5, b)


def kernel(**inputs):
    import ml_dtypes
    import numpy as np
    import concourse.bacc as bacc
    from concourse.bass_utils import run_bass_kernel_spmd

    v = {k: np.asarray(a) for k, a in inputs.items()}

    def tiles(a):
        return a.reshape(-1, P, a.shape[-1]).transpose(1, 0, 2)

    def up(routed, shared):
        return tiles(np.concatenate([routed.reshape(-1, H), shared], 0).T)

    def down(routed, shared):
        return np.concatenate([routed.transpose(0, 2, 1).reshape(-1, H), shared.T], 0)

    def padded(rows):
        return np.concatenate([rows, np.zeros((-len(rows) % P, H), rows.dtype)], 0)

    def members(width, n, rows):
        expert = np.minimum(np.arange(n) // width, rows - 1)
        return np.tile(expert[None, :] == np.arange(rows)[:, None], (3, 1)).astype(ml_dtypes.bfloat16)

    gate, up_ = (tiles(padded(np.concatenate([v["L0_ffn_" + a].reshape(-1, H), v["L0_ffn_" + b]], 0)).T)
                 .reshape(P, HT, F0T // 2, 2 * P).transpose(0, 2, 1, 3) for a, b in (("Wg", "Wsg"), ("Wu", "Wsu")))
    downs = [tiles(padded(down(v[a], v[b]))).reshape(P, -1, 2, H)
             for a, b in (("L0_ffn_Wd", "L0_ffn_Wsd"), ("L1_ffn_w_down", "L1_ffn_sh_down"))]
    stream = np.concatenate([np.stack([gate, up_], 2).reshape(P, F0T, HT, 2 * P)] + downs, 1)
    picks = np.zeros((4, 2 * N, 2 * N), ml_dtypes.bfloat16)
    for quarter in (0, 2, 3):
        picks[quarter] = np.eye(2 * N)
    picks = picks.reshape(P, 2 * N)
    xf = v["x"].reshape(B * L, H)
    a = {
        "x": tiles(xf), "xT": tiles(xf.T), "ctxT": v["ctx_512"].reshape(B * L, C).T,
        "w_in": tiles(v["L0_attn_W_in"]), "cw": tiles(v["L0_attn_conv_kernel"].reshape(E, KC)),
        "cb": v["L0_attn_conv_bias"].reshape(ET, P).T,
        "w_x": tiles(np.concatenate([v["L0_attn_W_x"]] + 3 * [v["L0_attn_W_x"][:, TR:]], 1)),
        "w_dt": v["L0_attn_W_dt"],
        "b_dt": v["L0_attn_b_dt"].reshape(ET, P).T, "a_log": tiles(v["L0_attn_A_log"]),
        "skip": v["L0_attn_D"].reshape(ET, P).T, "w_out": tiles(v["L0_attn_W_out"]),
        "wkvT": v["L0_xattn_W_k"].T, "b_k": v["L0_xattn_b_k"].reshape(C, 1),
        "lng": v["L0_xattn_ln_gamma"].reshape(L), "lnb": v["L0_xattn_ln_beta"].reshape(L),
        "wr": tiles(v["L0_ffn_Wr"].T), "stream": stream,
        "whi": tiles(v["L1_attn_Wi"]), "whf": tiles(v["L1_attn_Wf"]), "whg": tiles(v["L1_attn_Wg"]),
        "who": tiles(v["L1_attn_Wo"]), "gn": v["L1_attn_g_norm_weight"].reshape(HT, P).T,
        "wqT": v["L1_xattn_Wq"].T, "wkT": v["L1_xattn_Wk"].T, "gam": v["L1_xattn_gamma_raw"].reshape(1),
        "wr1": tiles(np.concatenate([v["L1_ffn_gate_w"], v["L1_ffn_se_gate_w"]], 0).T),
        "wg1": up(v["L1_ffn_w_gate"], v["L1_ffn_sh_gate"]), "wu1": up(v["L1_ffn_w_up"], v["L1_ffn_sh_up"]),
        "ident": np.eye(P, dtype=np.float32), "iota": np.arange(F0E, dtype=np.float32),
        "sel0": members(F0F, F0E * F0F, F0E), "sel1": members(F1F, F1, F1E + 1)[:, ::P], "sel_bc": picks,
    }
    arrays = {f"in_{k}": np.ascontiguousarray(t) for k, t in a.items()}
    nc = bacc.Bacc("TRN2", target_bir_lowering=False, num_devices=1)
    d = {k: nc.dram_tensor(f"in_{k}", arrays[f"in_{k}"].shape, mybir.dt.from_np(arrays[f"in_{k}"].dtype),
                           kind="ExternalInput").ap() for k in a}
    out = nc.dram_tensor("out", (P, B * LT, H), F32, kind="ExternalOutput").ap()
    decoder(nc, d, out)
    got = run_bass_kernel_spmd(nc, [arrays], core_ids=[0]).results[0]["out"]
    return got.transpose(1, 0, 2).reshape(B, L, H)
```
